# Optimizing a Trainium2 kernel written in Bass

```python
import numpy as np
import jax
import jax.numpy as jnp

def _softmax(x, axis=-1):
    return jax.nn.softmax(x, axis=axis)

def _gelu(x):
    return jax.nn.gelu(x, approximate=True)

def _silu(x):
    return jax.nn.silu(x)

def _sigmoid(x):
    return jax.nn.sigmoid(x)

def _layernorm(x, axis=-1, eps=1e-05):
    m = jnp.mean(x, axis=axis, keepdims=True)
    v = jnp.var(x, axis=axis, keepdims=True)
    return (x - m) / jnp.sqrt(v + eps)

def _scatter_add(tgt, idx, src, axis=0):
    return tgt.at[idx].add(src)

def _segment_sum(src, seg, n):
    return jax.ops.segment_sum(src, seg, n)
kernel_name = 'mk_gnn_resnorm_d4_gnn_r32_5db10b'

def setup_inputs(seed: int=0):
    np.random.seed(seed)
    _w = jnp.asarray

    def _rec_inputs():
        import jax
        import jax.numpy as jnp
        _gk = jax.random.key(seed)
        x = -0.0005121 + 1.001 * jax.random.normal(jax.random.fold_in(_gk, 1), (50000, 64), jnp.float32)
        src = jax.random.randint(jax.random.fold_in(_gk, 2), (50000,), 0, 50000, jnp.int32)
        dst = jax.random.randint(jax.random.fold_in(_gk, 3), (50000,), 0, 50000, jnp.int32)
        _o = jnp.argsort(dst, stable=True)
        src = src[_o]
        dst = dst[_o]
        edge_attr_2 = 0.00070975 + 1.00011 * jax.random.normal(jax.random.fold_in(_gk, 12), (50000, 2), jnp.float32)
        edge_attr_48 = -4.21973e-05 + 0.999841 * jax.random.normal(jax.random.fold_in(_gk, 13), (50000, 48), jnp.float32)
        edge_attr_64 = -5.16925e-05 + 1.00005 * jax.random.normal(jax.random.fold_in(_gk, 14), (50000, 64), jnp.float32)
        edge_weight = jax.random.uniform(jax.random.fold_in(_gk, 16), (50000,), jnp.float32, 0.0, 1)
        return (x, src, dst, edge_attr_2, edge_attr_48, edge_attr_64, edge_weight)
    x, src, dst, edge_attr_2, edge_attr_48, edge_attr_64, edge_weight = _rec_inputs()

    def _L0_gnn_setup():
        import jax, jax.numpy as jnp
        import numpy as np
        N_NODES = 50000
        N_EDGES = 25000
        IN_C, HID_C, OUT_C = (64, 64, 64)

        def _glorot(key, shape):
            fan_in, fan_out = shape
            s = jnp.sqrt(6.0 / (fan_in + fan_out))
            return jax.random.uniform(key, shape, jnp.float32, -s, s)

        def _cheb_norm(edge_index, edge_weight, n):
            src, dst = (edge_index[0], edge_index[1])
            deg = jax.ops.segment_sum(edge_weight, src, num_segments=n)
            dinv = jnp.where(deg > 0, jax.lax.rsqrt(jnp.maximum(deg, 1e-12)), 0.0)
            return -dinv[src] * edge_weight * dinv[dst]

        def _cheb_conv(x, edge_index, w_norm, W0, W1, b):
            src, dst = (edge_index[0], edge_index[1])
            tx1 = jax.ops.segment_sum(w_norm[:, None] * x[src], dst, num_segments=x.shape[0])
            return x @ W0 + tx1 @ W1 + b
        key = jax.random.key(seed)
        ks = jax.random.split(key, 8)
        x = jax.random.normal(ks[0], (N_NODES, IN_C), jnp.float32)
        edge_index = jax.random.randint(ks[1], (2, N_EDGES), 0, N_NODES, jnp.int64)
        edge_weight = jnp.ones((N_EDGES,), jnp.float32)
        return {'x': x, 'edge_index': edge_index, 'edge_weight': edge_weight, 'W0_1': _glorot(ks[2], (IN_C, HID_C)), 'W1_1': _glorot(ks[3], (IN_C, HID_C)), 'b1': jnp.zeros((HID_C,), jnp.float32), 'W0_2': _glorot(ks[4], (HID_C, OUT_C)), 'W1_2': _glorot(ks[5], (HID_C, OUT_C)), 'b2': jnp.zeros((OUT_C,), jnp.float32)}
    _L0_gnn_all = _L0_gnn_setup()
    _L0_gnn_in = {k: v for k, v in _L0_gnn_all.items() if k in ('W0_1', 'W1_1', 'b1', 'W0_2', 'W1_2', 'b2')}
    del _L0_gnn_all

    def _L1_gnn_setup():
        import jax, jax.numpy as jnp
        import numpy as np
        N_NODES = 3125
        N_EDGES = 50000
        RBF_DIM = 48
        DIM = 64
        BETA = 0.5
        THRESHOLD = 14.0

        def softplus_b(x):
            bx = BETA * x
            return jnp.where(bx > THRESHOLD, x, 1.0 / BETA * jnp.log1p(jnp.exp(jnp.minimum(bx, THRESHOLD))))
        key = jax.random.key(seed)
        ks = jax.random.split(key, 12)
        inp = {'new_node': jax.random.normal(ks[0], (N_NODES, DIM), jnp.float32), 'rbf': jax.random.normal(ks[1], (N_EDGES, RBF_DIM), jnp.float32), 'edge_f': jax.random.normal(ks[2], (N_EDGES, DIM), jnp.float32), 'W1': jax.random.normal(ks[3], (RBF_DIM, DIM), jnp.float32) * 0.1, 'b1': jnp.zeros((DIM,), jnp.float32), 'W2': jax.random.normal(ks[4], (DIM, DIM), jnp.float32) * 0.1, 'b2': jnp.zeros((DIM,), jnp.float32), 'W3': jax.random.normal(ks[5], (DIM, DIM), jnp.float32) * 0.1, 'b3': jnp.zeros((DIM,), jnp.float32), 'W4': jax.random.normal(ks[6], (DIM, DIM), jnp.float32) * 0.1, 'b4': jnp.zeros((DIM,), jnp.float32), 'src': jax.random.randint(ks[7], (N_EDGES,), 0, N_NODES, jnp.int32), 'dst': jax.random.randint(ks[8], (N_EDGES,), 0, N_NODES, jnp.int32)}
        return inp
    _L1_gnn_all = _L1_gnn_setup()
    _L1_gnn_in = {k: v for k, v in _L1_gnn_all.items() if k in ('W1', 'b1', 'W2', 'b2', 'W3', 'b3', 'W4', 'b4')}
    del _L1_gnn_all

    def _L2_gnn_setup():
        import jax, jax.numpy as jnp
        import numpy as np
        N_NODES = 3125
        N_EDGES = 50000
        IN_FEATS = 64
        OUT_FEATS = 64
        NEG_SLOPE = 0.01
        key = jax.random.key(seed)
        k_feat, k_w, k_al, k_ar, k_src, k_dst = jax.random.split(key, 6)
        feat = jax.random.normal(k_feat, (N_NODES, IN_FEATS), dtype=jnp.float32)
        W = jax.random.normal(k_w, (IN_FEATS, OUT_FEATS), dtype=jnp.float32)
        al = jax.random.normal(k_al, (IN_FEATS, 1), dtype=jnp.float32)
        ar = jax.random.normal(k_ar, (IN_FEATS, 1), dtype=jnp.float32)
        src = jax.random.randint(k_src, (N_EDGES,), 0, N_NODES, dtype=jnp.int32)
        dst = jax.random.randint(k_dst, (N_EDGES,), 0, N_NODES, dtype=jnp.int32)
        return {'feat': feat, 'W': W, 'al': al, 'ar': ar, 'src': src, 'dst': dst}
    _L2_gnn_all = _L2_gnn_setup()
    _L2_gnn_in = {k: v for k, v in _L2_gnn_all.items() if k in ('W', 'al', 'ar')}
    del _L2_gnn_all

    def _L3_gnn_setup():
        import jax, jax.numpy as jnp
        import numpy as np
        N = 3125
        E = 1250000
        D = 64
        K = 3
        EPS = 1e-05

        def _transformer_conv(x, src, dst, edge_attr, Wq, bq, Wk, bk, Wv, bv, We, Wskip, bskip):
            n, d = x.shape
            q = x @ Wq.T + bq
            k = x @ Wk.T + bk
            v = x @ Wv.T + bv
            e = edge_attr @ We.T
            ke = k[src] + e
            logits = jnp.sum(q[dst] * ke, axis=-1) / jnp.sqrt(jnp.float32(d))
            m = jax.ops.segment_max(logits, dst, num_segments=n)
            ex = jnp.exp(logits - m[dst])
            den = jax.ops.segment_sum(ex, dst, num_segments=n)
            alpha = ex / den[dst]
            msg = (v[src] + e) * alpha[:, None]
            out = jax.ops.segment_sum(msg, dst, num_segments=n)
            return out + x @ Wskip.T + bskip

        def _layer_norm(h, g, b):
            mu = jnp.mean(h, axis=-1, keepdims=True)
            var = jnp.mean(jnp.square(h - mu), axis=-1, keepdims=True)
            return (h - mu) * jax.lax.rsqrt(var + EPS) * g + b
        key = jax.random.key(seed)
        ks = jax.random.split(key, 12)
        s = 0.05
        X = jax.random.normal(ks[0], (N, D), jnp.float32)
        edge_index = jax.random.randint(ks[1], (2, E), 0, N, jnp.int32)
        edge_attr = jax.random.normal(ks[2], (E, 2), jnp.float32)
        Wq = jax.random.normal(ks[3], (K, D, D), jnp.float32) * s
        bq = jnp.zeros((K, D), jnp.float32)
        Wk = jax.random.normal(ks[4], (K, D, D), jnp.float32) * s
        bk = jnp.zeros((K, D), jnp.float32)
        Wv = jax.random.normal(ks[5], (K, D, D), jnp.float32) * s
        bv = jnp.zeros((K, D), jnp.float32)
        We = jax.random.normal(ks[6], (K, D, 2), jnp.float32) * s
        Wskip = jax.random.normal(ks[7], (K, D, D), jnp.float32) * s
        bskip = jnp.zeros((K, D), jnp.float32)
        gamma = jnp.ones((K, D), jnp.float32)
        beta = jnp.zeros((K, D), jnp.float32)
        return dict(X=X, edge_index=edge_index, edge_attr=edge_attr, Wq=Wq, bq=bq, Wk=Wk, bk=bk, Wv=Wv, bv=bv, We=We, Wskip=Wskip, bskip=bskip, gamma=gamma, beta=beta)
    _L3_gnn_all = _L3_gnn_setup()
    _L3_gnn_in = {k: v for k, v in _L3_gnn_all.items() if k in ('Wq', 'bq', 'Wk', 'bk', 'Wv', 'bv', 'We', 'Wskip', 'bskip', 'gamma', 'beta')}
    del _L3_gnn_all
    return {'x': x, 'src': src, 'dst': dst, 'edge_attr_2': edge_attr_2, 'edge_attr_48': edge_attr_48, 'edge_attr_64': edge_attr_64, 'edge_weight': edge_weight, 'L0_gnn_W0_1': _L0_gnn_in['W0_1'], 'L0_gnn_W1_1': _L0_gnn_in['W1_1'], 'L0_gnn_b1': _L0_gnn_in['b1'], 'L0_gnn_W0_2': _L0_gnn_in['W0_2'], 'L0_gnn_W1_2': _L0_gnn_in['W1_2'], 'L0_gnn_b2': _L0_gnn_in['b2'], 'L1_gnn_W1': _L1_gnn_in['W1'], 'L1_gnn_b1': _L1_gnn_in['b1'], 'L1_gnn_W2': _L1_gnn_in['W2'], 'L1_gnn_b2': _L1_gnn_in['b2'], 'L1_gnn_W3': _L1_gnn_in['W3'], 'L1_gnn_b3': _L1_gnn_in['b3'], 'L1_gnn_W4': _L1_gnn_in['W4'], 'L1_gnn_b4': _L1_gnn_in['b4'], 'L2_gnn_W': _L2_gnn_in['W'], 'L2_gnn_al': _L2_gnn_in['al'], 'L2_gnn_ar': _L2_gnn_in['ar'], 'L3_gnn_Wq': _L3_gnn_in['Wq'], 'L3_gnn_bq': _L3_gnn_in['bq'], 'L3_gnn_Wk': _L3_gnn_in['Wk'], 'L3_gnn_bk': _L3_gnn_in['bk'], 'L3_gnn_Wv': _L3_gnn_in['Wv'], 'L3_gnn_bv': _L3_gnn_in['bv'], 'L3_gnn_We': _L3_gnn_in['We'], 'L3_gnn_Wskip': _L3_gnn_in['Wskip'], 'L3_gnn_bskip': _L3_gnn_in['bskip'], 'L3_gnn_gamma': _L3_gnn_in['gamma'], 'L3_gnn_beta': _L3_gnn_in['beta']}

def reference(x, src, dst, edge_attr_2, edge_attr_48, edge_attr_64, edge_weight, L0_gnn_W0_1, L0_gnn_W1_1, L0_gnn_b1, L0_gnn_W0_2, L0_gnn_W1_2, L0_gnn_b2, L1_gnn_W1, L1_gnn_b1, L1_gnn_W2, L1_gnn_b2, L1_gnn_W3, L1_gnn_b3, L1_gnn_W4, L1_gnn_b4, L2_gnn_W, L2_gnn_al, L2_gnn_ar, L3_gnn_Wq, L3_gnn_bq, L3_gnn_Wk, L3_gnn_bk, L3_gnn_Wv, L3_gnn_bv, L3_gnn_We, L3_gnn_Wskip, L3_gnn_bskip, L3_gnn_gamma, L3_gnn_beta):
    import jax
    import jax.numpy as jnp

    def _L0_gnn_ref(x, edge_index, edge_weight, W0_1, W1_1, b1, W0_2, W1_2, b2):
        import jax, jax.numpy as jnp
        import numpy as np
        N_NODES = 50000
        N_EDGES = 25000
        IN_C, HID_C, OUT_C = (64, 64, 64)

        def _glorot(key, shape):
            fan_in, fan_out = shape
            s = jnp.sqrt(6.0 / (fan_in + fan_out))
            return jax.random.uniform(key, shape, jnp.float32, -s, s)

        def _cheb_norm(edge_index, edge_weight, n):
            src, dst = (edge_index[0], edge_index[1])
            deg = jax.ops.segment_sum(edge_weight, src, num_segments=n)
            dinv = jnp.where(deg > 0, jax.lax.rsqrt(jnp.maximum(deg, 1e-12)), 0.0)
            return -dinv[src] * edge_weight * dinv[dst]

        def _cheb_conv(x, edge_index, w_norm, W0, W1, b):
            src, dst = (edge_index[0], edge_index[1])
            tx1 = jax.ops.segment_sum(w_norm[:, None] * x[src], dst, num_segments=x.shape[0])
            return x @ W0 + tx1 @ W1 + b
        w_norm = _cheb_norm(edge_index, edge_weight, x.shape[0])
        h = jax.nn.relu(_cheb_conv(x, edge_index, w_norm, W0_1, W1_1, b1))
        return _cheb_conv(h, edge_index, w_norm, W0_2, W1_2, b2)

    def _L1_gnn_ref(new_node, rbf, edge_f, W1, b1, W2, b2, W3, b3, W4, b4, src, dst):
        import jax, jax.numpy as jnp
        import numpy as np
        N_NODES = 3125
        N_EDGES = 50000
        RBF_DIM = 48
        DIM = 64
        BETA = 0.5
        THRESHOLD = 14.0

        def softplus_b(x):
            bx = BETA * x
            return jnp.where(bx > THRESHOLD, x, 1.0 / BETA * jnp.log1p(jnp.exp(jnp.minimum(bx, THRESHOLD))))
        n_nodes = new_node.shape[0]
        h = softplus_b(rbf @ W1 + b1) @ W2 + b2
        ef = (edge_f @ W3 + b3) @ W4 + b4
        m = new_node[src] * h + ef
        out = jax.ops.segment_sum(m, dst, num_segments=n_nodes)
        return out

    def _L2_gnn_ref(feat, W, al, ar, src, dst):
        import jax, jax.numpy as jnp
        import numpy as np
        N_NODES = 3125
        N_EDGES = 50000
        IN_FEATS = 64
        OUT_FEATS = 64
        NEG_SLOPE = 0.01
        n = feat.shape[0]
        h = feat @ W
        el = (feat @ al)[:, 0]
        er = (feat @ ar)[:, 0]
        e = el[src] + er[dst]
        e = jnp.where(e >= 0, e, NEG_SLOPE * e)
        seg_max = jax.ops.segment_max(e, dst, num_segments=n)
        w = jnp.exp(e - seg_max[dst])
        seg_sum = jax.ops.segment_sum(w, dst, num_segments=n)
        w = w / seg_sum[dst]
        out = jax.ops.segment_sum(w[:, None] * h[src], dst, num_segments=n)
        return out

    def _L3_gnn_ref(X, edge_index, edge_attr, Wq, bq, Wk, bk, Wv, bv, We, Wskip, bskip, gamma, beta):
        import jax, jax.numpy as jnp
        import numpy as np
        N = 3125
        E = 1250000
        D = 64
        K = 3
        EPS = 1e-05

        def _transformer_conv(x, src, dst, edge_attr, Wq, bq, Wk, bk, Wv, bv, We, Wskip, bskip):
            n, d = x.shape
            q = x @ Wq.T + bq
            k = x @ Wk.T + bk
            v = x @ Wv.T + bv
            e = edge_attr @ We.T
            ke = k[src] + e
            logits = jnp.sum(q[dst] * ke, axis=-1) / jnp.sqrt(jnp.float32(d))
            m = jax.ops.segment_max(logits, dst, num_segments=n)
            ex = jnp.exp(logits - m[dst])
            den = jax.ops.segment_sum(ex, dst, num_segments=n)
            alpha = ex / den[dst]
            msg = (v[src] + e) * alpha[:, None]
            out = jax.ops.segment_sum(msg, dst, num_segments=n)
            return out + x @ Wskip.T + bskip

        def _layer_norm(h, g, b):
            mu = jnp.mean(h, axis=-1, keepdims=True)
            var = jnp.mean(jnp.square(h - mu), axis=-1, keepdims=True)
            return (h - mu) * jax.lax.rsqrt(var + EPS) * g + b
        src, dst = (edge_index[0], edge_index[1])
        s = jnp.zeros((X.shape[0], D), X.dtype)
        for i in range(K):
            out = _transformer_conv(X, src, dst, edge_attr, Wq[i], bq[i], Wk[i], bk[i], Wv[i], bv[i], We[i], Wskip[i], bskip[i])
            s = _layer_norm(s + out, gamma[i], beta[i])
        return jax.nn.relu(s)
    edge_index = jnp.stack([src, dst])
    x = _layernorm(x + _L0_gnn_ref(x, edge_index, edge_weight, L0_gnn_W0_1, L0_gnn_W1_1, L0_gnn_b1, L0_gnn_W0_2, L0_gnn_W1_2, L0_gnn_b2), axis=-1)
    x = _layernorm(x + _L1_gnn_ref(x, edge_attr_48, edge_attr_64, L1_gnn_W1, L1_gnn_b1, L1_gnn_W2, L1_gnn_b2, L1_gnn_W3, L1_gnn_b3, L1_gnn_W4, L1_gnn_b4, src, dst), axis=-1)
    x = _layernorm(x + _L2_gnn_ref(x, L2_gnn_W, L2_gnn_al, L2_gnn_ar, src, dst), axis=-1)
    x = _layernorm(x + _L3_gnn_ref(x, edge_index, edge_attr_2, L3_gnn_Wq, L3_gnn_bq, L3_gnn_Wk, L3_gnn_bk, L3_gnn_Wv, L3_gnn_bv, L3_gnn_We, L3_gnn_Wskip, L3_gnn_bskip, L3_gnn_gamma, L3_gnn_beta), axis=-1)
    return x

_drawn_inputs = setup_inputs


def setup_inputs(seed=0):
    import zlib

    import numpy as np

    out = dict(_drawn_inputs(seed))
    spreads = {'L0_gnn_b1': (0.0, 0.1),
     'L0_gnn_b2': (0.0, 0.1),
     'L1_gnn_b1': (0.0, 0.372),
     'L1_gnn_b2': (0.0, 0.1),
     'L1_gnn_b3': (0.0, 0.1),
     'L1_gnn_b4': (0.0, 0.1),
     'L3_gnn_bq': (0.0, 0.8),
     'L3_gnn_bk': (0.0, 0.8),
     'L3_gnn_bv': (0.0, 0.1),
     'L3_gnn_bskip': (0.0, 0.1),
     'L3_gnn_gamma': (1.0, 0.2),
     'L3_gnn_beta': (0.0, 0.1)}
    factors = {'L3_gnn_Wq': 2.792, 'L3_gnn_Wk': 2.707}
    for name, (base, spread) in spreads.items():
        noise = np.random.default_rng([zlib.crc32(name.encode()), seed]).standard_normal(out[name].shape)
        drawn = base * np.exp(spread * noise) if base else spread * noise
        out[name] = jnp.asarray(drawn.astype(out[name].dtype))
    for name, factor in factors.items():
        out[name] = (out[name] * factor).astype(out[name].dtype)
    return out
```

```python
import concourse.bass as bass
from concourse import mybir
from contextlib import ExitStack, contextmanager

F32 = mybir.dt.float32
I32 = mybir.dt.int32
U32 = mybir.dt.uint32
ALU = mybir.AluOpType
ACT = mybir.ActivationFunctionType
AX = mybir.AxisListType

N = 50000
P = 125
T = N // P
D = 64
W = D + 1
H = 3
F3 = D + 3
W3 = H * F3
R = 48
G = 8
NB = T // G
HALF = G // 2
SKIP = 65000.0
BIG = 1.0e30
EPS = 1e-5


def plain(eng, body):
    body(0, 0, 0)
    body(1, 1, 0)
    with eng.Fori(1, NB // 2) as r:
        body(r * 2, 0, r)
        body(r * 2 + 1, 1, r)


def ahead(eng, first, second):
    first(0, 0, 0)
    first(1, 1, 0)
    second(0, 0, 0)
    first(2, 0, 1)
    second(1, 1, 0)
    with eng.Fori(1, NB // 2 - 1) as r:
        first(r * 2 + 1, 1, r)
        second(r * 2, 0, r)
        first(r * 2 + 2, 0, r + 1)
        second(r * 2 + 1, 1, r)
    last = NB // 2 - 1
    first(NB - 1, 1, last)
    second(NB - 2, 0, last)
    second(NB - 1, 1, last)


def started(r):
    return not (isinstance(r, int) and r == 0)


class Chain:

    def __init__(self, eng, sem, per, start=0):
        self.eng, self.sem, self.per, self.start = eng, sem, per, start

    def at(self, b):
        self.base, self.n = b * self.per + self.start, 0

    def link(self, ins):
        self.n += 1
        ins.then_inc(self.sem, 1)
        self.eng.wait_ge(self.sem, self.base + self.n)

    def end(self):
        assert self.n == self.per, (self.n, self.per)


class Program:
    def __init__(self, nc, a, out, keep):
        self.nc, self.a, self.out = nc, a, out
        self.count = 0
        self.raised, self.taken, self.keep = {}, {}, keep

    def sem(self, ctx, name):
        mine = self.raised.setdefault(name, [])
        nth = self.taken.get(name, 0)
        self.taken[name] = nth + 1
        if nth == len(mine):
            mine.append(self.keep.enter_context(self.nc.semaphore(f"{name}{nth}")))
        return mine[nth]

    def pool_dma_sem(self, name):
        self.count += 1
        return self.keep.enter_context(self.nc.semaphore(f"{name}_{self.count}"))

    @contextmanager
    def stage(self):
        with ExitStack() as ctx:
            self.taken = {}
            yield ctx
            with self.nc.Block() as block:
                @block.sync
                def _(sp):
                    for name, n in self.taken.items():
                        for s in self.raised[name][:n]:
                            sp.sem_clear(s)

    def sb(self, ctx, name, shape, dt=F32):
        self.count += 1
        return ctx.enter_context(self.nc.sbuf_tensor(f"{name}_{self.count}", shape, dt))

    def ps(self, ctx, name, shape):
        self.count += 1
        return ctx.enter_context(self.nc.psum_tensor(f"{name}_{self.count}", shape, F32))


def cols(t, b):
    return t[:, bass.ds(b * G, G)]


def rows(dram, b, width):
    return dram.rearrange("(p t) d -> p t d", t=T)[:, bass.ds(b * G, G), 0:width]


def wide(ap, shape):
    return ap.to_broadcast(shape)



def setup(k, keep):
    nc, a, sb, sem = k.nc, k.a, k.sb, k.sem
    k.src = sb(keep, "src", [P, T], I32)
    k.dst = sb(keep, "dst", [P, T], I32)
    k.target = sb(keep, "target", [P, T], I32)
    k.weight = sb(keep, "weight", [P, T])
    k.cont = sb(keep, "cont", [P, T])
    k.pen_prev = sb(keep, "pen_prev", [P, T])
    k.pen_next = sb(keep, "pen_next", [P, T])
    k.pen_first = sb(keep, "pen_first", [P, T])
    k.pen_last = sb(keep, "pen_last", [P, T])
    k.eq = sb(keep, "eq", [P, 4, P])
    k.carry = sb(keep, "carry", [P, P])
    k.fix = sb(keep, "fix", [P, 1], I32)
    k.dinv = sb(keep, "dinv", [P, T])
    k.ident = sb(keep, "ident", [P, P])
    k.ones = sb(keep, "ones", [P, P])
    with k.stage() as ctx:
        nxt = sb(ctx, "nxt", [P, T], I32)
        prv = sb(ctx, "prv", [P, 1], I32)
        dstf = sb(ctx, "dstf", [P, T])
        nxtf = sb(ctx, "nxtf", [P, T])
        srcf = sb(ctx, "srcf", [P, T])
        prvf = sb(ctx, "prvf", [P, 1])
        hi = sb(ctx, "hi", [P, T])
        lo = sb(ctx, "lo", [P, T])
        tmp = sb(ctx, "tmp", [P, T])
        tmpi = sb(ctx, "tmpi", [P, T], I32)
        fixf = sb(ctx, "fixf", [P, 2])
        iota_i = sb(ctx, "iota_i", [P, T], I32)
        iota = sb(ctx, "iota", [P, T])
        part_i = sb(ctx, "part_i", [P, 1], I32)
        part = sb(ctx, "part", [P, 1])
        diag = sb(ctx, "diag", [P, 2, P])
        above = sb(ctx, "above", [P, P])
        ohp = sb(ctx, "ohp", [P, 2, G, P])
        oht = sb(ctx, "oht", [P, 2, G, T])
        zero = sb(ctx, "zero", [P, 2680])
        pos = sb(ctx, "pos", [P, T])
        XB = 40 * D
        xin = sb(ctx, "xin", [P, 2, XB])
        xout = sb(ctx, "xout", [P, 2, XB])
        ends = k.ps(ctx, "ends", [P, 2, 512])
        deg = k.ps(ctx, "deg", [P, T])
        s_pre, s_load, s_iota = sem(ctx, "s_pre"), sem(ctx, "s_load"), sem(ctx, "s_iota")
        s_v, s_diag, s_ends = sem(ctx, "s_v"), sem(ctx, "s_diag"), sem(ctx, "s_ends")
        s_oh, s_hist, s_clamp, s_root = (sem(ctx, n) for n in ("s_oh", "s_hist", "s_clamp", "s_root"))
        s_zero, s_zeroed = sem(ctx, "s_zero"), sem(ctx, "s_zeroed")
        s_x = [sem(ctx, "s_x") for _ in range(2)]
        s_y, s_st = sem(ctx, "s_y"), [sem(ctx, "s_st") for _ in range(2)]
        s_hv = sem(ctx, "s_hv")
        dst_pt = a["dst"].rearrange("(p t) -> p t", t=T)
        XN = T * D // XB
        with nc.Block() as block:

            @block.sync
            def _(sp):
                sp.dma_start(k.dst[:, :], dst_pt).then_inc(s_load, 16)
                sp.dma_start(k.src[:, :], a["src"].rearrange("(p t) -> p t", t=T)).then_inc(s_load, 16)
                sp.dma_start(k.weight[:, :], a["edge_weight"].rearrange("(p t) -> p t", t=T)).then_inc(s_load, 16)
                sp.wait_ge(s_pre, 2)
                sp.dma_start(nxt[0:P - 1, :], a["dst"][1:1 + (P - 1) * T].rearrange("(p t) -> p t", t=T)).then_inc(s_load, 16)
                sp.dma_start(nxt[P - 1:P, 0:T - 1], a["dst"][N - T + 1:N].unsqueeze(0)).then_inc(s_load, 16)
                sp.dma_start(prv[1:P, :], dst_pt[0:P - 1, T - 1:T], allow_slow_non_contiguous=True).then_inc(s_load, 16)
                xv = a["x"].rearrange("(p t) d -> p (t d)", t=T)
                yv = k.scaled.rearrange("(p t) d -> p (t d)", t=T)
                for i in range(XN):
                    if i >= 2:
                        sp.wait_ge(s_y, i - 1)
                    sp.dma_start(xin[:, i % 2, :], xv[:, i * XB:(i + 1) * XB]).then_inc(s_x[i % 2], 16)
                    if i >= 1:
                        sp.wait_ge(s_y, i)
                        sp.dma_start(yv[:, (i - 1) * XB:i * XB], xout[:, (i - 1) % 2, :]).then_inc(s_st[(i - 1) % 2], 16)
                sp.wait_ge(s_y, XN)
                sp.dma_start(yv[:, (XN - 1) * XB:], xout[:, (XN - 1) % 2, :]).then_inc(s_st[(XN - 1) % 2], 16)
                for h in range(2):
                    sp.wait_ge(s_st[h], 16 * XN // 2)

            @block.gpsimd
            def _(pool):
                pool.memset(nxt[:, :], -1).then_inc(s_pre, 1)
                pool.memset(prv[:, :], -1).then_inc(s_pre, 1)
                pool.iota(iota_i[:, :], [[1, T]], base=0, channel_multiplier=0).then_inc(s_iota, 1)
                pool.iota(part_i[:, :], [[0, 1]], base=0, channel_multiplier=1).then_inc(s_iota, 1)

            @block.vector
            def _(dve):
                c = Chain(dve, s_v, 0)
                c.at(0)
                link = c.link
                dve.memset(zero[:, :], 0.0).then_inc(s_zero, 1)
                link(dve.memset(k.ones[:, :], 1.0))
                dve.wait_ge(s_iota, 2)
                link(dve.tensor_copy(iota[:, :], iota_i[:, :]))
                link(dve.tensor_copy(part[:, :], part_i[:, :]))
                link(dve.tensor_scalar(k.ident[:, :], iota[:, 0:P], part[:, 0:1], None, ALU.is_equal))
                link(dve.tensor_scalar(above[:, :], iota[:, 0:P], part[:, 0:1], None, ALU.is_gt))
                dve.wait_ge(s_load, 6 * 16)
                link(dve.tensor_copy(dstf[:, :], k.dst[:, :]))
                link(dve.tensor_copy(srcf[:, :], k.src[:, :]))
                link(dve.tensor_copy(nxtf[:, :], nxt[:, :]))
                link(dve.tensor_copy(prvf[:, :], prv[:, :]))
                for i, t in enumerate((0, T - 1)):
                    link(dve.tensor_scalar(diag[:, i, :], k.ident[:, :], dstf[:, t:t + 1], None, ALU.mult))
                dve.sem_inc(s_diag, 1)
                link(dve.memset(k.cont[:, 0:1], 0.0))
                link(dve.tensor_tensor(k.cont[:, 1:T], dstf[:, 1:T], dstf[:, 0:T - 1], ALU.is_equal))
                link(dve.tensor_scalar(k.pen_prev[:, :], k.cont[:, :], -1.0, BIG, ALU.add, ALU.mult))
                link(dve.memset(k.pen_next[:, T - 1:T], -BIG))
                link(dve.tensor_copy(k.pen_next[:, 0:T - 1], k.pen_prev[:, 1:T]))
                link(dve.tensor_scalar(k.pen_first[:, :], dstf[:, :], dstf[:, 0:1], -BIG, ALU.not_equal, ALU.mult))
                link(dve.tensor_scalar(k.pen_last[:, :], dstf[:, :], dstf[:, T - 1:T], -BIG, ALU.not_equal, ALU.mult))
                link(dve.tensor_tensor(tmp[:, :], dstf[:, :], nxtf[:, :], ALU.not_equal))
                link(dve.scalar_tensor_tensor(tmp[:, :], dstf[:, :], -SKIP, tmp[:, :], ALU.add, ALU.mult))
                link(dve.tensor_scalar(tmp[:, :], tmp[:, :], SKIP, None, ALU.add))
                link(dve.tensor_copy(k.target[:, :], tmp[:, :]))
                link(dve.tensor_tensor(fixf[:, 0:1], prvf[:, :], dstf[:, 0:1], ALU.is_equal))
                link(dve.tensor_tensor(fixf[:, 1:2], nxtf[:, T - 1:T], dstf[:, 0:1], ALU.not_equal))
                link(dve.tensor_tensor(fixf[:, 0:1], fixf[:, 0:1], fixf[:, 1:2], ALU.mult))
                link(dve.scalar_tensor_tensor(fixf[:, 0:1], dstf[:, 0:1], -SKIP, fixf[:, 0:1], ALU.add, ALU.mult))
                link(dve.tensor_scalar(fixf[:, 0:1], fixf[:, 0:1], SKIP, None, ALU.add))
                link(dve.tensor_copy(k.fix[:, :], fixf[:, 0:1]))
                dve.wait_ge(s_ends, 1)
                for i in range(2):
                    for j, t in enumerate((0, T - 1)):
                        link(dve.tensor_scalar(k.eq[:, 2 * i + j, :], ends[:, i, 0:P], dstf[:, t:t + 1], -BIG, ALU.not_equal, ALU.mult))
                link(dve.scalar_tensor_tensor(k.carry[:, :], ends[:, 0, 0:P], dstf[:, T - 1:T], above[:, :], ALU.is_equal, ALU.mult))
                link(dve.tensor_scalar(tmp[:, :], srcf[:, :], 1.0 / T, None, ALU.mult))
                link(dve.tensor_copy(tmpi[:, :], tmp[:, :]))
                link(dve.tensor_copy(hi[:, :], tmpi[:, :]))
                link(dve.scalar_tensor_tensor(lo[:, :], hi[:, :], -float(T), srcf[:, :], ALU.mult, ALU.add))
                link(dve.tensor_scalar(tmp[:, :], lo[:, :], 0.0, None, ALU.is_lt))
                link(dve.tensor_tensor(hi[:, :], hi[:, :], tmp[:, :], ALU.subtract))
                link(dve.scalar_tensor_tensor(lo[:, :], tmp[:, :], float(T), lo[:, :], ALU.mult, ALU.add))
                link(dve.tensor_scalar(tmp[:, :], lo[:, :], float(T), None, ALU.is_ge))
                link(dve.tensor_tensor(hi[:, :], hi[:, :], tmp[:, :], ALU.add))
                link(dve.scalar_tensor_tensor(lo[:, :], tmp[:, :], -float(T), lo[:, :], ALU.mult, ALU.add))

                def one_hots(b, h, r):
                    if started(r):
                        dve.wait_ge(s_hist, b - 1)
                    for u in range(G):
                        t = bass.ds(b * G + u, 1)
                        dve.tensor_scalar(ohp[:, h, u, :], iota[:, 0:P], hi[:, t], k.weight[:, t], ALU.is_equal, ALU.mult).then_inc(s_hv, 1)
                        dve.tensor_scalar(oht[:, h, u, :], iota[:, :], lo[:, t], None, ALU.is_equal).then_inc(s_hv, 1)
                plain(dve, one_hots)
                dve.wait_ge(s_hist, NB)
                link(dve.tensor_scalar(pos[:, :], deg[:, :], 0.0, None, ALU.is_gt))
                dve.tensor_scalar(tmp[:, :], deg[:, :], 1e-12, None, ALU.max).then_inc(s_clamp, 1)
                dve.wait_ge(s_root, 1)
                link(dve.reciprocal(k.dinv[:, :], tmp[:, :]))
                link(dve.tensor_tensor(k.dinv[:, :], k.dinv[:, :], pos[:, :], ALU.mult))
                for i in range(XN):
                    dve.wait_ge(s_x[i % 2], 16 * (i // 2 + 1))
                    if i >= 2:
                        dve.wait_ge(s_st[i % 2], 16 * (i // 2))
                    dve.tensor_tensor(xout[:, i % 2, :].rearrange("p (t d) -> p t d", d=D), xin[:, i % 2, :].rearrange("p (t d) -> p t d", d=D),
                                      wide(k.dinv[:, i * 40:(i + 1) * 40].unsqueeze(2), [P, 40, D]), ALU.mult).then_inc(s_y, 1)

            @block.tensor
            def _(pe):
                pe.wait_ge(s_diag, 1)
                pe.matmul(ends[:, 0, 0:P], k.ones[:, :], diag[:, 0, :], start=True, stop=True)
                pe.matmul(ends[:, 1, 0:P], k.ones[:, :], diag[:, 1, :], start=True, stop=True).then_inc(s_ends, 1)

                def histogram(b, h, r):
                    pe.wait_ge(s_hv, b * 2 * G + 2 * G)
                    for u in range(G):
                        ins = pe.matmul(deg[:, :], ohp[:, h, u, :], oht[:, h, u, :], start=isinstance(b, int) and b == 0 and u == 0,
                                        stop=False, skip_group_check=True)
                    ins.then_inc(s_hist, 1)
                plain(pe, histogram)

            @block.scalar
            def _(act):
                act.wait_ge(s_zero, 1)
                n = 0
                for table, width in ((k.agg, W), (k.agg3, W3)):
                    flat = table.rearrange("(p t) d -> p (t d)", t=T)
                    for i in range(0, T * width, 2680):
                        j = min(i + 2680, T * width)
                        act.dma_start(flat[:, i:j], zero[:, 0:j - i]).then_inc(s_zeroed, 16)
                        n += 1
                act.wait_ge(s_clamp, 1)
                act.activation(tmp[:, :], tmp[:, :], ACT.Sqrt).then_inc(s_root, 1)
                act.wait_ge(s_zeroed, 16 * n)


class Edges:

    def __init__(self, k, ctx, gathers, width):
        self.k, self.width = k, width
        self.gathers = [(index, table, k.sb(ctx, "rows", [P, 2, G, w]), k.sb(ctx, "now", [P, 2, G], I32)) for index, table, w in gathers]
        self.s_rows = [k.pool_dma_sem("s_rows") for _ in range(2)]
        self.s_used = k.sem(ctx, "s_used")
        self.s_index = k.sem(ctx, "s_index")
        self.s_pool = k.sem(ctx, "s_pool")
        self.landed = 16 * G * len(self.gathers)
        if width:
            self.messages = k.sb(ctx, "messages", [P, G, width])
            self.sums = k.sb(ctx, "sums", [P, 2, G, width])
            self.to = k.sb(ctx, "to", [P, 2, G], I32)
            self.mend = k.sb(ctx, "mend", [P, width])
            self.carried = k.ps(ctx, "carried", [P, width])
            self.s_sums = k.sem(ctx, "s_sums")
            self.s_sent = [k.pool_dma_sem("s_sent") for _ in range(2)]
            self.s_to = k.sem(ctx, "s_to")
            self.s_mend0 = k.sem(ctx, "s_mend0")
            self.s_mend = k.sem(ctx, "s_mend")
            self.s_carried = k.sem(ctx, "s_carried")
            self.s_mended = k.pool_dma_sem("s_mended")

    def pool(self, pool, agg):
        k = self.k

        def gather(b, h, r):
            if started(r):
                pool.wait_ge(self.s_used, b - 1)
                pool.sem_inc(self.s_pool, 1)
            for index, _, _, now in self.gathers:
                pool.tensor_copy(now[:, h, :], cols(index, b)).then_inc(self.s_index, 1)
            pool.wait_ge(self.s_index, b * len(self.gathers) + len(self.gathers))
            pool.sem_inc(self.s_pool, 1)
            for index, table, ring, now in self.gathers:
                for u in range(G):
                    pool.indirect_dma_start(ring[:, h, u, :], None, table, bass.IndirectOffsetOnAxis(ap=now[:, h, u:u + 1].bitcast(U32), axis=0)).then_inc(self.s_rows[h], 16)

        def scatter(b, h, r):
            pool.wait_ge(self.s_sums, b + 1)
            pool.sem_inc(self.s_pool, 1)
            pool.tensor_copy(self.to[:, h, :], cols(k.target, b)).then_inc(self.s_to, 1)
            pool.wait_ge(self.s_to, b + 1)
            pool.sem_inc(self.s_pool, 1)
            for u in range(G):
                pool.indirect_dma_start(agg, bass.IndirectOffsetOnAxis(ap=self.to[:, h, u:u + 1].bitcast(U32), axis=0), self.sums[:, h, u, :], None,
                                        bounds_check=N - 1, oob_is_err=False).then_inc(self.s_sent[h], 16)

        if not self.width:
            plain(pool, gather)
            return
        if self.gathers:
            ahead(pool, gather, scatter)
        else:
            plain(pool, scatter)
        fix = bass.IndirectOffsetOnAxis(ap=k.fix[:, :].bitcast(U32), axis=0)
        for h in range(2):
            pool.wait_ge(self.s_sent[h], 16 * G * NB // 2)
        pool.wait_ge(self.s_mend0, 1)
        pool.indirect_dma_start(self.mend[:, :], None, agg, fix, bounds_check=N - 1, oob_is_err=False).then_inc(self.s_mended, 16)
        pool.wait_ge(self.s_mend, 1)
        pool.indirect_dma_start(agg, fix, self.mend[:, :], None, bounds_check=N - 1, oob_is_err=False).then_inc(self.s_mended, 16)
        pool.wait_ge(self.s_mended, 32)

    def tensor_mend(self, pe):
        pe.wait_ge(self.s_sums, NB)
        pe.matmul(self.carried[:, :], self.k.carry[:, :], self.sums[:, 1, G - 1, :], start=True, stop=True).then_inc(self.s_carried, 1)

    def vector_start(self, dve, link):
        link(dve.memset(self.sums[:, 1, G - 1, :], 0.0))
        link(dve.memset(self.messages[:, :, :], 1.0))
        dve.memset(self.mend[:, :], 0.0).then_inc(self.s_mend0, 1)

    def vector_sums(self, dve, link, b, h, r):
        for u in range(G):
            before = self.sums[:, h, u - 1, :] if u else self.sums[:, 1 - h, G - 1, :]
            link(dve.scalar_tensor_tensor(self.sums[:, h, u, :], before, self.k.cont[:, bass.ds(b * G + u, 1)],
                                          self.messages[:, u, :], ALU.mult, ALU.add))
        dve.sem_inc(self.s_sums, 1)

    def vector_sent(self, dve, h, r):
        if started(r):
            dve.wait_ge(self.s_sent[h], r * (16 * G))

    def vector_mend(self, dve):
        dve.wait_ge(self.s_carried, 1)
        dve.wait_ge(self.s_mended, 16)
        dve.tensor_tensor(self.mend[:, :], self.mend[:, :], self.carried[:, :], ALU.add).then_inc(self.s_mend, 1)


def cheb_edges(k, table):
    nc = k.nc
    with k.stage() as ctx:
        e = Edges(k, ctx, [(k.src, table, D)], W)
        s_v = k.sem(ctx, "s_v")
        ring = e.gathers[0][2]
        with nc.Block() as block:

            @block.gpsimd
            def _(pool):
                e.pool(pool, k.agg)

            @block.tensor
            def _(pe):
                e.tensor_mend(pe)

            @block.vector
            def _(dve):
                c = Chain(dve, s_v, 1 + G, start=2)
                c.base, c.n = 0, 0
                e.vector_start(dve, c.link)

                def body(b, h, r):
                    c.at(b)
                    dve.wait_ge(e.s_rows[h], r * e.landed + e.landed)
                    c.link(dve.tensor_tensor(e.messages[:, :, 0:D], ring[:, h, :, :], wide(cols(k.weight, b).unsqueeze(2), [P, G, D]), ALU.mult))
                    dve.sem_inc(e.s_used, 1)
                    e.vector_sent(dve, h, r)
                    e.vector_sums(dve, c.link, b, h, r)
                    c.end()
                plain(dve, body)
                e.vector_mend(dve)


def filter_edges(k, table):
    nc, a, sb, sem, ps = k.nc, k.a, k.sb, k.sem, k.ps
    HC = HALF * P
    with k.stage() as ctx:
        e = Edges(k, ctx, [(k.src, table, D)], W)
        ring = e.gathers[0][2]
        stack = sb(ctx, "stack", [P, 2, G, 2 * D])
        stackT = sb(ctx, "stackT", [2 * D, 2, HC])
        act_in = sb(ctx, "act_in", [D, 2, HC])
        soft = sb(ctx, "soft", [D + 1, 2, HC])
        w1 = sb(ctx, "w1", [R + 1, D])
        w2 = sb(ctx, "w2", [D + 1, D])
        w3 = sb(ctx, "w3", [D, D])
        w3T = sb(ctx, "w3T", [D, D])
        w4 = sb(ctx, "w4", [D, D])
        w34 = sb(ctx, "w34", [D, D])
        w34_low = sb(ctx, "w34_low", [2 * D, D])
        b3 = sb(ctx, "b3", [D, 1])
        b4 = sb(ctx, "b4", [1, D])
        b34 = sb(ctx, "b34", [1, D])
        pT = ps(ctx, "pT", [2 * D, 2, 512])
        pZ = ps(ctx, "pZ", [D, 2, 512])
        pH = ps(ctx, "pH", [P, G * D])
        pE = ps(ctx, "pE", [P, G * D])
        s_v, s_a = sem(ctx, "s_v"), sem(ctx, "s_a")
        s_w, s_w34, s_fold, s_low, s_one = (sem(ctx, n) for n in ("s_w", "s_w34", "s_fold", "s_low", "s_one"))
        s_in = [sem(ctx, "s_in") for _ in range(2)]
        s_T, s_Ts, s_Z, s_zb, s_zc, s_sp, s_soft, s_HE = (sem(ctx, n) for n in ("s_T", "s_Ts", "s_Z", "s_zb", "s_zc", "s_sp", "s_soft", "s_HE"))
        s_msg = sem(ctx, "s_msg")
        zb = sb(ctx, "zb", [D, 2, HC])
        with nc.Block() as block:

            @block.sync
            def _(sp):
                for t, x in ((w1[0:R, :], a["L1_gnn_W1"]), (w1[R:R + 1, :], a["L1_gnn_b1"].unsqueeze(0)), (w2[0:D, :], a["L1_gnn_W2"]),
                             (w2[D:D + 1, :], a["L1_gnn_b2"].unsqueeze(0)), (w3[:, :], a["L1_gnn_W3"]), (w4[:, :], a["L1_gnn_W4"]),
                             (b3[:, :], a["L1_gnn_b3"].unsqueeze(1)), (b4[:, :], a["L1_gnn_b4"].unsqueeze(0))):
                    sp.dma_start(t, x).then_inc(s_w, 16)
                sp.wait_ge(s_fold, 3)
                sp.dma_start(w34_low[D:2 * D, :], w34[:, :]).then_inc(s_low, 16)
                sp.wait_ge(s_one, 2)

                def load(b, h, r):
                    if started(r):
                        sp.wait_ge(s_T, b - 1)
                    sp.dma_start(stack[:, h, :, 0:R], rows(a["edge_attr_48"], b, R)).then_inc(s_in[h], 16)
                    sp.dma_start(stack[:, h, :, D:2 * D], rows(a["edge_attr_64"], b, D)).then_inc(s_in[h], 16)
                plain(sp, load)

            @block.gpsimd
            def _(pool):
                e.pool(pool, k.agg)

            @block.tensor
            def _(pe):
                pe.wait_ge(s_w, 8 * 16)
                pe.transpose(pT[0:D, 0, 0:D], w3[:, :], k.ident[0:D, 0:D]).then_inc(s_w34, 1)
                pe.wait_ge(s_fold, 1)
                pe.matmul(pH[0:D, 0:D], w3T[:, :], w4[:, :], start=True, stop=True)
                pe.matmul(pE[0:1, 0:D], b3[:, :], w4[:, :], start=True, stop=False)
                pe.matmul(pE[0:1, 0:D], k.ones[0:1, 0:1], b4[:, :], start=False, stop=True).then_inc(s_w34, 1)
                pe.wait_ge(s_fold, 3)
                pe.wait_ge(s_low, 16)

                def transposes(b, h, r):
                    pe.wait_ge(s_in[h], r * 32 + 32)
                    if not (isinstance(b, int) and b == 0):
                        pe.wait_ge(s_Ts, b)
                    pe.sem_inc(k.s_pe, 1)
                    for u in range(G):
                        ins = pe.transpose(pT[:, u // HALF, (u % HALF) * P:(u % HALF + 1) * P], stack[:, h, u, :], k.ident[:, :])
                    ins.then_inc(s_T, 1)

                def products(b, h, r):
                    pe.wait_ge(s_Ts, b + 1)
                    pe.sem_inc(k.s_pe, 1)
                    for j in range(2):
                        ins = pe.matmul(pZ[:, j, 0:HC], w1[:, :], stackT[0:R + 1, j, :], start=True, stop=True)
                    ins.then_inc(s_Z, 1)
                    if not (isinstance(b, int) and b == 0):
                        pe.wait_ge(s_msg, b)
                    pe.sem_inc(k.s_pe, 1)
                    for u in range(G):
                        t = (slice(None), u // HALF, slice((u % HALF) * P, (u % HALF + 1) * P))
                        pe.matmul(pE[:, u * D:(u + 1) * D], stackT[D:2 * D, t[1], t[2]], w34_low[D:2 * D, :], start=True, stop=False)
                        pe.matmul(pE[:, u * D:(u + 1) * D], k.ones[0:1, :], b34[:, :], start=False, stop=True)
                    pe.wait_ge(s_soft, b + 1)
                    pe.sem_inc(k.s_pe, 1)
                    for u in range(G):
                        t = (slice(None), u // HALF, slice((u % HALF) * P, (u % HALF + 1) * P))
                        ins = pe.matmul(pH[:, u * D:(u + 1) * D], soft[:, t[1], t[2]], w2[:, :], start=True, stop=True)
                    ins.then_inc(s_HE, 1)

                def both(b, h, r):
                    transposes(b, h, r)
                    products(b, h, r)
                plain(pe, both)
                e.tensor_mend(pe)

            @block.scalar
            def _(act):
                def body(b, h, r):
                    act.wait_ge(s_T, b + 1)
                    if not (isinstance(b, int) and b == 0):
                        act.wait_ge(s_HE, b)
                    act.activation(stackT[:, :, :], pT[:, :, 0:HC], ACT.Copy).then_inc(s_Ts, 1)
                    act.wait_ge(s_Z, b + 1)
                    act.activation(zb[:, :, :], pZ[:, :, 0:HC], ACT.Copy).then_inc(s_zb, 1)
                    act.wait_ge(s_zc, b + 1)
                    act.activation(act_in[:, :, :], act_in[:, :, :], ACT.Exp, scale=0.5).then_inc(s_a, 1)
                    act.wait_ge(s_a, b + 1)
                    act.activation(act_in[:, :, :], act_in[:, :, :], ACT.Ln, bias=1.0).then_inc(s_sp, 1)
                plain(act, body)

            @block.vector
            def _(dve):
                c = Chain(dve, s_v, 2 + G, start=2)
                c.base, c.n = 0, 0
                e.vector_start(dve, c.link)
                dve.memset(stack[:, :, :, R:D], 0.0).then_inc(s_one, 1)
                dve.wait_ge(s_one, 1)
                dve.memset(stack[:, :, :, R:R + 1], 1.0).then_inc(s_one, 1)
                dve.memset(soft[D:D + 1, :, :], 1.0)
                dve.wait_ge(s_w34, 1)
                dve.tensor_copy(w3T[:, :], pT[0:D, 0, 0:D]).then_inc(s_fold, 1)
                dve.wait_ge(s_w34, 2)
                dve.tensor_copy(w34[:, :], pH[0:D, 0:D]).then_inc(s_fold, 1)
                dve.tensor_copy(b34[:, :], pE[0:1, 0:D]).then_inc(s_fold, 1)

                def body(b, h, r):
                    c.at(b)
                    dve.wait_ge(s_zb, b + 1)
                    dve.tensor_scalar(act_in[:, :, :], zb[:, :, :], 28.0, None, ALU.min).then_inc(s_zc, 1)
                    dve.wait_ge(s_sp, b + 1)
                    dve.scalar_tensor_tensor(soft[0:D, :, :], act_in[:, :, :], 2.0, zb[:, :, :], ALU.mult, ALU.max).then_inc(s_soft, 1)
                    dve.wait_ge(s_HE, b + 1)
                    dve.wait_ge(e.s_rows[h], r * e.landed + e.landed)
                    c.link(dve.tensor_tensor(e.messages[:, :, 0:D], ring[:, h, :, :], pH[:, :].rearrange("p (u d) -> p u d", d=D), ALU.mult))
                    dve.sem_inc(e.s_used, 1)
                    c.link(dve.tensor_tensor(e.messages[:, :, 0:D], e.messages[:, :, 0:D], pE[:, :].rearrange("p (u d) -> p u d", d=D), ALU.add))
                    dve.sem_inc(s_msg, 1)
                    e.vector_sent(dve, h, r)
                    e.vector_sums(dve, c.link, b, h, r)
                    c.end()
                plain(dve, body)
                e.vector_mend(dve)


def segment_softmax(k, logits, heads):
    nc, sb, sem = k.nc, k.sb, k.sem
    with k.stage() as ctx:
        top = sb(ctx, "top", [P, T])
        full = sb(ctx, "full", [P, T])
        diag = sb(ctx, "diag", [P, 2, P])
        cand = sb(ctx, "cand", [P, 4, P])
        best = sb(ctx, "best", [P, 4])
        both = sb(ctx, "both", [P, 2])
        ends = k.ps(ctx, "ends", [P, 2, 512])
        s_v, s_diag, s_ends, s_ready, s_exp = (sem(ctx, n) for n in ("s_v", "s_diag", "s_ends", "s_ready", "s_exp"))
        with nc.Block() as block:

            @block.vector
            def _(dve):
                c = Chain(dve, s_v, 0)
                c.at(0)
                link = c.link
                for i in range(heads):
                    one = logits[:, :, i]
                    link(dve.tensor_tensor_scan(top[:, :], k.pen_prev[:, :], one, -BIG, ALU.add, ALU.max))
                    link(dve.tensor_tensor_scan(full[:, ::-1], k.pen_next[:, ::-1], top[:, ::-1], -BIG, ALU.add, ALU.max))
                    for j, t in enumerate((0, T - 1)):
                        link(dve.tensor_scalar(diag[:, j, :], k.ident[:, :], full[:, t:t + 1], None, ALU.mult))
                    dve.sem_inc(s_diag, 1)
                    dve.wait_ge(s_ends, i + 1)
                    for j in range(4):
                        link(dve.tensor_tensor(cand[:, j, :], ends[:, j // 2, 0:P], k.eq[:, j, :], ALU.add))
                    link(dve.tensor_reduce(best[:, :], cand[:, :, :], AX.X, ALU.max))
                    link(dve.tensor_tensor(both[:, :], best[:, 0:2], best[:, 2:4], ALU.max))
                    link(dve.scalar_tensor_tensor(full[:, :], k.pen_first[:, :], both[:, 0:1], full[:, :], ALU.add, ALU.max))
                    link(dve.scalar_tensor_tensor(full[:, :], k.pen_last[:, :], both[:, 1:2], full[:, :], ALU.add, ALU.max))
                    dve.tensor_tensor(one, one, full[:, :], ALU.subtract).then_inc(s_ready, 1)
                    dve.wait_ge(s_ready, i + 1)

            @block.tensor
            def _(pe):
                for i in range(heads):
                    pe.wait_ge(s_diag, i + 1)
                    pe.matmul(ends[:, 0, 0:P], k.ones[:, :], diag[:, 0, :], start=True, stop=True)
                    pe.matmul(ends[:, 1, 0:P], k.ones[:, :], diag[:, 1, :], start=True, stop=True).then_inc(s_ends, 1)

            @block.scalar
            def _(act):
                act.wait_ge(s_ready, heads)
                act.activation(logits[:, :, :], logits[:, :, :], ACT.Exp).then_inc(s_exp, 1)
                act.wait_ge(s_exp, 1)


def attend_logits(k, kept, logits, table, near):
    nc, a, sb, sem = k.nc, k.a, k.sb, k.sem
    with k.stage() as ctx:
        e = Edges(k, ctx, [(k.src, table, D), (k.dst, near, 1)], 0)
        ring, er = e.gathers[0][2], e.gathers[1][2]
        al = sb(ctx, "al", [P, D])
        prod = sb(ctx, "prod", [P, G, D])
        red = sb(ctx, "red", [P, G])
        s_al, s_v, s_kept = sem(ctx, "s_al"), sem(ctx, "s_v"), sem(ctx, "s_kept")
        with nc.Block() as block:

            @block.sync
            def _(sp):
                sp.dma_start(al[:, :], a["L2_gnn_al"].rearrange("d o -> (d o)").partition_broadcast(P)).then_inc(s_al, 16)

            @block.gpsimd
            def _(pool):
                e.pool(pool, None)

            @block.scalar
            def _(act):
                def keep(b, h, r):
                    act.wait_ge(e.s_rows[h], r * e.landed + e.landed)
                    act.sem_inc(k.s_act, 1)
                    act.activation(kept[:, bass.ds(b * G, G), 0:D], ring[:, h, :, :], ACT.Copy).then_inc(s_kept, 1)
                plain(act, keep)

            @block.vector
            def _(dve):
                c = Chain(dve, s_v, 4, start=1)
                c.base, c.n = 0, 0
                c.link(dve.memset(kept[:, :, D:D + 1], 1.0))
                dve.wait_ge(s_al, 16)

                def body(b, h, r):
                    c.at(b)
                    dve.wait_ge(e.s_rows[h], r * e.landed + e.landed)
                    c.link(dve.tensor_tensor(prod[:, :, :], ring[:, h, :, :], wide(al[:, :].unsqueeze(1), [P, G, D]), ALU.mult))
                    c.link(dve.tensor_reduce(red[:, :], prod[:, :, :], AX.X, ALU.add))
                    c.link(dve.tensor_tensor(red[:, :], red[:, :], er[:, h, :, 0], ALU.add))
                    c.link(dve.scalar_tensor_tensor(logits[:, bass.ds(b * G, G), 0], red[:, :], 0.01, red[:, :], ALU.mult, ALU.max))
                    dve.wait_ge(s_kept, b + 1)
                    dve.sem_inc(e.s_used, 1)
                    c.end()
                plain(dve, body)


def attend_sums(k, kept, logits, agg, heads, features):
    nc = k.nc
    with k.stage() as ctx:
        e = Edges(k, ctx, [], heads * features)
        s_v = k.sem(ctx, "s_v")
        with nc.Block() as block:

            @block.gpsimd
            def _(pool):
                e.pool(pool, agg)

            @block.tensor
            def _(pe):
                e.tensor_mend(pe)

            @block.vector
            def _(dve):
                c = Chain(dve, s_v, 1 + G, start=2)
                c.base, c.n = 0, 0
                e.vector_start(dve, c.link)

                def body(b, h, r):
                    c.at(b)
                    if heads == 1:
                        rows_, ex = kept[:, bass.ds(b * G, G), :], wide(logits[:, bass.ds(b * G, G), :], [P, G, features])
                        out = e.messages[:, :, :]
                    else:
                        rows_ = wide(kept[:, bass.ds(b * G, G), :].unsqueeze(2), [P, G, heads, features])
                        ex = wide(logits[:, bass.ds(b * G, G), :].unsqueeze(3), [P, G, heads, features])
                        out = e.messages[:, :, :].rearrange("p u (i f) -> p u i f", i=heads)
                    c.link(dve.tensor_tensor(out, rows_, ex, ALU.mult))
                    e.vector_sent(dve, h, r)
                    e.vector_sums(dve, c.link, b, h, r)
                    c.end()
                plain(dve, body)
                e.vector_mend(dve)


def transformer_logits(k, kept, logits, table):
    nc, a, sb, sem, ps = k.nc, k.a, k.sb, k.sem, k.ps
    HC = HALF * P
    with k.stage() as ctx:
        e = Edges(k, ctx, [(k.src, table, D), (k.dst, table, D)], 0)
        near, far = e.gathers[0][2], e.gathers[1][2]
        farT = sb(ctx, "farT", [D + 1, 2, HC])
        prod = sb(ctx, "prod", [P, 2, H, F3])
        red = sb(ctx, "red", [P, G, H])
        wq = sb(ctx, "wq", [D, H, D + 1])
        wk = sb(ctx, "wk", [D, H, F3])
        fold = sb(ctx, "fold", [D + 1, W3])
        ea = sb(ctx, "ea", [P, T * 2])
        pT = ps(ctx, "pT", [D, 2, 512])
        pU = ps(ctx, "pU", [P, 4, 512])
        s_w, s_fold, s_ea, s_v, s_kept, s_T, s_Ts, s_U, s_dot, s_c = (
            sem(ctx, n) for n in ("s_w", "s_fold", "s_ea", "s_v", "s_kept", "s_T", "s_Ts", "s_U", "s_dot", "s_c"))
        with nc.Block() as block:

            @block.sync
            def _(sp):
                sp.dma_start(ea[:, :], a["edge_attr_2"].rearrange("(p t) f -> p (t f)", t=T)).then_inc(s_ea, 16)
                for i in range(H):
                    sp.dma_start(wq[:, i, 0:D], a["L3_gnn_Wq"][i, :, :]).then_inc(s_w, 16)
                    sp.dma_start(wq[:, i, D:D + 1], a["L3_gnn_bq"][i, :].unsqueeze(1)).then_inc(s_w, 16)
                    sp.dma_start(wk[:, i, 0:D], a["L3_gnn_Wk"][i, :, :]).then_inc(s_w, 16)
                    sp.dma_start(wk[:, i, D:D + 2], a["L3_gnn_We"][i, :, :]).then_inc(s_w, 16)
                    sp.dma_start(wk[:, i, D + 2:D + 3], a["L3_gnn_bk"][i, :].unsqueeze(1)).then_inc(s_w, 16)

            @block.gpsimd
            def _(pool):
                e.pool(pool, None)

            @block.scalar
            def _(act):
                def body(b, h, r):
                    act.wait_ge(e.s_rows[h], r * e.landed + e.landed)
                    act.sem_inc(k.s_act, 1)
                    act.activation(kept[:, bass.ds(b * G, G), 0:D], near[:, h, :, :], ACT.Copy).then_inc(s_kept, 1)
                    act.wait_ge(s_T, b + 1)
                    if not (isinstance(b, int) and b == 0):
                        act.wait_ge(s_U, b)
                    act.activation(farT[0:D, :, :], pT[:, :, 0:HC], ACT.Copy).then_inc(s_Ts, 1)
                plain(act, body)

            @block.tensor
            def _(pe):
                pe.wait_ge(s_w, 16 * 5 * H)
                for i in range(H):
                    ins = pe.matmul(pU[0:D + 1, 0, i * F3:(i + 1) * F3], wq[:, i, :], wk[:, i, :], start=True, stop=True)
                ins.then_inc(s_fold, 1)
                pe.wait_ge(s_c, 4)

                def transposes(b, h, r):
                    pe.wait_ge(e.s_rows[h], r * e.landed + e.landed)
                    if not (isinstance(b, int) and b == 0):
                        pe.wait_ge(s_Ts, b)
                    pe.sem_inc(k.s_pe, 1)
                    for u in range(G):
                        ins = pe.transpose(pT[:, u // HALF, (u % HALF) * P:(u % HALF + 1) * P], far[:, h, u, :], k.ident[:, :])
                    ins.then_inc(s_T, 1)

                def products(b, h, r):
                    pe.wait_ge(s_Ts, b + 1)
                    if not (isinstance(b, int) and b == 0):
                        pe.wait_ge(s_dot, b)
                    pe.sem_inc(k.s_pe, 1)
                    for u in range(G):
                        ins = pe.matmul(pU[:, u // 2, (u % 2) * W3:(u % 2 + 1) * W3], farT[:, u // HALF, (u % HALF) * P:(u % HALF + 1) * P],
                                        fold[:, :], start=True, stop=True)
                    ins.then_inc(s_U, 1)

                def both(b, h, r):
                    transposes(b, h, r)
                    products(b, h, r)
                plain(pe, both)

            @block.vector
            def _(dve):
                dve.memset(kept[:, :, D + 2:D + 3], 1.0).then_inc(s_c, 1)
                dve.memset(farT[D:D + 1, :, :], 1.0).then_inc(s_c, 1)
                dve.wait_ge(s_ea, 16)
                dve.tensor_copy(kept[:, :, D:D + 2], ea[:, :].rearrange("p (t f) -> p t f", f=2)).then_inc(s_c, 1)
                dve.wait_ge(s_fold, 1)
                dve.tensor_copy(fold[:, :], pU[0:D + 1, 0, 0:W3]).then_inc(s_c, 1)
                dve.wait_ge(s_c, 4)
                c = Chain(dve, s_v, 9)

                def body(b, h, r):
                    c.at(b)
                    dve.wait_ge(s_U, b + 1)
                    dve.wait_ge(s_kept, b + 1)
                    for j in range(4):
                        c.link(dve.tensor_tensor(prod[:, :, :, :], pU[:, j, 0:2 * W3].rearrange("p (u i f) -> p u i f", u=2, i=H),
                                                 wide(kept[:, bass.ds(b * G + 2 * j, 2), :].unsqueeze(2), [P, 2, H, F3]), ALU.mult))
                        c.link(dve.tensor_reduce(red[:, 2 * j:2 * j + 2, :], prod[:, :, :, :], AX.X, ALU.add))
                    dve.sem_inc(s_dot, 1)
                    dve.sem_inc(e.s_used, 1)
                    c.link(dve.tensor_scalar(logits[:, bass.ds(b * G, G), :], red[:, :, :], float(D) ** -0.5, None, ALU.mult))
                    c.end()
                plain(dve, body)


def norm_steps(k, dve, link, r, tmp, stat, s_var, s_std, nth, out, eps=EPS):
    mean, var = stat[:, 0, :], stat[:, 1, :]
    link(dve.tensor_reduce(mean, r, AX.X, ALU.add))
    link(dve.tensor_scalar(mean, mean, 1.0 / D, None, ALU.mult))
    link(dve.tensor_tensor(r, r, wide(mean.unsqueeze(2), [P, G, D]), ALU.subtract))
    link(dve.tensor_tensor(tmp, r, r, ALU.mult))
    link(dve.tensor_reduce(var, tmp, AX.X, ALU.add))
    link(dve.tensor_scalar(var, var, 1.0 / D, eps, ALU.mult, ALU.add))
    dve.sem_inc(s_var, 1)
    dve.wait_ge(s_std, nth)
    link(dve.reciprocal(var, var))
    link(dve.tensor_tensor(out, r, wide(var.unsqueeze(2), [P, G, D]), ALU.mult))


def node_pass(k, kind, xs, agg_used, weights, bias, outs, skip=None):
    nc, a, sb, sem, ps = k.nc, k.a, k.sb, k.sem, k.ps
    HC = HALF * P
    product = kind != "filter"
    KD = D if kind == "attend" else 2 * D
    with k.stage() as ctx:
        agg = sb(ctx, "agg", [P, 2, G, W])
        left = sb(ctx, "left", [P, 2, G, D])
        stack = sb(ctx, "stack", [P, 2, G, KD])
        stackT = sb(ctx, "stackT", [KD, 2, HC])
        w = sb(ctx, "w", [KD, D])
        brow = sb(ctx, "brow", [1, D])
        arow = sb(ctx, "arow", [P, D])
        r_ = sb(ctx, "r", [P, G, D])
        tmp = sb(ctx, "tmp", [P, G, D])
        stat = sb(ctx, "stat", [P, 3, G])
        y = [sb(ctx, "y", [P, 2, G, o[1]]) for o in outs]
        pT = ps(ctx, "pT", [KD, 2, 512])
        pO = ps(ctx, "pO", [P, G * D])
        s_w, s_v, s_f, s_T, s_Ts, s_O, s_var, s_std, s_y, s_stack, s_a = (
            sem(ctx, n) for n in ("s_w", "s_v", "s_f", "s_T", "s_Ts", "s_O", "s_var", "s_std", "s_y", "s_stack", "s_a"))
        s_in = [sem(ctx, "s_in") for _ in range(2)]
        s_out = [sem(ctx, "s_out") for _ in range(2)]
        n_in = 1 + (xs is not None) + (skip is not None)
        n_w = len(weights) + (bias is not None) + (kind == "filter")
        with nc.Block() as block:

            @block.sync
            def _(sp):
                for i, x in enumerate(weights):
                    sp.dma_start(w[i * D:(i + 1) * D, :], x).then_inc(s_w, 16)
                if bias is not None:
                    sp.dma_start(brow[:, :], bias.unsqueeze(0)).then_inc(s_w, 16)
                if kind == "filter":
                    sp.dma_start(arow[:, :], a["L2_gnn_ar"].rearrange("d o -> (d o)").partition_broadcast(P)).then_inc(s_w, 16)

                def load(b, h, r):
                    sp.dma_start(agg[:, h, :, :], rows(k.agg, b, W)).then_inc(s_in[h], 16)
                    if xs is not None:
                        sp.dma_start(stack[:, h, :, 0:D], rows(xs, b, D)).then_inc(s_in[h], 16)
                    if skip is not None:
                        sp.dma_start(left[:, h, :, :], rows(skip, b, D)).then_inc(s_in[h], 16)

                def store(b, h, r):
                    sp.wait_ge(s_y, b + 1)
                    for t, o in zip(y, outs):
                        sp.dma_start(rows(o[0], b, o[1]), t[:, h, :, :]).then_inc(s_out[h], 16)
                ahead(sp, load, store)
                for h in range(2):
                    sp.wait_ge(s_out[h], 16 * len(outs) * NB // 2)

            if product:
                @block.tensor
                def _(pe):
                    pe.wait_ge(s_w, 16 * n_w)

                    def transposes(b, h, r):
                        pe.wait_ge(s_stack, b + 1)
                        if not (isinstance(b, int) and b == 0):
                            pe.wait_ge(s_Ts, b)
                        pe.sem_inc(k.s_pe, 1)
                        for u in range(G):
                            ins = pe.transpose(pT[:, u // HALF, (u % HALF) * P:(u % HALF + 1) * P], stack[:, h, u, :], k.ident[:, :])
                        ins.then_inc(s_T, 1)

                    def products(b, h, r):
                        pe.wait_ge(s_Ts, b + 1)
                        if not (isinstance(b, int) and b == 0):
                            pe.wait_ge(s_a, b)
                        pe.sem_inc(k.s_pe, 1)
                        for u in range(G):
                            last = bias is None
                            ins = pe.matmul(pO[:, u * D:(u + 1) * D], stackT[:, u // HALF, (u % HALF) * P:(u % HALF + 1) * P], w[:, :], start=True, stop=last)
                            if not last:
                                ins = pe.matmul(pO[:, u * D:(u + 1) * D], k.ones[0:1, :], brow[:, :], start=False, stop=True)
                        ins.then_inc(s_O, 1)

                    def both(b, h, r):
                        transposes(b, h, r)
                        products(b, h, r)
                    plain(pe, both)

            @block.scalar
            def _(act):
                def body(b, h, r):
                    if product:
                        act.wait_ge(s_T, b + 1)
                        if not (isinstance(b, int) and b == 0):
                            act.wait_ge(s_O, b)
                        act.activation(stackT[:, :, :], pT[:, :, 0:HC], ACT.Copy).then_inc(s_Ts, 1)
                    if kind != "cheb1":
                        act.wait_ge(s_var, b + 1)
                        act.activation(stat[:, 1, :], stat[:, 1, :], ACT.Sqrt).then_inc(s_std, 1)
                plain(act, body)

            @block.vector
            def _(dve):
                first = Chain(dve, s_f, {"attend": 3, "filter": 1}.get(kind, 1))
                c = Chain(dve, s_v, {"cheb1": 2, "cheb2": 9, "filter": 11, "attend": 9}[kind])
                dve.wait_ge(s_w, 16 * n_w)

                def stacking(b, h, r):
                    first.at(b)
                    dve.wait_ge(s_in[h], r * (16 * n_in) + 16 * n_in)
                    if kind == "filter":
                        first.link(dve.tensor_tensor(left[:, h, :, :], left[:, h, :, :], agg[:, h, :, 0:D], ALU.add))
                    elif kind == "attend":
                        den = stat[:, 2, :]
                        first.link(dve.tensor_scalar(den, agg[:, h, :, D], 1e-30, None, ALU.max))
                        first.link(dve.reciprocal(den, den))
                        first.link(dve.tensor_tensor(stack[:, h, :, :], agg[:, h, :, 0:D], wide(den.unsqueeze(2), [P, G, D]), ALU.mult))
                    else:
                        first.link(dve.scalar_tensor_tensor(stack[:, h, :, D:2 * D], agg[:, h, :, 0:D], -1.0, wide(cols(k.dinv, b).unsqueeze(2), [P, G, D]), ALU.mult, ALU.mult))
                    first.end()
                    dve.sem_inc(s_stack, 1)

                def rest(b, h, r):
                    c.at(b)
                    po = pO[:, :].rearrange("p (u d) -> p u d", d=D)
                    if product:
                        dve.wait_ge(s_O, b + 1)
                    if started(r):
                        dve.wait_ge(s_out[h], r * (16 * len(outs)))
                    if kind == "cheb1":
                        c.link(dve.tensor_scalar(y[0][:, h, :, :], po, 0.0, None, ALU.max))
                        dve.sem_inc(s_a, 1)
                        c.link(dve.tensor_tensor(y[1][:, h, :, :], y[0][:, h, :, :], wide(cols(k.dinv, b).unsqueeze(2), [P, G, D]), ALU.mult))
                    elif kind == "filter":
                        norm_steps(k, dve, c.link, left[:, h, :, :], tmp[:, :, :], stat, s_var, s_std, b + 1, y[0][:, h, :, :])
                        c.link(dve.tensor_tensor(tmp[:, :, :], y[0][:, h, :, :], wide(arow[:, :].unsqueeze(1), [P, G, D]), ALU.mult))
                        c.link(dve.tensor_reduce(y[1][:, h, :, :], tmp[:, :, :], AX.X, ALU.add))
                        c.link(dve.tensor_scalar(stat[:, 2, :], stat[:, 0, :], 1.0, None, ALU.mult))
                    else:
                        c.link(dve.tensor_tensor(r_[:, :, :], po, left[:, h, :, :], ALU.add))
                        dve.sem_inc(s_a, 1)
                        norm_steps(k, dve, c.link, r_[:, :, :], tmp[:, :, :], stat, s_var, s_std, b + 1, y[0][:, h, :, :])
                    dve.sem_inc(s_y, 1)
                    c.end()

                ahead(dve, stacking, rest)


def transformer_nodes(k, x, agg3, out):
    nc, a, sb, sem, ps = k.nc, k.a, k.sb, k.sem, k.ps
    HC = HALF * P
    with k.stage() as ctx:
        agg = sb(ctx, "agg", [P, 2, G, H, F3])
        xin = sb(ctx, "xin", [P, 2, G, W])
        aggT = sb(ctx, "aggT", [F3, H, P])
        aggT2 = sb(ctx, "aggT2", [F3, H, P])
        xT = sb(ctx, "xT", [W, P])
        xT2 = sb(ctx, "xT2", [W, P])
        nat = sb(ctx, "nat", [D, H, F3 + W])
        wv = sb(ctx, "wv", [F3, H, D])
        ws = sb(ctx, "ws", [W, H * D])
        gamma = sb(ctx, "gamma", [P, H, D])
        beta = sb(ctx, "beta", [P, H, D])
        o3 = sb(ctx, "o3", [P, G, H * D])
        s_ = sb(ctx, "s", [P, G, D])
        tmp = sb(ctx, "tmp", [P, G, D])
        stat = sb(ctx, "stat", [P, 3, G])
        den = sb(ctx, "den", [P, G, H])
        y = sb(ctx, "y", [P, 2, G, D])
        pT = [ps(ctx, "pT", [F3, 512]) for _ in range(2)]
        pO = [ps(ctx, "pO", [P, 512]) for _ in range(2)]
        names = ("s_w", "s_wT", "s_wc", "s_v", "s_f", "s_T", "s_Ts", "s_O", "s_Oc", "s_var", "s_std", "s_y", "s_stack", "s_one", "s_part", "s_o3")
        s_w, s_wT, s_wc, s_v, s_f, s_T, s_Ts, s_O, s_Oc, s_var, s_std, s_y, s_stack, s_one, s_part, s_o3 = (sem(ctx, n) for n in names)
        s_in = [sem(ctx, "s_in") for _ in range(2)]
        s_out = [sem(ctx, "s_out") for _ in range(2)]
        aT, xTs = [aggT, aggT2], [xT, xT2]
        with nc.Block() as block:

            @block.sync
            def _(sp):
                for i in range(H):
                    for t, src in ((nat[:, i, 0:D], a["L3_gnn_Wv"][i, :, :]), (nat[:, i, D:D + 2], a["L3_gnn_We"][i, :, :]),
                                   (nat[:, i, D + 2:F3], a["L3_gnn_bv"][i, :].unsqueeze(1)),
                                   (nat[:, i, F3:F3 + D], a["L3_gnn_Wskip"][i, :, :]), (nat[:, i, F3 + D:F3 + W], a["L3_gnn_bskip"][i, :].unsqueeze(1)),
                                   (gamma[:, i, :], a["L3_gnn_gamma"][i, :].partition_broadcast(P)), (beta[:, i, :], a["L3_gnn_beta"][i, :].partition_broadcast(P))):
                        sp.dma_start(t, src).then_inc(s_w, 16)
                sp.wait_ge(s_one, 1)

                def load(b, h, r):
                    sp.dma_start(agg[:, h, :, :, :].rearrange("p u i f -> p u (i f)"), rows(agg3, b, W3)).then_inc(s_in[h], 16)
                    sp.dma_start(xin[:, h, :, 0:D], rows(x, b, D)).then_inc(s_in[h], 16)

                def store(b, h, r):
                    sp.wait_ge(s_y, b + 1)
                    sp.dma_start(rows(out, b, D), y[:, h, :, :]).then_inc(s_out[h], 16)
                ahead(sp, load, store)
                for h in range(2):
                    sp.wait_ge(s_out[h], 16 * NB // 2)

            @block.tensor
            def _(pe):
                pe.wait_ge(s_w, 16 * 7 * H)
                for i in range(H):
                    if i:
                        pe.wait_ge(s_wc, 2 * i)
                    pe.transpose(pT[0][0:F3, 0:D], nat[:, i, 0:F3], k.ident[0:D, 0:D])
                    pe.transpose(pT[1][0:W, 0:D], nat[:, i, F3:F3 + W], k.ident[0:D, 0:D]).then_inc(s_wT, 1)
                pe.wait_ge(s_wc, 2 * H)

                def body(b, h, r):
                    pe.wait_ge(s_stack, b + 1)

                    def turn(u):
                        i = u % 2
                        if not (isinstance(b, int) and b == 0 and u < 2):
                            pe.wait_ge(s_Ts, b * G + u - 1)
                        pe.sem_inc(k.s_pe, 1)
                        for j in range(H):
                            pe.transpose(pT[i][:, j * P:(j + 1) * P], agg[:, h, u, j, :], k.ident[:, :])
                        pe.transpose(pT[i][0:W, H * P:H * P + P], xin[:, h, u, :], k.ident[:, :]).then_inc(s_T, 1)

                    def product(u):
                        i = u % 2
                        pe.wait_ge(s_Ts, b * G + u + 1)
                        if not (isinstance(b, int) and b == 0 and u < 2):
                            pe.wait_ge(s_Oc, b * G + u - 1)
                        pe.sem_inc(k.s_pe, 1)
                        pe.matmul(pO[i][:, 0:H * D], xTs[i][:, :], ws[:, :], start=True, stop=False, skip_group_check=True)
                        for j in range(H):
                            ins = pe.matmul(pO[i][:, j * D:(j + 1) * D], aT[i][:, j, :], wv[:, j, :], start=False, stop=True, skip_group_check=True)
                        ins.then_inc(s_O, 1)
                    turn(0)
                    for u in range(G):
                        if u + 1 < G:
                            turn(u + 1)
                        product(u)
                plain(pe, body)

            @block.scalar
            def _(act):
                for i in range(H):
                    act.wait_ge(s_wT, i + 1)
                    act.activation(wv[:, i, :], pT[0][0:F3, 0:D], ACT.Copy).then_inc(s_wc, 1)
                    act.activation(ws[:, i * D:(i + 1) * D], pT[1][0:W, 0:D], ACT.Copy).then_inc(s_wc, 1)

                def body(b, h, r):
                    for u in range(G + 1):
                        if u < G:
                            i = u % 2
                            act.wait_ge(s_T, b * G + u + 1)
                            if not (isinstance(b, int) and b == 0 and u < 2):
                                act.wait_ge(s_O, b * G + u - 1)
                            act.activation(aT[i][:, :, :], pT[i][:, 0:H * P].rearrange("f (i p) -> f i p", i=H), ACT.Copy).then_inc(s_part, 1)
                            act.activation(xTs[i][:, :], pT[i][0:W, H * P:H * P + P], ACT.Copy).then_inc(s_part, 1)
                            act.wait_ge(s_part, b * (2 * G) + 2 * u + 2)
                            act.sem_inc(s_Ts, 1)
                        if u:
                            i = (u - 1) % 2
                            if u == 1 and not (isinstance(b, int) and b == 0):
                                act.wait_ge(s_o3, b)
                            act.wait_ge(s_O, b * G + u)
                            act.activation(o3[:, u - 1, :], pO[i][:, 0:H * D], ACT.Copy).then_inc(s_Oc, 1)
                    for j in range(H + 1):
                        act.wait_ge(s_var, b * (H + 1) + j + 1)
                        act.activation(stat[:, 1, :], stat[:, 1, :], ACT.Sqrt).then_inc(s_std, 1)
                plain(act, body)

            @block.vector
            def _(dve):
                first = Chain(dve, s_f, 3)
                c = Chain(dve, s_v, H + H * (8 + 2) + 1 + 8)
                dve.memset(xin[:, :, :, D:W], 1.0).then_inc(s_one, 1)
                dve.wait_ge(s_w, 16 * 7 * H)

                def stacking(b, h, r):
                    first.at(b)
                    dve.wait_ge(s_in[h], r * 32 + 32)
                    first.link(dve.tensor_scalar(den[:, :, :], agg[:, h, :, :, F3 - 1], 1e-30, None, ALU.max))
                    first.link(dve.reciprocal(den[:, :, :], den[:, :, :]))
                    first.link(dve.tensor_tensor(agg[:, h, :, :, :], agg[:, h, :, :, :], wide(den[:, :, :].unsqueeze(3), [P, G, H, F3]), ALU.mult))
                    first.end()
                    dve.sem_inc(s_stack, 1)

                def rest(b, h, r):
                    c.at(b)
                    dve.wait_ge(s_Oc, b * G + G)
                    s = s_[:, :, :]
                    c.link(dve.tensor_scalar(s, o3[:, :, 0:D], 1.0, None, ALU.mult))
                    for j in range(H):
                        if j:
                            c.link(dve.tensor_tensor(s, s, o3[:, :, j * D:(j + 1) * D], ALU.add))
                        if j == H - 1:
                            dve.sem_inc(s_o3, 1)
                        norm_steps(k, dve, c.link, s, tmp[:, :, :], stat, s_var, s_std, b * (H + 1) + j + 1, s)
                        c.link(dve.tensor_tensor(s, s, wide(gamma[:, j, :].unsqueeze(1), [P, G, D]), ALU.mult))
                        c.link(dve.tensor_tensor(s, s, wide(beta[:, j, :].unsqueeze(1), [P, G, D]), ALU.add))
                    c.link(dve.scalar_tensor_tensor(s, s, 0.0, xin[:, h, :, 0:D], ALU.max, ALU.add))
                    if started(r):
                        dve.wait_ge(s_out[h], r * 16)
                    norm_steps(k, dve, c.link, s, tmp[:, :, :], stat, s_var, s_std, b * (H + 1) + H + 1, y[:, h, :, :])
                    dve.sem_inc(s_y, 1)
                    c.end()

                ahead(dve, stacking, rest)


def build(nc, a, out):
    with ExitStack() as keep:
        k = Program(nc, a, out, keep)
        k.s_act, k.s_pe = k.sem(keep, "s_act"), k.sem(keep, "s_pe")

        def table(name, width):
            return nc.dram_tensor(name, (N, width), F32).ap()
        k.scaled = table("scaled", D)
        k.agg, k.agg3 = table("agg", W), table("agg3", W3)
        hidden, scaled2, x1, x2, x3, er = table("hidden", D), table("scaled2", D), table("x1", D), table("x2", D), table("x3", D), table("er", 1)
        setup(k, keep)
        cheb_edges(k, k.scaled)
        node_pass(k, "cheb1", a["x"], True, [a["L0_gnn_W0_1"], a["L0_gnn_W1_1"]], a["L0_gnn_b1"], [(hidden, D), (scaled2, D)])
        cheb_edges(k, scaled2)
        node_pass(k, "cheb2", hidden, True, [a["L0_gnn_W0_2"], a["L0_gnn_W1_2"]], a["L0_gnn_b2"], [(x1, D)], skip=a["x"])
        filter_edges(k, x1)
        node_pass(k, "filter", None, True, [], None, [(x2, D), (er, 1)], skip=x1)
        with ExitStack() as ctx:
            kept, logits = k.sb(ctx, "kept", [P, T, W]), k.sb(ctx, "logits", [P, T, 1])
            attend_logits(k, kept, logits, x2, er)
            segment_softmax(k, logits, 1)
            attend_sums(k, kept, logits, k.agg, 1, W)
        node_pass(k, "attend", None, True, [a["L2_gnn_W"]], None, [(x3, D)], skip=x2)
        with ExitStack() as ctx:
            kept, logits = k.sb(ctx, "kept", [P, T, F3]), k.sb(ctx, "logits", [P, T, H])
            transformer_logits(k, kept, logits, x3)
            segment_softmax(k, logits, H)
            attend_sums(k, kept, logits, k.agg3, H, F3)
        transformer_nodes(k, x3, k.agg3, out)


_INS = ['x', 'src', 'dst', 'edge_attr_2', 'edge_attr_48', 'edge_attr_64', 'edge_weight',
        'L0_gnn_W0_1', 'L0_gnn_W1_1', 'L0_gnn_b1', 'L0_gnn_W0_2', 'L0_gnn_W1_2', 'L0_gnn_b2',
        'L1_gnn_W1', 'L1_gnn_b1', 'L1_gnn_W2', 'L1_gnn_b2', 'L1_gnn_W3', 'L1_gnn_b3', 'L1_gnn_W4', 'L1_gnn_b4',
        'L2_gnn_W', 'L2_gnn_al', 'L2_gnn_ar',
        'L3_gnn_Wq', 'L3_gnn_bq', 'L3_gnn_Wk', 'L3_gnn_bk', 'L3_gnn_Wv', 'L3_gnn_bv', 'L3_gnn_We',
        'L3_gnn_Wskip', 'L3_gnn_bskip', 'L3_gnn_gamma', 'L3_gnn_beta']


def kernel(**inputs):
    import numpy as _np
    import concourse.bacc as _bacc
    from concourse import mybir as _mybir
    from concourse.bass_utils import run_bass_kernel_spmd as _run

    nc = _bacc.Bacc("TRN2", target_bir_lowering=False, num_devices=1)
    arrays, args = {}, {}
    for name in _INS:
        a = _np.ascontiguousarray(inputs[name])
        arrays[f"in_{name}_dram"] = a
        args[name] = nc.dram_tensor(f"in_{name}_dram", a.shape, _mybir.dt.from_np(a.dtype), kind="ExternalInput").ap()
    out = nc.dram_tensor("out_0_dram", (N, D), _mybir.dt.float32, kind="ExternalOutput").ap()
    build(nc, args, out)
    r = _run(nc, [arrays], core_ids=[0])
    return r.results[0]["out_0_dram"]
```

```python
import concourse.bass as bass
from concourse import mybir
from contextlib import ExitStack, contextmanager

F32 = mybir.dt.float32
I32 = mybir.dt.int32
U32 = mybir.dt.uint32
BF16 = mybir.dt.bfloat16
ALU = mybir.AluOpType
ACT = mybir.ActivationFunctionType
AX = mybir.AxisListType

N = 50000
P = 125
T = N // P
D = 64
W = D + 1
H = 3
F3 = D + 3
W3 = H * F3
R = 48
G = 8
NB = T // G
HALF = G // 2
SKIP = 65000.0
BIG = 1.0e30
EPS = 1e-5


def plain(eng, body, nb=NB, tail=False):
    body(0, 0, 0)
    body(1, 1, 0)
    end = nb // 2 - tail
    with eng.Fori(1, end) as r:
        body(r * 2, 0, r)
        body(r * 2 + 1, 1, r)
    if tail:
        body(nb - 2, 0, end)
        body(nb - 1, 1, end)


def ahead(eng, first, second, nb=NB):
    first(0, 0, 0)
    first(1, 1, 0)
    second(0, 0, 0)
    first(2, 0, 1)
    second(1, 1, 0)
    with eng.Fori(1, nb // 2 - 1) as r:
        first(r * 2 + 1, 1, r)
        second(r * 2, 0, r)
        first(r * 2 + 2, 0, r + 1)
        second(r * 2 + 1, 1, r)
    last = nb // 2 - 1
    first(nb - 1, 1, last)
    second(nb - 2, 0, last)
    second(nb - 1, 1, last)


def stagger(eng, nb, *stages):
    leads = [lead for lead, _ in stages]
    start = 2 - min(leads) + (min(leads) % 2)
    end = start + (nb - max(leads) - start) // 2 * 2

    def step(s, r, i):
        for lead, body in stages:
            if r is not None:
                body(r * 2 + (i + lead), (i + lead) % 2, r + (i + lead) // 2)
            elif 0 <= s + lead < nb:
                body(s + lead, (s + lead) % 2, (s + lead) // 2)
    for s in range(-max(leads), start):
        step(s, None, 0)
    with eng.Fori(start // 2, end // 2) as r:
        step(None, r, 0)
        step(None, r, 1)
    for s in range(end, nb - min(leads)):
        step(s, None, 0)


def begun(b):
    return not (isinstance(b, int) and b == 0)


def started(r):
    return not (isinstance(r, int) and r == 0)


class Chain:

    def __init__(self, eng, sem, per, start=0):
        self.eng, self.sem, self.per, self.start = eng, sem, per, start

    def at(self, b):
        self.base, self.n = b * self.per + self.start, 0

    def link(self, ins):
        self.n += 1
        ins.then_inc(self.sem, 1)
        self.eng.wait_ge(self.sem, self.base + self.n)

    def end(self):
        assert self.n == self.per, (self.n, self.per)


class Program:
    def __init__(self, nc, a, out, keep):
        self.nc, self.a, self.out = nc, a, out
        self.count = 0
        self.raised, self.taken, self.keep = {}, {}, keep

    def sem(self, ctx, name):
        mine = self.raised.setdefault(name, [])
        nth = self.taken.get(name, 0)
        self.taken[name] = nth + 1
        if nth == len(mine):
            mine.append(self.keep.enter_context(self.nc.semaphore(f"{name}{nth}")))
        return mine[nth]

    def pool_dma_sem(self, name):
        self.count += 1
        return self.keep.enter_context(self.nc.semaphore(f"{name}_{self.count}"))

    @contextmanager
    def stage(self):
        with ExitStack() as ctx:
            self.taken = {}
            yield ctx
            with self.nc.Block() as block:
                @block.sync
                def _(sp):
                    for name, n in self.taken.items():
                        for s in self.raised[name][:n]:
                            sp.sem_clear(s)

    def sb(self, ctx, name, shape, dt=F32):
        self.count += 1
        return ctx.enter_context(self.nc.sbuf_tensor(f"{name}_{self.count}", shape, dt))

    def ps(self, ctx, name, shape):
        self.count += 1
        return ctx.enter_context(self.nc.psum_tensor(f"{name}_{self.count}", shape, F32))


def cols(t, b):
    return t[:, bass.ds(b * G, G)]


def rows(dram, b, width):
    return dram.rearrange("(p t) d -> p t d", t=T)[:, bass.ds(b * G, G), 0:width]


def wide(ap, shape):
    return ap.to_broadcast(shape)


def setup(k, keep):
    nc, a, sb, sem = k.nc, k.a, k.sb, k.sem
    k.src = sb(keep, "src", [P, T], I32)
    k.dst = sb(keep, "dst", [P, T], I32)
    k.target = sb(keep, "target", [P, T], I32)
    k.weight = sb(keep, "weight", [P, T])
    k.cont = sb(keep, "cont", [P, T])
    k.pen_prev = sb(keep, "pen_prev", [P, T])
    k.pen_next = sb(keep, "pen_next", [P, T])
    k.pen_first = sb(keep, "pen_first", [P, T])
    k.pen_last = sb(keep, "pen_last", [P, T])
    k.eq = sb(keep, "eq", [P, 4, P])
    k.carry = sb(keep, "carry", [P, P])
    k.fix = sb(keep, "fix", [P, 1], I32)
    k.dinv = sb(keep, "dinv", [P, T])
    k.ident = sb(keep, "ident", [P, P])
    k.ones = sb(keep, "ones", [P, P])
    with k.stage() as ctx:
        nxt = sb(ctx, "nxt", [P, T], I32)
        prv = sb(ctx, "prv", [P, 1], I32)
        dstf = sb(ctx, "dstf", [P, T])
        nxtf = sb(ctx, "nxtf", [P, T])
        srcf = sb(ctx, "srcf", [P, T])
        prvf = sb(ctx, "prvf", [P, 1])
        hi = sb(ctx, "hi", [P, T])
        lo = sb(ctx, "lo", [P, T])
        tmp = sb(ctx, "tmp", [P, T])
        tmpi = sb(ctx, "tmpi", [P, T], I32)
        fixf = sb(ctx, "fixf", [P, 2])
        iota_i = sb(ctx, "iota_i", [P, T], I32)
        iota = sb(ctx, "iota", [P, T])
        part_i = sb(ctx, "part_i", [P, 1], I32)
        part = sb(ctx, "part", [P, 1])
        diag = sb(ctx, "diag", [P, 2, P])
        above = sb(ctx, "above", [P, P])
        ohp = sb(ctx, "ohp", [P, 2, G, P])
        oht = sb(ctx, "oht", [P, 2, G, T])
        zero = sb(ctx, "zero", [P, 2680])
        pos = sb(ctx, "pos", [P, T])
        XB = 40 * D
        xin = sb(ctx, "xin", [P, 2, XB])
        xout = sb(ctx, "xout", [P, 2, XB])
        ends = k.ps(ctx, "ends", [P, 2, 512])
        deg = k.ps(ctx, "deg", [P, T])
        s_pre, s_load, s_iota = sem(ctx, "s_pre"), sem(ctx, "s_load"), sem(ctx, "s_iota")
        s_v, s_diag, s_ends = sem(ctx, "s_v"), sem(ctx, "s_diag"), sem(ctx, "s_ends")
        s_oh, s_hist, s_clamp, s_root = (sem(ctx, n) for n in ("s_oh", "s_hist", "s_clamp", "s_root"))
        s_zero, s_zeroed = sem(ctx, "s_zero"), sem(ctx, "s_zeroed")
        s_x = [sem(ctx, "s_x") for _ in range(2)]
        s_y, s_st = sem(ctx, "s_y"), [sem(ctx, "s_st") for _ in range(2)]
        s_hv = sem(ctx, "s_hv")
        dst_pt = a["dst"].rearrange("(p t) -> p t", t=T)
        XN = T * D // XB
        with nc.Block() as block:

            @block.sync
            def _(sp):
                sp.dma_start(k.dst[:, :], dst_pt).then_inc(s_load, 16)
                sp.dma_start(k.src[:, :], a["src"].rearrange("(p t) -> p t", t=T)).then_inc(s_load, 16)
                sp.dma_start(k.weight[:, :], a["edge_weight"].rearrange("(p t) -> p t", t=T)).then_inc(s_load, 16)
                sp.wait_ge(s_pre, 2)
                sp.dma_start(nxt[0:P - 1, :], a["dst"][1:1 + (P - 1) * T].rearrange("(p t) -> p t", t=T)).then_inc(s_load, 16)
                sp.dma_start(nxt[P - 1:P, 0:T - 1], a["dst"][N - T + 1:N].unsqueeze(0)).then_inc(s_load, 16)
                sp.dma_start(prv[1:P, :], dst_pt[0:P - 1, T - 1:T], allow_slow_non_contiguous=True).then_inc(s_load, 16)
                xv = a["x"].rearrange("(p t) d -> p (t d)", t=T)
                yv = k.scaled.rearrange("(p t) d -> p (t d)", t=T)
                for i in range(XN):
                    if i >= 2:
                        sp.wait_ge(s_y, i - 1)
                    sp.dma_start(xin[:, i % 2, :], xv[:, i * XB:(i + 1) * XB]).then_inc(s_x[i % 2], 16)
                    if i >= 1:
                        sp.wait_ge(s_y, i)
                        sp.dma_start(yv[:, (i - 1) * XB:i * XB], xout[:, (i - 1) % 2, :]).then_inc(s_st[(i - 1) % 2], 16)
                sp.wait_ge(s_y, XN)
                sp.dma_start(yv[:, (XN - 1) * XB:], xout[:, (XN - 1) % 2, :]).then_inc(s_st[(XN - 1) % 2], 16)
                for h in range(2):
                    sp.wait_ge(s_st[h], 16 * XN // 2)

            @block.gpsimd
            def _(pool):
                pool.memset(nxt[:, :], -1).then_inc(s_pre, 1)
                pool.memset(prv[:, :], -1).then_inc(s_pre, 1)
                pool.iota(iota_i[:, :], [[1, T]], base=0, channel_multiplier=0).then_inc(s_iota, 1)
                pool.iota(part_i[:, :], [[0, 1]], base=0, channel_multiplier=1).then_inc(s_iota, 1)

            @block.vector
            def _(dve):
                c = Chain(dve, s_v, 0)
                c.at(0)
                link = c.link
                dve.memset(zero[:, :], 0.0).then_inc(s_zero, 1)
                link(dve.memset(k.ones[:, :], 1.0))
                dve.wait_ge(s_iota, 2)
                link(dve.tensor_copy(iota[:, :], iota_i[:, :]))
                link(dve.tensor_copy(part[:, :], part_i[:, :]))
                link(dve.tensor_scalar(k.ident[:, :], iota[:, 0:P], part[:, 0:1], None, ALU.is_equal))
                link(dve.tensor_scalar(above[:, :], iota[:, 0:P], part[:, 0:1], None, ALU.is_gt))
                dve.wait_ge(s_load, 6 * 16)
                link(dve.tensor_copy(dstf[:, :], k.dst[:, :]))
                link(dve.tensor_copy(srcf[:, :], k.src[:, :]))
                link(dve.tensor_copy(nxtf[:, :], nxt[:, :]))
                link(dve.tensor_copy(prvf[:, :], prv[:, :]))
                for i, t in enumerate((0, T - 1)):
                    link(dve.tensor_scalar(diag[:, i, :], k.ident[:, :], dstf[:, t:t + 1], None, ALU.mult))
                dve.sem_inc(s_diag, 1)
                link(dve.memset(k.cont[:, 0:1], 0.0))
                link(dve.tensor_tensor(k.cont[:, 1:T], dstf[:, 1:T], dstf[:, 0:T - 1], ALU.is_equal))
                link(dve.tensor_scalar(k.pen_prev[:, :], k.cont[:, :], -1.0, BIG, ALU.add, ALU.mult))
                link(dve.memset(k.pen_next[:, T - 1:T], -BIG))
                link(dve.tensor_copy(k.pen_next[:, 0:T - 1], k.pen_prev[:, 1:T]))
                link(dve.tensor_scalar(k.pen_first[:, :], dstf[:, :], dstf[:, 0:1], -BIG, ALU.not_equal, ALU.mult))
                link(dve.tensor_scalar(k.pen_last[:, :], dstf[:, :], dstf[:, T - 1:T], -BIG, ALU.not_equal, ALU.mult))
                link(dve.tensor_tensor(tmp[:, :], dstf[:, :], nxtf[:, :], ALU.not_equal))
                link(dve.scalar_tensor_tensor(tmp[:, :], dstf[:, :], -SKIP, tmp[:, :], ALU.add, ALU.mult))
                link(dve.tensor_scalar(tmp[:, :], tmp[:, :], SKIP, None, ALU.add))
                link(dve.tensor_copy(k.target[:, :], tmp[:, :]))
                link(dve.tensor_tensor(fixf[:, 0:1], prvf[:, :], dstf[:, 0:1], ALU.is_equal))
                link(dve.tensor_tensor(fixf[:, 1:2], nxtf[:, T - 1:T], dstf[:, 0:1], ALU.not_equal))
                link(dve.tensor_tensor(fixf[:, 0:1], fixf[:, 0:1], fixf[:, 1:2], ALU.mult))
                link(dve.scalar_tensor_tensor(fixf[:, 0:1], dstf[:, 0:1], -SKIP, fixf[:, 0:1], ALU.add, ALU.mult))
                link(dve.tensor_scalar(fixf[:, 0:1], fixf[:, 0:1], SKIP, None, ALU.add))
                link(dve.tensor_copy(k.fix[:, :], fixf[:, 0:1]))
                dve.wait_ge(s_ends, 1)
                for i in range(2):
                    for j, t in enumerate((0, T - 1)):
                        link(dve.tensor_scalar(k.eq[:, 2 * i + j, :], ends[:, i, 0:P], dstf[:, t:t + 1], -BIG, ALU.not_equal, ALU.mult))
                link(dve.scalar_tensor_tensor(k.carry[:, :], ends[:, 0, 0:P], dstf[:, T - 1:T], above[:, :], ALU.is_equal, ALU.mult))
                link(dve.tensor_scalar(tmp[:, :], srcf[:, :], 1.0 / T, None, ALU.mult))
                link(dve.tensor_copy(tmpi[:, :], tmp[:, :]))
                link(dve.tensor_copy(hi[:, :], tmpi[:, :]))
                link(dve.scalar_tensor_tensor(lo[:, :], hi[:, :], -float(T), srcf[:, :], ALU.mult, ALU.add))
                link(dve.tensor_scalar(tmp[:, :], lo[:, :], 0.0, None, ALU.is_lt))
                link(dve.tensor_tensor(hi[:, :], hi[:, :], tmp[:, :], ALU.subtract))
                link(dve.scalar_tensor_tensor(lo[:, :], tmp[:, :], float(T), lo[:, :], ALU.mult, ALU.add))
                link(dve.tensor_scalar(tmp[:, :], lo[:, :], float(T), None, ALU.is_ge))
                link(dve.tensor_tensor(hi[:, :], hi[:, :], tmp[:, :], ALU.add))
                link(dve.scalar_tensor_tensor(lo[:, :], tmp[:, :], -float(T), lo[:, :], ALU.mult, ALU.add))

                def one_hots(b, h, r):
                    if started(r):
                        dve.wait_ge(s_hist, b - 1)
                    for u in range(G):
                        t = bass.ds(b * G + u, 1)
                        dve.tensor_scalar(ohp[:, h, u, :], iota[:, 0:P], hi[:, t], k.weight[:, t], ALU.is_equal, ALU.mult).then_inc(s_hv, 1)
                        dve.tensor_scalar(oht[:, h, u, :], iota[:, :], lo[:, t], None, ALU.is_equal).then_inc(s_hv, 1)
                plain(dve, one_hots)
                dve.wait_ge(s_hist, NB)
                link(dve.tensor_scalar(pos[:, :], deg[:, :], 0.0, None, ALU.is_gt))
                dve.tensor_scalar(tmp[:, :], deg[:, :], 1e-12, None, ALU.max).then_inc(s_clamp, 1)
                dve.wait_ge(s_root, 1)
                link(dve.reciprocal(k.dinv[:, :], tmp[:, :]))
                link(dve.tensor_tensor(k.dinv[:, :], k.dinv[:, :], pos[:, :], ALU.mult))
                for i in range(XN):
                    dve.wait_ge(s_x[i % 2], 16 * (i // 2 + 1))
                    if i >= 2:
                        dve.wait_ge(s_st[i % 2], 16 * (i // 2))
                    dve.tensor_tensor(xout[:, i % 2, :].rearrange("p (t d) -> p t d", d=D), xin[:, i % 2, :].rearrange("p (t d) -> p t d", d=D),
                                      wide(k.dinv[:, i * 40:(i + 1) * 40].unsqueeze(2), [P, 40, D]), ALU.mult).then_inc(s_y, 1)

            @block.tensor
            def _(pe):
                pe.wait_ge(s_diag, 1)
                pe.matmul(ends[:, 0, 0:P], k.ones[:, :], diag[:, 0, :], start=True, stop=True)
                pe.matmul(ends[:, 1, 0:P], k.ones[:, :], diag[:, 1, :], start=True, stop=True).then_inc(s_ends, 1)

                def histogram(b, h, r):
                    pe.wait_ge(s_hv, b * 2 * G + 2 * G)
                    for u in range(G):
                        ins = pe.matmul(deg[:, :], ohp[:, h, u, :], oht[:, h, u, :], start=isinstance(b, int) and b == 0 and u == 0,
                                        stop=False, skip_group_check=True)
                    ins.then_inc(s_hist, 1)
                plain(pe, histogram)

            @block.scalar
            def _(act):
                act.wait_ge(s_zero, 1)
                n = 0
                for table, width in ((k.agg, W), (k.agg3, W3)):
                    flat = table.rearrange("(p t) d -> p (t d)", t=T)
                    for i in range(0, T * width, 2680):
                        j = min(i + 2680, T * width)
                        act.dma_start(flat[:, i:j], zero[:, 0:j - i]).then_inc(s_zeroed, 16)
                        n += 1
                act.wait_ge(s_clamp, 1)
                act.activation(tmp[:, :], tmp[:, :], ACT.Sqrt).then_inc(s_root, 1)
                act.wait_ge(s_zeroed, 16 * n)


class Edges:

    def __init__(self, k, ctx, gathers, width):
        self.k, self.width = k, width
        self.gathers = [(index, table, k.sb(ctx, "rows", [P, 2, G, w]), k.sb(ctx, "now", [P, 2, G], I32)) for index, table, w in gathers]
        self.s_rows = [k.pool_dma_sem("s_rows") for _ in range(2)]
        self.s_used = k.sem(ctx, "s_used")
        self.s_index = k.sem(ctx, "s_index")
        self.s_pool = k.sem(ctx, "s_pool")
        self.landed = 16 * G * len(self.gathers)
        if width:
            self.messages = k.sb(ctx, "messages", [P, G, width])
            self.sums = k.sb(ctx, "sums", [P, 2, G, width])
            self.to = k.sb(ctx, "to", [P, 2, G], I32)
            self.mend = k.sb(ctx, "mend", [P, width])
            self.carried = k.ps(ctx, "carried", [P, width])
            self.s_sums = k.sem(ctx, "s_sums")
            self.s_sent = [k.pool_dma_sem("s_sent") for _ in range(2)]
            self.s_to = k.sem(ctx, "s_to")
            self.s_mend0 = k.sem(ctx, "s_mend0")
            self.s_mend = k.sem(ctx, "s_mend")
            self.s_carried = k.sem(ctx, "s_carried")
            self.s_mended = k.pool_dma_sem("s_mended")

    def pool(self, pool, agg):
        k = self.k

        def gather(b, h, r):
            if started(r):
                pool.wait_ge(self.s_used, b - 1)
                pool.sem_inc(self.s_pool, 1)
            for index, _, _, now in self.gathers:
                pool.tensor_copy(now[:, h, :], cols(index, b)).then_inc(self.s_index, 1)
            pool.wait_ge(self.s_index, b * len(self.gathers) + len(self.gathers))
            pool.sem_inc(self.s_pool, 1)
            for index, table, ring, now in self.gathers:
                for u in range(G):
                    pool.indirect_dma_start(ring[:, h, u, :], None, table, bass.IndirectOffsetOnAxis(ap=now[:, h, u:u + 1].bitcast(U32), axis=0)).then_inc(self.s_rows[h], 16)

        def scatter(b, h, r):
            pool.wait_ge(self.s_sums, b + 1)
            pool.sem_inc(self.s_pool, 1)
            pool.tensor_copy(self.to[:, h, :], cols(k.target, b)).then_inc(self.s_to, 1)
            pool.wait_ge(self.s_to, b + 1)
            pool.sem_inc(self.s_pool, 1)
            for u in range(G):
                pool.indirect_dma_start(agg, bass.IndirectOffsetOnAxis(ap=self.to[:, h, u:u + 1].bitcast(U32), axis=0), self.sums[:, h, u, :], None,
                                        bounds_check=N - 1, oob_is_err=False).then_inc(self.s_sent[h], 16)

        if not self.width:
            plain(pool, gather)
            return
        if self.gathers:
            ahead(pool, gather, scatter)
        else:
            plain(pool, scatter)
        fix = bass.IndirectOffsetOnAxis(ap=k.fix[:, :].bitcast(U32), axis=0)
        for h in range(2):
            pool.wait_ge(self.s_sent[h], 16 * G * NB // 2)
        pool.wait_ge(self.s_mend0, 1)
        pool.indirect_dma_start(self.mend[:, :], None, agg, fix, bounds_check=N - 1, oob_is_err=False).then_inc(self.s_mended, 16)
        pool.wait_ge(self.s_mend, 1)
        pool.indirect_dma_start(agg, fix, self.mend[:, :], None, bounds_check=N - 1, oob_is_err=False).then_inc(self.s_mended, 16)
        pool.wait_ge(self.s_mended, 32)

    def tensor_mend(self, pe):
        pe.wait_ge(self.s_sums, NB)
        pe.matmul(self.carried[:, :], self.k.carry[:, :], self.sums[:, 1, G - 1, :], start=True, stop=True).then_inc(self.s_carried, 1)

    def vector_start(self, dve, link):
        link(dve.memset(self.sums[:, 1, G - 1, :], 0.0))
        link(dve.memset(self.messages[:, :, :], 1.0))
        dve.memset(self.mend[:, :], 0.0).then_inc(self.s_mend0, 1)

    def vector_sums(self, dve, link, b, h, r):
        for u in range(G):
            before = self.sums[:, h, u - 1, :] if u else self.sums[:, 1 - h, G - 1, :]
            link(dve.scalar_tensor_tensor(self.sums[:, h, u, :], before, self.k.cont[:, bass.ds(b * G + u, 1)],
                                          self.messages[:, u, :], ALU.mult, ALU.add))
        dve.sem_inc(self.s_sums, 1)

    def vector_sent(self, dve, h, r):
        if started(r):
            dve.wait_ge(self.s_sent[h], r * (16 * G))

    def vector_mend(self, dve):
        dve.wait_ge(self.s_carried, 1)
        dve.wait_ge(self.s_mended, 16)
        dve.tensor_tensor(self.mend[:, :], self.mend[:, :], self.carried[:, :], ALU.add).then_inc(self.s_mend, 1)


def cheb_edges(k, table):
    nc = k.nc
    with k.stage() as ctx:
        e = Edges(k, ctx, [(k.src, table, D)], W)
        s_v = k.sem(ctx, "s_v")
        ring = e.gathers[0][2]
        with nc.Block() as block:

            @block.gpsimd
            def _(pool):
                e.pool(pool, k.agg)

            @block.tensor
            def _(pe):
                e.tensor_mend(pe)

            @block.vector
            def _(dve):
                c = Chain(dve, s_v, 1 + G, start=2)
                c.base, c.n = 0, 0
                e.vector_start(dve, c.link)

                def body(b, h, r):
                    c.at(b)
                    dve.wait_ge(e.s_rows[h], r * e.landed + e.landed)
                    c.link(dve.tensor_tensor(e.messages[:, :, 0:D], ring[:, h, :, :], wide(cols(k.weight, b).unsqueeze(2), [P, G, D]), ALU.mult))
                    dve.sem_inc(e.s_used, 1)
                    e.vector_sent(dve, h, r)
                    e.vector_sums(dve, c.link, b, h, r)
                    c.end()
                plain(dve, body)
                e.vector_mend(dve)


def filter_edges(k, table):
    nc, a, sb, sem, ps = k.nc, k.a, k.sb, k.sem, k.ps
    HC = HALF * P
    with k.stage() as ctx:
        e = Edges(k, ctx, [(k.src, table, D)], W)
        ring = e.gathers[0][2]
        stack = sb(ctx, "stack", [P, 2, G, 2 * D])
        stackT = sb(ctx, "stackT", [2 * D, 2, HC])
        act_in = sb(ctx, "act_in", [D, 2, HC])
        soft = sb(ctx, "soft", [D + 1, 2, HC])
        w1 = sb(ctx, "w1", [R + 1, D])
        w2 = sb(ctx, "w2", [D + 1, D])
        w3 = sb(ctx, "w3", [D, D])
        w3T = sb(ctx, "w3T", [D, D])
        w4 = sb(ctx, "w4", [D, D])
        w34 = sb(ctx, "w34", [D, D])
        w34_low = sb(ctx, "w34_low", [2 * D, D])
        b3 = sb(ctx, "b3", [D, 1])
        b4 = sb(ctx, "b4", [1, D])
        b34 = sb(ctx, "b34", [1, D])
        pT = ps(ctx, "pT", [2 * D, 2, 512])
        pZ = ps(ctx, "pZ", [D, 2, 512])
        pH = ps(ctx, "pH", [P, G * D])
        pE = ps(ctx, "pE", [P, G * D])
        s_v, s_a = sem(ctx, "s_v"), sem(ctx, "s_a")
        s_w, s_w34, s_fold, s_low, s_one = (sem(ctx, n) for n in ("s_w", "s_w34", "s_fold", "s_low", "s_one"))
        s_in = [sem(ctx, "s_in") for _ in range(2)]
        s_T, s_Ts, s_Z, s_zb, s_zc, s_sp, s_soft, s_HE = (sem(ctx, n) for n in ("s_T", "s_Ts", "s_Z", "s_zb", "s_zc", "s_sp", "s_soft", "s_HE"))
        s_msg = sem(ctx, "s_msg")
        zb = sb(ctx, "zb", [D, 2, HC])
        with nc.Block() as block:

            @block.sync
            def _(sp):
                for t, x in ((w1[0:R, :], a["L1_gnn_W1"]), (w1[R:R + 1, :], a["L1_gnn_b1"].unsqueeze(0)), (w2[0:D, :], a["L1_gnn_W2"]),
                             (w2[D:D + 1, :], a["L1_gnn_b2"].unsqueeze(0)), (w3[:, :], a["L1_gnn_W3"]), (w4[:, :], a["L1_gnn_W4"]),
                             (b3[:, :], a["L1_gnn_b3"].unsqueeze(1)), (b4[:, :], a["L1_gnn_b4"].unsqueeze(0))):
                    sp.dma_start(t, x).then_inc(s_w, 16)
                sp.wait_ge(s_fold, 3)
                sp.dma_start(w34_low[D:2 * D, :], w34[:, :]).then_inc(s_low, 16)
                sp.wait_ge(s_one, 2)

                def load(b, h, r):
                    if started(r):
                        sp.wait_ge(s_T, b - 1)
                    sp.dma_start(stack[:, h, :, 0:R], rows(a["edge_attr_48"], b, R)).then_inc(s_in[h], 16)
                    sp.dma_start(stack[:, h, :, D:2 * D], rows(a["edge_attr_64"], b, D)).then_inc(s_in[h], 16)
                plain(sp, load)

            @block.gpsimd
            def _(pool):
                e.pool(pool, k.agg)

            @block.tensor
            def _(pe):
                pe.wait_ge(s_w, 8 * 16)
                pe.transpose(pT[0:D, 0, 0:D], w3[:, :], k.ident[0:D, 0:D]).then_inc(s_w34, 1)
                pe.wait_ge(s_fold, 1)
                pe.matmul(pH[0:D, 0:D], w3T[:, :], w4[:, :], start=True, stop=True)
                pe.matmul(pE[0:1, 0:D], b3[:, :], w4[:, :], start=True, stop=False)
                pe.matmul(pE[0:1, 0:D], k.ones[0:1, 0:1], b4[:, :], start=False, stop=True).then_inc(s_w34, 1)
                pe.wait_ge(s_fold, 3)
                pe.wait_ge(s_low, 16)

                def transposes(b, h, r):
                    pe.wait_ge(s_in[h], r * 32 + 32)
                    if not (isinstance(b, int) and b == 0):
                        pe.wait_ge(s_Ts, b)
                    pe.sem_inc(k.s_pe, 1)
                    for u in range(G):
                        ins = pe.transpose(pT[:, u // HALF, (u % HALF) * P:(u % HALF + 1) * P], stack[:, h, u, :], k.ident[:, :])
                    ins.then_inc(s_T, 1)

                def products(b, h, r):
                    pe.wait_ge(s_Ts, b + 1)
                    pe.sem_inc(k.s_pe, 1)
                    for j in range(2):
                        ins = pe.matmul(pZ[:, j, 0:HC], w1[:, :], stackT[0:R + 1, j, :], start=True, stop=True)
                    ins.then_inc(s_Z, 1)
                    if not (isinstance(b, int) and b == 0):
                        pe.wait_ge(s_msg, b)
                    pe.sem_inc(k.s_pe, 1)
                    for u in range(G):
                        t = (slice(None), u // HALF, slice((u % HALF) * P, (u % HALF + 1) * P))
                        pe.matmul(pE[:, u * D:(u + 1) * D], stackT[D:2 * D, t[1], t[2]], w34_low[D:2 * D, :], start=True, stop=False)
                        pe.matmul(pE[:, u * D:(u + 1) * D], k.ones[0:1, :], b34[:, :], start=False, stop=True)
                    pe.wait_ge(s_soft, b + 1)
                    pe.sem_inc(k.s_pe, 1)
                    for u in range(G):
                        t = (slice(None), u // HALF, slice((u % HALF) * P, (u % HALF + 1) * P))
                        ins = pe.matmul(pH[:, u * D:(u + 1) * D], soft[:, t[1], t[2]], w2[:, :], start=True, stop=True)
                    ins.then_inc(s_HE, 1)

                def both(b, h, r):
                    transposes(b, h, r)
                    products(b, h, r)
                plain(pe, both)
                e.tensor_mend(pe)

            @block.scalar
            def _(act):
                def body(b, h, r):
                    act.wait_ge(s_T, b + 1)
                    if not (isinstance(b, int) and b == 0):
                        act.wait_ge(s_HE, b)
                    act.activation(stackT[:, :, :], pT[:, :, 0:HC], ACT.Copy).then_inc(s_Ts, 1)
                    act.wait_ge(s_Z, b + 1)
                    act.activation(zb[:, :, :], pZ[:, :, 0:HC], ACT.Copy).then_inc(s_zb, 1)
                    act.wait_ge(s_zc, b + 1)
                    act.activation(act_in[:, :, :], act_in[:, :, :], ACT.Exp, scale=0.5).then_inc(s_a, 1)
                    act.wait_ge(s_a, b + 1)
                    act.activation(act_in[:, :, :], act_in[:, :, :], ACT.Ln, bias=1.0).then_inc(s_sp, 1)
                plain(act, body)

            @block.vector
            def _(dve):
                c = Chain(dve, s_v, 2 + G, start=2)
                c.base, c.n = 0, 0
                e.vector_start(dve, c.link)
                dve.memset(stack[:, :, :, R:D], 0.0).then_inc(s_one, 1)
                dve.wait_ge(s_one, 1)
                dve.memset(stack[:, :, :, R:R + 1], 1.0).then_inc(s_one, 1)
                dve.memset(soft[D:D + 1, :, :], 1.0)
                dve.wait_ge(s_w34, 1)
                dve.tensor_copy(w3T[:, :], pT[0:D, 0, 0:D]).then_inc(s_fold, 1)
                dve.wait_ge(s_w34, 2)
                dve.tensor_copy(w34[:, :], pH[0:D, 0:D]).then_inc(s_fold, 1)
                dve.tensor_copy(b34[:, :], pE[0:1, 0:D]).then_inc(s_fold, 1)

                def body(b, h, r):
                    c.at(b)
                    dve.wait_ge(s_zb, b + 1)
                    dve.tensor_scalar(act_in[:, :, :], zb[:, :, :], 28.0, None, ALU.min).then_inc(s_zc, 1)
                    dve.wait_ge(s_sp, b + 1)
                    dve.scalar_tensor_tensor(soft[0:D, :, :], act_in[:, :, :], 2.0, zb[:, :, :], ALU.mult, ALU.max).then_inc(s_soft, 1)
                    dve.wait_ge(s_HE, b + 1)
                    dve.wait_ge(e.s_rows[h], r * e.landed + e.landed)
                    c.link(dve.tensor_tensor(e.messages[:, :, 0:D], ring[:, h, :, :], pH[:, :].rearrange("p (u d) -> p u d", d=D), ALU.mult))
                    dve.sem_inc(e.s_used, 1)
                    c.link(dve.tensor_tensor(e.messages[:, :, 0:D], e.messages[:, :, 0:D], pE[:, :].rearrange("p (u d) -> p u d", d=D), ALU.add))
                    dve.sem_inc(s_msg, 1)
                    e.vector_sent(dve, h, r)
                    e.vector_sums(dve, c.link, b, h, r)
                    c.end()
                plain(dve, body)
                e.vector_mend(dve)


def segment_softmax(k, logits, heads):
    nc, sb, sem = k.nc, k.sb, k.sem
    with k.stage() as ctx:
        top = sb(ctx, "top", [P, T])
        full = sb(ctx, "full", [P, T])
        diag = sb(ctx, "diag", [P, 2, P])
        cand = sb(ctx, "cand", [P, 4, P])
        best = sb(ctx, "best", [P, 4])
        both = sb(ctx, "both", [P, 2])
        ends = k.ps(ctx, "ends", [P, 2, 512])
        s_v, s_diag, s_ends, s_ready, s_exp = (sem(ctx, n) for n in ("s_v", "s_diag", "s_ends", "s_ready", "s_exp"))
        with nc.Block() as block:

            @block.vector
            def _(dve):
                c = Chain(dve, s_v, 0)
                c.at(0)
                link = c.link
                for i in range(heads):
                    one = logits[:, :, i]
                    link(dve.tensor_tensor_scan(top[:, :], k.pen_prev[:, :], one, -BIG, ALU.add, ALU.max))
                    link(dve.tensor_tensor_scan(full[:, ::-1], k.pen_next[:, ::-1], top[:, ::-1], -BIG, ALU.add, ALU.max))
                    for j, t in enumerate((0, T - 1)):
                        link(dve.tensor_scalar(diag[:, j, :], k.ident[:, :], full[:, t:t + 1], None, ALU.mult))
                    dve.sem_inc(s_diag, 1)
                    dve.wait_ge(s_ends, i + 1)
                    for j in range(4):
                        link(dve.tensor_tensor(cand[:, j, :], ends[:, j // 2, 0:P], k.eq[:, j, :], ALU.add))
                    link(dve.tensor_reduce(best[:, :], cand[:, :, :], AX.X, ALU.max))
                    link(dve.tensor_tensor(both[:, :], best[:, 0:2], best[:, 2:4], ALU.max))
                    link(dve.scalar_tensor_tensor(full[:, :], k.pen_first[:, :], both[:, 0:1], full[:, :], ALU.add, ALU.max))
                    link(dve.scalar_tensor_tensor(full[:, :], k.pen_last[:, :], both[:, 1:2], full[:, :], ALU.add, ALU.max))
                    dve.tensor_tensor(one, one, full[:, :], ALU.subtract).then_inc(s_ready, 1)
                    dve.wait_ge(s_ready, i + 1)

            @block.tensor
            def _(pe):
                for i in range(heads):
                    pe.wait_ge(s_diag, i + 1)
                    pe.matmul(ends[:, 0, 0:P], k.ones[:, :], diag[:, 0, :], start=True, stop=True)
                    pe.matmul(ends[:, 1, 0:P], k.ones[:, :], diag[:, 1, :], start=True, stop=True).then_inc(s_ends, 1)

            @block.scalar
            def _(act):
                act.wait_ge(s_ready, heads)
                act.activation(logits[:, :, :], logits[:, :, :], ACT.Exp).then_inc(s_exp, 1)
                act.wait_ge(s_exp, 1)


def attend_logits(k, kept, logits, table, near):
    nc, a, sb, sem = k.nc, k.a, k.sb, k.sem
    with k.stage() as ctx:
        e = Edges(k, ctx, [(k.src, table, D), (k.dst, near, 1)], 0)
        ring, er = e.gathers[0][2], e.gathers[1][2]
        al = sb(ctx, "al", [P, D])
        prod = sb(ctx, "prod", [P, G, D])
        red = sb(ctx, "red", [P, G])
        s_al, s_v, s_kept = sem(ctx, "s_al"), sem(ctx, "s_v"), sem(ctx, "s_kept")
        with nc.Block() as block:

            @block.sync
            def _(sp):
                sp.dma_start(al[:, :], a["L2_gnn_al"].rearrange("d o -> (d o)").partition_broadcast(P)).then_inc(s_al, 16)

            @block.gpsimd
            def _(pool):
                e.pool(pool, None)

            @block.scalar
            def _(act):
                def keep(b, h, r):
                    act.wait_ge(e.s_rows[h], r * e.landed + e.landed)
                    act.sem_inc(k.s_act, 1)
                    act.activation(kept[:, bass.ds(b * G, G), 0:D], ring[:, h, :, :], ACT.Copy).then_inc(s_kept, 1)
                plain(act, keep)

            @block.vector
            def _(dve):
                c = Chain(dve, s_v, 4, start=1)
                c.base, c.n = 0, 0
                c.link(dve.memset(kept[:, :, D:D + 1], 1.0))
                dve.wait_ge(s_al, 16)

                def body(b, h, r):
                    c.at(b)
                    dve.wait_ge(e.s_rows[h], r * e.landed + e.landed)
                    c.link(dve.tensor_tensor(prod[:, :, :], ring[:, h, :, :], wide(al[:, :].unsqueeze(1), [P, G, D]), ALU.mult))
                    c.link(dve.tensor_reduce(red[:, :], prod[:, :, :], AX.X, ALU.add))
                    c.link(dve.tensor_tensor(red[:, :], red[:, :], er[:, h, :, 0], ALU.add))
                    c.link(dve.scalar_tensor_tensor(logits[:, bass.ds(b * G, G), 0], red[:, :], 0.01, red[:, :], ALU.mult, ALU.max))
                    dve.wait_ge(s_kept, b + 1)
                    dve.sem_inc(e.s_used, 1)
                    c.end()
                plain(dve, body)


def attend_sums(k, kept, logits, agg, heads, features):
    nc = k.nc
    with k.stage() as ctx:
        e = Edges(k, ctx, [], heads * features)
        s_v = k.sem(ctx, "s_v")
        with nc.Block() as block:

            @block.gpsimd
            def _(pool):
                e.pool(pool, agg)

            @block.tensor
            def _(pe):
                e.tensor_mend(pe)

            @block.vector
            def _(dve):
                c = Chain(dve, s_v, 1 + G, start=2)
                c.base, c.n = 0, 0
                e.vector_start(dve, c.link)

                def body(b, h, r):
                    c.at(b)
                    if heads == 1:
                        rows_, ex = kept[:, bass.ds(b * G, G), :], wide(logits[:, bass.ds(b * G, G), :], [P, G, features])
                        out = e.messages[:, :, :]
                    else:
                        rows_ = wide(kept[:, bass.ds(b * G, G), :].unsqueeze(2), [P, G, heads, features])
                        ex = wide(logits[:, bass.ds(b * G, G), :].unsqueeze(3), [P, G, heads, features])
                        out = e.messages[:, :, :].rearrange("p u (i f) -> p u i f", i=heads)
                    c.link(dve.tensor_tensor(out, rows_, ex, ALU.mult))
                    e.vector_sent(dve, h, r)
                    e.vector_sums(dve, c.link, b, h, r)
                    c.end()
                plain(dve, body)
                e.vector_mend(dve)


def transformer_logits(k, kept, logits, table):
    nc, a, sb, sem, ps = k.nc, k.a, k.sb, k.sem, k.ps
    HC = HALF * P
    with k.stage() as ctx:
        e = Edges(k, ctx, [(k.src, table, D), (k.dst, table, D)], 0)
        near, far = e.gathers[0][2], e.gathers[1][2]
        farT = sb(ctx, "farT", [D + 1, 2, HC])
        prod = sb(ctx, "prod", [P, 2, H, F3])
        red = sb(ctx, "red", [P, G, H])
        wq = sb(ctx, "wq", [D, H, D + 1])
        wk = sb(ctx, "wk", [D, H, F3])
        fold = sb(ctx, "fold", [D + 1, W3])
        ea = sb(ctx, "ea", [P, T * 2])
        pT = ps(ctx, "pT", [D, 2, 512])
        pU = ps(ctx, "pU", [P, 4, 512])
        s_w, s_fold, s_ea, s_v, s_kept, s_T, s_Ts, s_U, s_dot, s_c = (
            sem(ctx, n) for n in ("s_w", "s_fold", "s_ea", "s_v", "s_kept", "s_T", "s_Ts", "s_U", "s_dot", "s_c"))
        with nc.Block() as block:

            @block.sync
            def _(sp):
                sp.dma_start(ea[:, :], a["edge_attr_2"].rearrange("(p t) f -> p (t f)", t=T)).then_inc(s_ea, 16)
                for i in range(H):
                    sp.dma_start(wq[:, i, 0:D], a["L3_gnn_Wq"][i, :, :]).then_inc(s_w, 16)
                    sp.dma_start(wq[:, i, D:D + 1], a["L3_gnn_bq"][i, :].unsqueeze(1)).then_inc(s_w, 16)
                    sp.dma_start(wk[:, i, 0:D], a["L3_gnn_Wk"][i, :, :]).then_inc(s_w, 16)
                    sp.dma_start(wk[:, i, D:D + 2], a["L3_gnn_We"][i, :, :]).then_inc(s_w, 16)
                    sp.dma_start(wk[:, i, D + 2:D + 3], a["L3_gnn_bk"][i, :].unsqueeze(1)).then_inc(s_w, 16)

            @block.gpsimd
            def _(pool):
                e.pool(pool, None)

            @block.scalar
            def _(act):
                def body(b, h, r):
                    act.wait_ge(e.s_rows[h], r * e.landed + e.landed)
                    act.sem_inc(k.s_act, 1)
                    act.activation(kept[:, bass.ds(b * G, G), 0:D], near[:, h, :, :], ACT.Copy).then_inc(s_kept, 1)
                    act.wait_ge(s_T, b + 1)
                    if not (isinstance(b, int) and b == 0):
                        act.wait_ge(s_U, b)
                    act.activation(farT[0:D, :, :], pT[:, :, 0:HC], ACT.Copy).then_inc(s_Ts, 1)
                plain(act, body)

            @block.tensor
            def _(pe):
                pe.wait_ge(s_w, 16 * 5 * H)
                for i in range(H):
                    ins = pe.matmul(pU[0:D + 1, 0, i * F3:(i + 1) * F3], wq[:, i, :], wk[:, i, :], start=True, stop=True)
                ins.then_inc(s_fold, 1)
                pe.wait_ge(s_c, 4)

                def transposes(b, h, r):
                    pe.wait_ge(e.s_rows[h], r * e.landed + e.landed)
                    if not (isinstance(b, int) and b == 0):
                        pe.wait_ge(s_Ts, b)
                    pe.sem_inc(k.s_pe, 1)
                    for u in range(G):
                        ins = pe.transpose(pT[:, u // HALF, (u % HALF) * P:(u % HALF + 1) * P], far[:, h, u, :], k.ident[:, :])
                    ins.then_inc(s_T, 1)

                def products(b, h, r):
                    pe.wait_ge(s_Ts, b + 1)
                    if not (isinstance(b, int) and b == 0):
                        pe.wait_ge(s_dot, b)
                    pe.sem_inc(k.s_pe, 1)
                    for u in range(G):
                        ins = pe.matmul(pU[:, u // 2, (u % 2) * W3:(u % 2 + 1) * W3], farT[:, u // HALF, (u % HALF) * P:(u % HALF + 1) * P],
                                        fold[:, :], start=True, stop=True)
                    ins.then_inc(s_U, 1)

                def both(b, h, r):
                    transposes(b, h, r)
                    products(b, h, r)
                plain(pe, both)

            @block.vector
            def _(dve):
                dve.memset(kept[:, :, D + 2:D + 3], 1.0).then_inc(s_c, 1)
                dve.memset(farT[D:D + 1, :, :], 1.0).then_inc(s_c, 1)
                dve.wait_ge(s_ea, 16)
                dve.tensor_copy(kept[:, :, D:D + 2], ea[:, :].rearrange("p (t f) -> p t f", f=2)).then_inc(s_c, 1)
                dve.wait_ge(s_fold, 1)
                dve.tensor_copy(fold[:, :], pU[0:D + 1, 0, 0:W3]).then_inc(s_c, 1)
                dve.wait_ge(s_c, 4)
                c = Chain(dve, s_v, 9)

                def body(b, h, r):
                    c.at(b)
                    dve.wait_ge(s_U, b + 1)
                    dve.wait_ge(s_kept, b + 1)
                    for j in range(4):
                        c.link(dve.tensor_tensor(prod[:, :, :, :], pU[:, j, 0:2 * W3].rearrange("p (u i f) -> p u i f", u=2, i=H),
                                                 wide(kept[:, bass.ds(b * G + 2 * j, 2), :].unsqueeze(2), [P, 2, H, F3]), ALU.mult))
                        c.link(dve.tensor_reduce(red[:, 2 * j:2 * j + 2, :], prod[:, :, :, :], AX.X, ALU.add))
                    dve.sem_inc(s_dot, 1)
                    dve.sem_inc(e.s_used, 1)
                    c.link(dve.tensor_scalar(logits[:, bass.ds(b * G, G), :], red[:, :, :], float(D) ** -0.5, None, ALU.mult))
                    c.end()
                plain(dve, body)


S = 100
K = 128
TILES = N // S
U = 5
WB = TILES // U
J = P
SU = S * U


def nodes(dram, b, width=D):
    return dram.rearrange("(j i) d -> i j d", i=S)[:, bass.ds(b * U, U), 0:width]


def windows(k, keep):
    nc, a, sb, sem, ps = k.nc, k.a, k.sb, k.sem, k.ps
    GR = TILES // J
    k.w_src = sb(keep, "w_src", [K, TILES], I32)
    k.w_rel = sb(keep, "w_rel", [K, TILES])
    k.w_weight = sb(keep, "w_weight", [K, TILES])
    k.w_attr = sb(keep, "w_attr", [K, TILES, 2])
    k.w_dinv = sb(keep, "w_dinv", [S, TILES])
    k.iota_s = sb(keep, "iota_s", [K, S])
    k.part = sb(keep, "part", [K, 1])
    k.ident128 = sb(keep, "ident128", [K, K])
    k.ident_b = sb(keep, "ident_b", [S, S], BF16)
    k.ones128 = sb(keep, "ones128", [1, K])
    k.start_row = sb(keep, "start_row", [1, TILES], I32)
    k.fits = sb(keep, "fits", [P, 1], I32)
    with k.stage() as ctx:
        iota_i = sb(ctx, "iota_i", [K, K], I32)
        iota = sb(ctx, "iota", [K, K])
        part_i = sb(ctx, "part_i", [K, 1], I32)
        bound = sb(ctx, "bound", [J, GR])
        where = sb(ctx, "where", [J, GR])
        where_i = sb(ctx, "where_i", [J, GR], I32)
        junk = sb(ctx, "junk", [J, T])
        row_i = sb(ctx, "row_i", [J, GR, T], I32)
        row = sb(ctx, "row", [J, T])
        start = sb(ctx, "start", [J, GR])
        start_i = sb(ctx, "start_i", [J, GR], I32)
        late = sb(ctx, "late", [J, GR])
        good = sb(ctx, "good", [J, GR])
        total = sb(ctx, "total", [J, 1])
        src_i = sb(ctx, "src_i", [J, GR, K], I32)
        dst_i = sb(ctx, "dst_i", [J, GR, K], I32)
        srcf = sb(ctx, "srcf", [J, GR, K])
        dstf = sb(ctx, "dstf", [J, GR, K])
        wgt = sb(ctx, "wgt", [J, GR, K])
        attr = sb(ctx, "attr", [J, GR, K * 2])
        dlast = sb(ctx, "dlast", [P, 1])
        diag = sb(ctx, "diag", [P, P])
        sdiag = sb(ctx, "sdiag", [J, GR, J])
        srow = sb(ctx, "srow", [1, TILES])
        pR = ps(ctx, "pR", [P, 512])
        pT = [ps(ctx, "pT", [K, 512]) for _ in range(2)]
        pS = ps(ctx, "pS", [P, 512])
        names = ("s_iota", "s_v", "s_diag", "s_ends", "s_where", "s_start", "s_conv", "s_t", "s_tc", "s_flag", "s_sum", "s_rel")
        s_iota, s_v, s_diag, s_ends, s_where, s_start, s_conv, s_t, s_tc, s_flag, s_sum, s_rel = (sem(ctx, n) for n in names)
        s_row = k.pool_dma_sem("s_row")
        s_win = k.pool_dma_sem("s_win")
        at = lambda t, g: bass.IndirectOffsetOnAxis(ap=t[:, g:g + 1].bitcast(U32), axis=0)
        with nc.Block() as block:

            @block.gpsimd
            def _(pool):
                pool.iota(iota_i[:, :], [[1, K]], base=0, channel_multiplier=0).then_inc(s_iota, 1)
                pool.iota(part_i[:, :], [[0, 1]], base=0, channel_multiplier=1).then_inc(s_iota, 1)
                pool.wait_ge(s_where, 1)
                for g in range(GR):
                    pool.indirect_dma_start(row_i[:, g, :], None, a["dst"].rearrange("(p t) -> p t", t=T), at(where_i, g)).then_inc(s_row, 16)
                pool.wait_ge(s_start, 1)
                one = lambda t: t.rearrange("(e o) -> e o", o=1)
                for g in range(GR):
                    for out, src in ((src_i, one(a["src"])), (dst_i, one(a["dst"])), (wgt, one(a["edge_weight"])), (attr, a["edge_attr_2"])):
                        pool.indirect_dma_start(out[:, g, :], None, src, at(start_i, g)).then_inc(s_win, 16)

            @block.sync
            def _(sp):
                sp.wait_ge(s_conv, 1)
                sp.dma_start(k.rel_rows.rearrange("(g j) e -> j g e", j=J), dstf[:, :, :]).then_inc(s_rel, 16)
                sp.wait_ge(s_rel, 16)

            @block.tensor
            def _(pe):
                pe.wait_ge(s_diag, 1)
                pe.matmul(pR[:, 0:P], k.ones[:, :], diag[:, :], start=True, stop=True).then_inc(s_ends, 1)
                pe.wait_ge(s_conv, 1)
                n = 0
                for g in range(GR):
                    for t in (srcf[:, g, :], dstf[:, g, :], wgt[:, g, :], attr[:, g, :].rearrange("j (e f) -> j f e", f=2)[:, 0, :],
                              attr[:, g, :].rearrange("j (e f) -> j f e", f=2)[:, 1, :]):
                        if n >= 2:
                            pe.wait_ge(s_tc, n - 1)
                        pe.transpose(pT[n % 2][:, 0:J], t, k.ident[:, :]).then_inc(s_t, 1)
                        n += 1
                for c in range(T // S):
                    pe.wait_ge(s_tc, n - 1)
                    pe.transpose(pT[n % 2][0:S, 0:P], k.dinv[:, c * S:(c + 1) * S], k.ident[:, :]).then_inc(s_t, 1)
                    n += 1
                pe.wait_ge(s_flag, 1)
                pe.matmul(pS[0:1, 0:TILES], k.ones[:, 0:1], sdiag[:, :, :].rearrange("j g q -> j (g q)"), start=True, stop=True)
                pe.matmul(pR[:, 0:1], k.ones[:, :], total[:, :], start=True, stop=True).then_inc(s_sum, 1)

            @block.vector
            def _(dve):
                c = Chain(dve, s_v, 0)
                c.at(0)
                link = c.link
                link(dve.memset(k.ones128[:, :], 1.0))
                dve.wait_ge(s_iota, 2)
                link(dve.tensor_copy(iota[:, :], iota_i[:, :]))
                link(dve.tensor_copy(k.part[:, :], part_i[:, :]))
                link(dve.tensor_copy(k.iota_s[:, :], iota[:, 0:S]))
                link(dve.tensor_scalar(k.ident128[:, :], iota[:, :], k.part[:, 0:1], None, ALU.is_equal))
                link(dve.tensor_copy(k.ident_b[:, :], k.ident128[0:S, 0:S]))
                link(dve.tensor_copy(dlast[:, :], k.dst[:, T - 1:T]))
                dve.tensor_scalar(diag[:, :], k.ident[:, :], dlast[:, 0:1], None, ALU.mult).then_inc(s_diag, 1)
                for g in range(GR):
                    link(dve.tensor_scalar(bound[:, g:g + 1], k.part[0:J, :], float(S), float(S * J * g), ALU.mult, ALU.add))
                dve.wait_ge(s_ends, 1)
                for g in range(GR):
                    link(dve.tensor_scalar(junk[:, 0:P], pR[:, 0:P], bound[:, g:g + 1], 0.0, ALU.is_lt, ALU.add, accum_out=where[:, g:g + 1]))
                link(dve.tensor_scalar(where[:, :], where[:, :], float(P - 1), None, ALU.min))
                dve.tensor_copy(where_i[:, :], where[:, :]).then_inc(s_where, 1)
                dve.wait_ge(s_row, 16 * GR)
                for g in range(GR):
                    link(dve.tensor_copy(row[:, :], row_i[:, g, :]))
                    link(dve.tensor_scalar(junk[:, :], row[:, :], bound[:, g:g + 1], 0.0, ALU.is_lt, ALU.add, accum_out=start[:, g:g + 1]))
                link(dve.scalar_tensor_tensor(start[:, :], where[:, :], float(T), start[:, :], ALU.mult, ALU.add))
                link(dve.tensor_scalar(late[:, :], start[:, :], float(N - K), None, ALU.is_ge))
                link(dve.tensor_scalar(start[:, :], start[:, :], float(N - K), None, ALU.min))
                dve.tensor_copy(start_i[:, :], start[:, :]).then_inc(s_start, 1)
                dve.wait_ge(s_win, 16 * 4 * GR)
                link(dve.tensor_copy(srcf[:, :, :], src_i[:, :, :]))
                link(dve.tensor_copy(dstf[:, :, :], dst_i[:, :, :]))
                link(dve.scalar_tensor_tensor(good[:, :], bound[:, :], float(S), dstf[:, :, K - 1], ALU.add, ALU.is_le))
                link(dve.tensor_tensor(good[:, :], good[:, :], late[:, :], ALU.max))
                link(dve.tensor_reduce(total[:, :], good[:, :], AX.X, ALU.add))
                for g in range(GR):
                    link(dve.tensor_scalar(dstf[:, g, :], dstf[:, g, :], bound[:, g:g + 1], None, ALU.subtract))
                    link(dve.tensor_scalar(sdiag[:, g, :], k.ident[:, :], start[:, g:g + 1], None, ALU.mult))
                dve.sem_inc(s_flag, 1)
                dve.sem_inc(s_conv, 1)
                n = 0
                for g in range(GR):
                    q = slice(g * J, (g + 1) * J)
                    for out in (k.w_src[:, q], k.w_rel[:, q], k.w_weight[:, q], k.w_attr[:, q, 0], k.w_attr[:, q, 1]):
                        dve.wait_ge(s_t, n + 1)
                        dve.tensor_copy(out, pT[n % 2][:, 0:J]).then_inc(s_tc, 1)
                        n += 1
                for c_ in range(T // S):
                    dve.wait_ge(s_t, n + 1)
                    dve.tensor_copy(k.w_dinv[:, c_::T // S], pT[n % 2][0:S, 0:P]).then_inc(s_tc, 1)
                    n += 1
                dve.wait_ge(s_sum, 1)
                link(dve.tensor_copy(k.start_row[:, :], pS[0:1, 0:TILES]))
                link(dve.tensor_scalar(total[:, :], pR[:, 0:1], float(TILES), None, ALU.is_ge))
                link(dve.tensor_copy(k.fits[:, :], total[:, :]))


class Gather:

    def __init__(self, k, ctx, table, width=D):
        self.k, self.table = k, table
        self.rows = k.sb(ctx, "rows", [K, 2, U, width])
        self.now = k.sb(ctx, "now", [K, 2, U], I32)
        self.s_rows = [k.pool_dma_sem("s_rows") for _ in range(2)]
        self.s_index, self.s_pool, self.s_used = k.sem(ctx, "s_index"), k.sem(ctx, "s_pool"), k.sem(ctx, "s_used")

    def pool(self, pool, *others, lead=0):
        def gather(b, h, r):
            if started(r):
                pool.wait_ge(self.s_used, b - 1)
                pool.sem_inc(self.s_pool, 1)
            pool.tensor_copy(self.now[:, h, :], self.k.w_src[:, bass.ds(b * U, U)]).then_inc(self.s_index, 1)
            pool.wait_ge(self.s_index, b + 1)
            pool.sem_inc(self.s_pool, 1)
            for u in range(U):
                pool.indirect_dma_start(self.rows[:, h, u, 0:D], None, self.table,
                                        bass.IndirectOffsetOnAxis(ap=self.now[:, h, u:u + 1].bitcast(U32), axis=0)).then_inc(self.s_rows[h], 16)
        if others:
            stagger(pool, WB, *others, (lead, gather))
        else:
            plain(pool, gather, WB)

    def landed(self, eng, h, r):
        eng.wait_ge(self.s_rows[h], r * (16 * U) + 16 * U)


class Norm:
    def __init__(self, k, ctx, newton=False):
        self.k, self.newton = k, newton
        self.FIRST, self.SECOND = (4, 1) if newton else (3, 2)
        self.stats = k.sb(ctx, "stats", [S, U, 6])
        self.mv = k.sb(ctx, "mv", [S, 2, U, 2])
        self.var = k.sb(ctx, "var", [S, 2, U])
        self.rstd = k.sb(ctx, "rstd", [S, 2, U])
        self.tmp = k.sb(ctx, "tmp", [S, 2, U])
        self.s_var, self.s_std, self.s_tick, self.s_step = (k.sem(ctx, n) for n in ("s_var", "s_std", "s_tick", "s_step"))

    def first(self, dve, link, r, h):
        dve.sem_inc(self.s_tick, 1)
        for u in range(U):
            ins = dve.bn_stats(self.stats[:, u, :], r[:, u, :])
        link(ins)
        dve.sem_inc(self.s_tick, 1)
        for u in range(U):
            ins = dve.bn_aggr(self.mv[:, h, u, :], self.stats[:, u, :])
        link(ins)
        link(dve.tensor_scalar(self.var[:, h, :], self.mv[:, h, :, 1], EPS, None, ALU.add))
        if self.newton:
            link(dve.tensor_scalar(self.rstd[:, h, :].bitcast(I32), self.var[:, h, :].bitcast(I32), -0.5, 1597463007.0, ALU.mult, ALU.add))
        dve.sem_inc(self.s_var, 1)

    def second(self, dve, link, r, h, out, nth):
        dve.wait_ge(self.s_std, nth)
        if not self.newton:
            link(dve.reciprocal(self.rstd[:, h, :], self.rstd[:, h, :]))
        for u in range(U):
            ins = dve.tensor_scalar(out[:, u, :], r[:, u, :], self.mv[:, h, u, 0:1], self.rstd[:, h, u:u + 1], ALU.subtract, ALU.mult)
        link(ins)

    def root(self, act, h, nth):
        act.wait_ge(self.s_var, nth)
        act.activation(self.rstd[:, h, :], self.var[:, h, :], ACT.Sqrt).then_inc(self.s_std, 1)

    def newton_steps(self, pool, h, nth, done):
        y, e, p = self.rstd[:, h, :], self.tmp[:, 0, :], self.tmp[:, 1, :]
        pool.wait_ge(self.s_var, nth)
        steps = (lambda: pool.tensor_tensor(e, y, y, ALU.mult), lambda: pool.tensor_tensor(e, e, self.var[:, h, :], ALU.mult),
                 lambda: pool.tensor_scalar(p, e, 0.375, -1.25, ALU.mult, ALU.add), lambda: pool.tensor_tensor(p, p, e, ALU.mult),
                 lambda: pool.tensor_scalar(p, p, 1.875, None, ALU.add), lambda: pool.tensor_tensor(y, y, p, ALU.mult),
                 lambda: pool.tensor_tensor(e, y, y, ALU.mult), lambda: pool.tensor_tensor(e, e, self.var[:, h, :], ALU.mult),
                 lambda: pool.tensor_scalar(p, e, -0.5, 1.5, ALU.mult, ALU.add), lambda: pool.tensor_tensor(y, y, p, ALU.mult))
        for n, step in enumerate(steps):
            if n in (2, 4, 8):
                pool.sem_inc(self.k.s_pool, 1)
            step().then_inc(self.s_step, 1)
            pool.wait_ge(self.s_step, done * len(steps) + n + 1)
        pool.sem_inc(self.s_std, 1)


def window_cheb(k, xs, table, w0, w1, bias, outs, skip=None):
    nc, a, sb, sem, ps = k.nc, k.a, k.sb, k.sem, k.ps
    with k.stage() as ctx:
        g = Gather(k, ctx, table)
        norm = Norm(k, ctx)
        hot = sb(ctx, "hot", [K, 2, U, S])
        xin = sb(ctx, "xin", [S, 2, U, D])
        left = sb(ctx, "left", [S, 2, U, D])
        xT = sb(ctx, "xT", [D + 1, 2, SU])
        aT = sb(ctx, "aT", [D, 2, SU])
        wx = sb(ctx, "wx", [D + 1, D])
        wa = sb(ctx, "wa", [D, D])
        z = sb(ctx, "z", [S, 2, U, D])
        y = [sb(ctx, "y", [S, 2, U, D]) for o in outs]
        pX = [ps(ctx, "pX", [D, SU]) for _ in range(2)]
        pA = [ps(ctx, "pA", [D, SU]) for _ in range(2)]
        pB = ps(ctx, "pB", [S, U * D])
        pC = ps(ctx, "pC", [S, U * D])
        names = ("s_w", "s_v", "s_xT", "s_xTs", "s_aTs", "s_hot", "s_B", "s_Bused", "s_y", "s_one", "s_v2", "s_leftused")
        s_w, s_v, s_xT, s_xTs, s_aTs, s_hot, s_B, s_Bused, s_y, s_one, s_v2, s_leftused = (sem(ctx, n) for n in names)
        s_in = [sem(ctx, "s_in") for _ in range(2)]
        s_left = [sem(ctx, "s_left") for _ in range(2)]
        s_out = [sem(ctx, "s_out") for _ in range(2)]
        with nc.Block() as block:

            @block.sync
            def _(sp):
                sp.dma_start(wx[0:D, :], w0).then_inc(s_w, 16)
                sp.dma_start(wx[D:D + 1, :], bias.unsqueeze(0)).then_inc(s_w, 16)
                sp.dma_start(wa[:, :], w1).then_inc(s_w, 16)

                def load(b, h, r):
                    if started(r):
                        sp.wait_ge(s_leftused, b - 1)
                    sp.dma_start(left[:, h, :, :], nodes(skip, b)).then_inc(s_left[h], 16)

                def store(b, h, r):
                    sp.wait_ge(s_y, b + 1)
                    for t, o in zip(y, outs):
                        sp.dma_start(nodes(o, b), t[:, h, :, :]).then_inc(s_out[h], 16)
                if skip is None:
                    stagger(sp, WB, (0, store))
                else:
                    stagger(sp, WB, (2, load), (0, store))
                for h in range(2):
                    sp.wait_ge(s_out[h], 16 * len(outs) * WB // 2)

            @block.gpsimd
            def _(pool):
                g.pool(pool)

            @block.tensor
            def _(pe):
                pe.wait_ge(s_w, 48)
                pe.wait_ge(s_one, 1)

                def turn_x(b, h, r):
                    pe.wait_ge(s_in[h], r * 16 + 16)
                    if started(r):
                        pe.wait_ge(s_xTs, b - 1)
                    pe.sem_inc(k.s_pe, 1)
                    for u in range(U):
                        ins = pe.transpose(pX[h][:, u * S:(u + 1) * S], xin[:, h, u, :], k.ident[0:S, 0:S])
                    ins.then_inc(s_xT, 1)

                def gathered(b, h, r):
                    pe.wait_ge(s_hot, b + 1)
                    if started(r):
                        pe.wait_ge(s_aTs, b - 1)
                    g.landed(pe, h, r)
                    pe.sem_inc(k.s_pe, 1)
                    for u in range(U):
                        ins = pe.matmul(pA[h][:, u * S:(u + 1) * S], g.rows[:, h, u, :], hot[:, h, u, :], start=True, stop=True)
                    ins.then_inc(g.s_used, 1)

                def products(b, h, r):
                    pe.wait_ge(s_xTs, b + 1)
                    if begun(b):
                        pe.wait_ge(s_Bused, b)
                    pe.sem_inc(k.s_pe, 1)
                    for u in range(U):
                        pe.matmul(pB[:, u * D:(u + 1) * D], xT[:, h, u * S:(u + 1) * S], wx[:, :], start=True, stop=True)
                    pe.wait_ge(s_aTs, b + 1)
                    pe.sem_inc(k.s_pe, 1)
                    for u in range(U):
                        ins = pe.matmul(pC[:, u * D:(u + 1) * D], aT[:, h, u * S:(u + 1) * S], wa[:, :], start=True, stop=True)
                    ins.then_inc(s_B, 1)
                stagger(pe, WB, (0, gathered), (1, turn_x), (0, products))

            @block.scalar
            def _(act):
                def load(b, h, r):
                    act.dma_start(xin[:, h, :, :], nodes(xs, b)).then_inc(s_in[h], 16)

                def copy_x(b, h, r):
                    act.wait_ge(s_xT, b + 1)
                    if started(r):
                        act.wait_ge(s_B, b - 1)
                    act.activation(xT[0:D, h, :], pX[h][:, :], ACT.Copy).then_inc(s_xTs, 1)

                def copy_agg(b, h, r):
                    act.wait_ge(g.s_used, b + 1)
                    if started(r):
                        act.wait_ge(s_B, b - 1)
                    act.activation(aT[:, h, :], pA[h][:, :], ACT.Copy).then_inc(s_aTs, 1)
                stages = [(0, copy_agg), (1, copy_x), (3, load)]
                if skip is not None:
                    stages.append((-1, lambda b, h, r: norm.root(act, h, b + 1)))
                stagger(act, WB, *stages)

            @block.vector
            def _(dve):
                dve.memset(xT[D:D + 1, :, :], 1.0).then_inc(s_one, 1)
                c = Chain(dve, s_v, 3 if skip is None else 3 + norm.FIRST)
                c2 = Chain(dve, s_v2, norm.SECOND)

                def one_hots(b, h, r):
                    if started(r):
                        dve.wait_ge(g.s_used, b - 1)
                    for u in range(U):
                        t = bass.ds(b * U + u, 1)
                        ins = dve.tensor_scalar(hot[:, h, u, :], k.iota_s[:, :], k.w_rel[:, t], k.w_weight[:, t], ALU.is_equal, ALU.mult)
                    ins.then_inc(s_hot, 1)

                def combine(b, h, r):
                    c.at(b)
                    dinv = wide(k.w_dinv[:, bass.ds(b * U, U)].unsqueeze(2), [S, U, D])
                    view = lambda t: t[:, :].rearrange("i (u d) -> i u d", d=D)
                    dve.wait_ge(s_B, b + 1)
                    c.link(dve.tensor_tensor(z[:, h, :, :], view(pC), dinv, ALU.mult))
                    c.link(dve.tensor_tensor(z[:, h, :, :], view(pB), z[:, h, :, :], ALU.subtract))
                    dve.sem_inc(s_Bused, 1)
                    if skip is None:
                        if started(r):
                            dve.wait_ge(s_out[h], r * (16 * len(outs)))
                        dve.tensor_scalar(y[0][:, h, :, :], z[:, h, :, :], 0.0, None, ALU.max)
                        c.link(dve.scalar_tensor_tensor(y[1][:, h, :, :], z[:, h, :, :], 0.0, dinv, ALU.max, ALU.mult))
                        dve.sem_inc(s_y, 1)
                    else:
                        dve.wait_ge(s_left[h], r * 16 + 16)
                        c.link(dve.tensor_tensor(z[:, h, :, :], z[:, h, :, :], left[:, h, :, :], ALU.add))
                        dve.sem_inc(s_leftused, 1)
                        norm.first(dve, c.link, z[:, h, :, :], h)
                    c.end()

                def finish(b, h, r):
                    c2.at(b)
                    if started(r):
                        dve.wait_ge(s_out[h], r * 16)
                    norm.second(dve, c2.link, z[:, h, :, :], h, y[0][:, h, :, :], b + 1)
                    dve.sem_inc(s_y, 1)
                    c2.end()
                if skip is None:
                    stagger(dve, WB, (1, one_hots), (0, combine))
                else:
                    stagger(dve, WB, (1, one_hots), (0, combine), (-1, finish))


def window_filter(k, x, out):
    nc, a, sb, sem, ps = k.nc, k.a, k.sb, k.sem, k.ps
    B0 = 3
    UK = U * K
    with k.stage() as ctx:
        g = Gather(k, ctx, x)
        norm = Norm(k, ctx, newton=True)
        stack = sb(ctx, "stack", [K, 2, U, 2 * D])
        stackT = sb(ctx, "stackT", [2 * D, 2, UK])
        zb = sb(ctx, "zb", [D, 2, UK])
        act_in = sb(ctx, "act_in", [D, 2, UK])
        soft = sb(ctx, "soft", [D + 1, 2, UK])
        hot = sb(ctx, "hot", [K, 2, U, S])
        messages = sb(ctx, "messages", [K, 2, U, D])
        left = sb(ctx, "left", [S, 2, U, D])
        z = sb(ctx, "z", [S, 2, U, D])
        y = sb(ctx, "y", [S, 2, U, D])
        w1 = sb(ctx, "w1", [R + 1, D])
        w2 = sb(ctx, "w2", [D + 1, D])
        w3 = sb(ctx, "w3", [D, D])
        w3T = sb(ctx, "w3T", [D, D])
        w4 = sb(ctx, "w4", [D, D])
        w34 = sb(ctx, "w34", [D, D])
        we = sb(ctx, "we", [2 * D, D])
        b3 = sb(ctx, "b3", [D, 1])
        b4 = sb(ctx, "b4", [1, D])
        b34 = sb(ctx, "b34", [1, D])
        pT = ps(ctx, "pT", [2 * D, 2, 512])
        pZ = ps(ctx, "pZ", [D, 2, 512])
        pH = ps(ctx, "pH", [K, 512])
        pE = [ps(ctx, "pE", [K, 512]) for _ in range(2)]
        pG = ps(ctx, "pG", [S, 512])
        names = ("s_w", "s_w34", "s_fold", "s_low", "s_one", "s_v", "s_a", "s_T", "s_Ts", "s_Z", "s_Zs", "s_E", "s_H", "s_G", "s_min", "s_sp",
                 "s_soft", "s_msg", "s_hot", "s_Gused", "s_y", "s_v2", "s_v3")
        (s_w, s_w34, s_fold, s_low, s_one, s_v, s_a, s_T, s_Ts, s_Z, s_Zs, s_E, s_H, s_G, s_min, s_sp,
         s_soft, s_msg, s_hot, s_Gused, s_y, s_v2, s_v3) = (sem(ctx, n) for n in names)
        s_in, s_left, s_out = ([sem(ctx, n) for _ in range(2)] for n in ("s_in", "s_left", "s_out"))
        banks = ((0, slice(0, B0 * K), slice(0, B0 * K)), (1, slice(0, (U - B0) * K), slice(B0 * K, UK)))
        view = lambda t: t[:, 0:U * D].rearrange("e (u d) -> e u d", d=D)
        with nc.Block() as block:

            @block.sync
            def _(sp):
                for t, w in ((w1[0:R, :], a["L1_gnn_W1"]), (w1[R:R + 1, :], a["L1_gnn_b1"].unsqueeze(0)), (w2[0:D, :], a["L1_gnn_W2"]),
                             (w2[D:D + 1, :], a["L1_gnn_b2"].unsqueeze(0)), (w3[:, :], a["L1_gnn_W3"]), (w4[:, :], a["L1_gnn_W4"]),
                             (b3[:, :], a["L1_gnn_b3"].unsqueeze(1)), (b4[:, :], a["L1_gnn_b4"].unsqueeze(0))):
                    sp.dma_start(t, w).then_inc(s_w, 16)
                sp.wait_ge(s_fold, 3)
                sp.wait_ge(s_one, 4)
                sp.dma_start(we[D:2 * D, :], w34[:, :]).then_inc(s_low, 16)
                sp.dma_start(we[R:R + 1, :], b34[:, :]).then_inc(s_low, 16)

                def load(b, h, r):
                    if started(r):
                        sp.wait_ge(s_T, b - 1)
                    starts = [sp.value_load(k.start_row[0:1, bass.ds(b * U + u, 1)], min_val=0, max_val=N - K) for u in range(U)]
                    for u, start in enumerate(starts):
                        sp.dma_start(stack[:, h, u, 0:R], a["edge_attr_48"][bass.ds(start, K), :]).then_inc(s_in[h], 16)
                        sp.dma_start(stack[:, h, u, D:2 * D], a["edge_attr_64"][bass.ds(start, K), :]).then_inc(s_in[h], 16)

                def load_left(b, h, r):
                    if started(r):
                        sp.wait_ge(s_Gused, b - 1)
                    sp.dma_start(left[:, h, :, :], nodes(x, b)).then_inc(s_left[h], 16)

                def store(b, h, r):
                    sp.wait_ge(s_y, b + 1)
                    sp.dma_start(nodes(out, b), y[:, h, :, :]).then_inc(s_out[h], 16)
                stagger(sp, WB, (0, load_left), (3, load), (-2, store))
                for h in range(2):
                    sp.wait_ge(s_out[h], 16 * WB // 2)

            @block.gpsimd
            def _(pool):
                g.pool(pool, (-2, lambda b, h, r: norm.newton_steps(pool, h, b + 1, b)), lead=1)

            @block.tensor
            def _(pe):
                pe.wait_ge(s_w, 8 * 16)
                pe.transpose(pT[0:D, 0, 0:D], w3[:, :], k.ident[0:D, 0:D]).then_inc(s_w34, 1)
                pe.wait_ge(s_fold, 1)
                pe.matmul(pH[0:D, 0:D], w3T[:, :], w4[:, :], start=True, stop=True)
                pe.matmul(pG[0:1, 0:D], b3[:, :], w4[:, :], start=True, stop=False)
                pe.matmul(pG[0:1, 0:D], k.ones[0:1, 0:1], b4[:, :], start=False, stop=True).then_inc(s_w34, 1)
                pe.wait_ge(s_fold, 3)
                pe.wait_ge(s_low, 32)

                def turn(b, h, r):
                    pe.wait_ge(s_in[h], r * (32 * U) + 32 * U)
                    if begun(b):
                        pe.wait_ge(s_Ts, b)
                    pe.sem_inc(k.s_pe, 1)
                    for u in range(U):
                        ins = pe.transpose(pT[:, u // B0, (u % B0) * K:(u % B0 + 1) * K], stack[:, h, u, :], k.ident128[:, :])
                    ins.then_inc(s_T, 1)

                def radial(b, h, r):
                    pe.wait_ge(s_Ts, b + 1)
                    if begun(b):
                        pe.wait_ge(s_Zs, b)
                    pe.sem_inc(k.s_pe, 1)
                    for i, c, t in banks:
                        ins = pe.matmul(pZ[:, i, c], w1[:, :], stackT[0:R + 1, h, t], start=True, stop=True)
                    ins.then_inc(s_Z, 1)

                def features(b, h, r):
                    if started(r):
                        pe.wait_ge(s_msg, b - 1)
                    pe.sem_inc(k.s_pe, 1)
                    for u in range(U):
                        ins = pe.matmul(pE[h][:, u * D:(u + 1) * D], stackT[:, h, u * K:(u + 1) * K], we[:, :], start=True, stop=True)
                    ins.then_inc(s_E, 1)

                def filters(b, h, r):
                    pe.wait_ge(s_soft, b + 1)
                    if begun(b):
                        pe.wait_ge(s_msg, b)
                    pe.sem_inc(k.s_pe, 1)
                    for u in range(U):
                        ins = pe.matmul(pH[:, u * D:(u + 1) * D], soft[:, h, u * K:(u + 1) * K], w2[:, :], start=True, stop=True)
                    ins.then_inc(s_H, 1)

                def sums(b, h, r):
                    pe.wait_ge(s_msg, b + 1)
                    pe.wait_ge(s_hot, b + 1)
                    if begun(b):
                        pe.wait_ge(s_Gused, b)
                    pe.sem_inc(k.s_pe, 1)
                    for u in range(U):
                        ins = pe.matmul(pG[:, u * D:(u + 1) * D], hot[:, h, u, :], messages[:, h, u, :], start=True, stop=True)
                    ins.then_inc(s_G, 1)
                stagger(pe, WB, (0, filters), (2, turn), (-1, sums), (2, radial), (2, features))

            @block.scalar
            def _(act):
                def copy_stack(b, h, r):
                    act.wait_ge(s_T, b + 1)
                    if started(r):
                        act.wait_ge(s_E, b - 1)
                    for i, c, t in banks:
                        ins = act.activation(stackT[:, h, t], pT[:, i, c], ACT.Copy)
                    ins.then_inc(s_Ts, 1)

                def exp_ln(b, h, r):
                    act.wait_ge(s_min, b + 1)
                    act.activation(act_in[:, h, :], act_in[:, h, :], ACT.Exp, scale=0.5).then_inc(s_a, 1)
                    act.wait_ge(s_a, b + 1)
                    act.activation(act_in[:, h, :], act_in[:, h, :], ACT.Ln, bias=1.0).then_inc(s_sp, 1)

                def copy_radial(b, h, r):
                    act.wait_ge(s_Z, b + 1)
                    if started(r):
                        act.wait_ge(s_soft, b - 1)
                    for i, c, t in banks:
                        ins = act.activation(zb[:, h, t], pZ[:, i, c], ACT.Copy)
                    ins.then_inc(s_Zs, 1)
                stagger(act, WB, (2, copy_stack), (1, exp_ln), (2, copy_radial))

            @block.vector
            def _(dve):
                dve.memset(stack[:, :, :, R:D], 0.0).then_inc(s_one, 1)
                dve.wait_ge(s_one, 1)
                dve.memset(stack[:, :, :, R:R + 1], 1.0).then_inc(s_one, 1)
                dve.memset(we[:, :], 0.0).then_inc(s_one, 1)
                dve.memset(soft[D:D + 1, :, :], 1.0).then_inc(s_one, 1)
                dve.wait_ge(s_w34, 1)
                dve.tensor_copy(w3T[:, :], pT[0:D, 0, 0:D]).then_inc(s_fold, 1)
                dve.wait_ge(s_w34, 2)
                dve.tensor_copy(w34[:, :], pH[0:D, 0:D]).then_inc(s_fold, 1)
                dve.tensor_copy(b34[:, :], pG[0:1, 0:D]).then_inc(s_fold, 1)
                c = Chain(dve, s_v, 2)
                c2 = Chain(dve, s_v2, 1 + norm.FIRST)
                c3 = Chain(dve, s_v3, norm.SECOND)

                def message(b, h, r):
                    c.at(b)
                    dve.wait_ge(s_H, b + 1)
                    dve.wait_ge(s_E, b + 1)
                    if started(r):
                        dve.wait_ge(s_G, b - 1)
                    g.landed(dve, h, r)
                    m = messages[:, h, :, :]
                    c.link(dve.tensor_tensor(m, g.rows[:, h, :, :], view(pH), ALU.mult))
                    dve.sem_inc(g.s_used, 1)
                    c.link(dve.tensor_tensor(m, m, view(pE[h]), ALU.add))
                    dve.sem_inc(s_msg, 1)
                    c.end()

                def softplus(b, h, r):
                    dve.wait_ge(s_sp, b + 1)
                    if started(r):
                        dve.wait_ge(s_H, b - 1)
                    dve.scalar_tensor_tensor(soft[0:D, h, :], act_in[:, h, :], 2.0, zb[:, h, :], ALU.mult, ALU.max).then_inc(s_soft, 1)

                def minimum(b, h, r):
                    dve.wait_ge(s_Zs, b + 1)
                    dve.tensor_scalar(act_in[:, h, :], zb[:, h, :], 28.0, None, ALU.min).then_inc(s_min, 1)

                def one_hots(b, h, r):
                    if started(r):
                        dve.wait_ge(s_G, b - 1)
                    for u in range(U):
                        ins = dve.tensor_scalar(hot[:, h, u, :], k.iota_s[:, :], k.w_rel[:, bass.ds(b * U + u, 1)], None, ALU.is_equal)
                    ins.then_inc(s_hot, 1)

                def combine(b, h, r):
                    c2.at(b)
                    dve.wait_ge(s_G, b + 1)
                    dve.wait_ge(s_left[h], r * 16 + 16)
                    c2.link(dve.tensor_tensor(z[:, h, :, :], view(pG), left[:, h, :, :], ALU.add))
                    dve.sem_inc(s_Gused, 1)
                    norm.first(dve, c2.link, z[:, h, :, :], h)
                    c2.end()

                def finish(b, h, r):
                    c3.at(b)
                    if started(r):
                        dve.wait_ge(s_out[h], r * 16)
                    norm.second(dve, c3.link, z[:, h, :, :], h, y[:, h, :, :], b + 1)
                    dve.sem_inc(s_y, 1)
                    c3.end()
                stagger(dve, WB, (0, one_hots), (0, message), (1, softplus), (-1, combine), (2, minimum), (-2, finish))


def window_attend(k, heads, x, out):
    nc, a, sb, sem, ps = k.nc, k.a, k.sb, k.sem, k.ps
    one = heads == 1
    F = D + 1 if one else F3
    HD = heads * D
    NORMS = 1 if one else heads + 1
    scale = 1.0 if one else float(D) ** -0.5
    B0 = 3
    with k.stage() as ctx:
        g = Gather(k, ctx, x, F)
        norm = Norm(k, ctx, newton=True)
        xin = sb(ctx, "xin", [S, 2, U, D])
        left = sb(ctx, "left", [S, 2, U, D])
        rel = sb(ctx, "rel", [S, 2, U * K])
        pen = sb(ctx, "pen", [S, 2, U, K], BF16)
        rowsT = sb(ctx, "rowsT", [F, 2, U, K])
        xT = sb(ctx, "xT", [D + 1, 2, SU])
        uT = sb(ctx, "uT", [F, 2, heads, SU])
        fold = sb(ctx, "fold", [D + 1, heads * F])
        wv = sb(ctx, "wv", [F, HD])
        ex = sb(ctx, "ex", [S, 2, heads, K])
        low = sb(ctx, "low", [S, 2, K])
        exT = sb(ctx, "exT", [K, 2, heads * S])
        value = sb(ctx, "value", [K, U, HD])
        top = sb(ctx, "top", [S, 2, heads])
        den = sb(ctx, "den", [S, 2, U, heads])
        o = sb(ctx, "o", [S, 2, U, HD])
        s_ = sb(ctx, "s", [S, U, D])
        y = sb(ctx, "y", [S, 2, U, D])
        pR = ps(ctx, "pR", [F, 2, 512])
        pX = ps(ctx, "pX", [F, 512])
        pU = ps(ctx, "pU", [D + 3, 512])
        pS = [ps(ctx, "pS", [S, 512]) for _ in range(2)]
        pA = ps(ctx, "pA", [K, 512])
        pO = ps(ctx, "pO", [S, 512])
        names = ("s_w", "s_fold", "s_c", "s_v", "s_pen", "s_xT", "s_xTs", "s_U", "s_Us", "s_R", "s_Rs", "s_S", "s_low", "s_m", "s_E", "s_P", "s_Ps",
                 "s_V", "s_Vs", "s_O", "s_Oused", "s_y", "s_attr", "s_leftused", "s_part", "s_chain", "s_clear", "s_co")
        (s_w, s_fold, s_c, s_v, s_pen, s_xT, s_xTs, s_U, s_Us, s_R, s_Rs, s_S, s_low, s_m, s_E, s_P, s_Ps,
         s_V, s_Vs, s_O, s_Oused, s_y, s_attr, s_leftused, s_part, s_chain, s_clear, s_co) = (sem(ctx, n) for n in names)
        s_in, s_left, s_rel, s_out = ([sem(ctx, n) for _ in range(2)] for n in ("s_in", "s_left", "s_rel", "s_out"))
        if one:
            loads = [(fold[0:D, D:D + 1], a["L2_gnn_ar"]), (fold[D:D + 1, 0:D], a["L2_gnn_al"].rearrange("d o -> o d")), (wv[0:D, :], a["L2_gnn_W"])]
        else:
            wq = sb(ctx, "wq", [D, H, D + 1])
            wk = sb(ctx, "wk", [D, H, F3])
            nat = sb(ctx, "nat", [D, H, F3 + W])
            ws = sb(ctx, "ws", [W, HD])
            late = sb(ctx, "late", [W, H - 1, D])
            gamma = sb(ctx, "gamma", [S, H, D])
            beta = sb(ctx, "beta", [S, D])
            loads = [(late[D:W, i, :], a["L3_gnn_beta"][i, :].unsqueeze(0)) for i in range(H - 1)]
            loads.append((beta[:, :], a["L3_gnn_beta"][H - 1, :].partition_broadcast(S)))
            for i in range(H):
                loads += [(wq[:, i, 0:D], a["L3_gnn_Wq"][i, :, :]), (wq[:, i, D:D + 1], a["L3_gnn_bq"][i, :].unsqueeze(1)),
                          (wk[:, i, 0:D], a["L3_gnn_Wk"][i, :, :]), (wk[:, i, D:D + 2], a["L3_gnn_We"][i, :, :]),
                          (wk[:, i, D + 2:F3], a["L3_gnn_bk"][i, :].unsqueeze(1)),
                          (nat[:, i, 0:D], a["L3_gnn_Wv"][i, :, :]), (nat[:, i, D:D + 2], a["L3_gnn_We"][i, :, :]),
                          (nat[:, i, D + 2:F3], a["L3_gnn_bv"][i, :].unsqueeze(1)),
                          (nat[:, i, F3:F3 + D], a["L3_gnn_Wskip"][i, :, :]), (nat[:, i, F3 + D:F3 + W], a["L3_gnn_bskip"][i, :].unsqueeze(1)),
                          (gamma[:, i, :], a["L3_gnn_gamma"][i, :].partition_broadcast(S))]
        FIRST_SLOT = 2
        end_lead = -1 - (FIRST_SLOT + NORMS) // U

        def tile(lead, u, body):
            return lead + u // U, lambda b, h, r: body(b, h, u % U)
        with nc.Block() as block:

            @block.sync
            def _(sp):
                if one:
                    sp.wait_ge(s_clear, 1)
                for t, w in loads:
                    sp.dma_start(t, w).then_inc(s_w, 16)
                relv = k.rel_rows.rearrange("(b u) e -> b (u e)", u=U)

                def load_x(b, h, r):
                    if started(r):
                        sp.wait_ge(s_xT, b - 1)
                    sp.dma_start(xin[:, h, :, :], nodes(x, b)).then_inc(s_in[h], 16)

                def load_rel(b, h, r):
                    if started(r):
                        sp.wait_ge(s_pen, b - 1)
                    sp.dma_start(rel[:, h, :], relv[bass.ds(b, 1), :].to_broadcast([S, U * K])).then_inc(s_rel[h], 16)

                def load_left(b, h, r):
                    if started(r):
                        sp.wait_ge(s_leftused, b - 1)
                    sp.dma_start(left[:, h, :, :], nodes(x, b)).then_inc(s_left[h], 16)

                def store(b, h, r):
                    sp.wait_ge(s_y, b + 1)
                    sp.dma_start(nodes(out, b), y[:, h, :, :]).then_inc(s_out[h], 16)
                stagger(sp, WB, (2, load_rel), (0 if one else -1, load_left), (3, load_x), (end_lead, store))
                for h in range(2):
                    sp.wait_ge(s_out[h], 16 * WB // 2)

            @block.gpsimd
            def _(pool):
                steps = []
                for u in range(U):
                    for j in range(NORMS):
                        if (FIRST_SLOT + j) % U == u:
                            steps.append((-1 - (FIRST_SLOT + j) // U, lambda b, h, r, j=j: norm.newton_steps(pool, 0, b * NORMS + j + 1, b * NORMS + j)))
                g.pool(pool, *steps, lead=2)

            @block.tensor
            def _(pe):
                pe.wait_ge(s_w, 16 * len(loads))
                if not one:
                    for i in range(H):
                        pe.matmul(pU[0:D + 1, i * F3:(i + 1) * F3], wq[:, i, :], wk[:, i, :], start=True, stop=True)
                        pe.transpose(pA[0:F3, i * D:(i + 1) * D], nat[:, i, 0:F3], k.ident[0:D, 0:D])
                        ins = pe.transpose(pO[0:W, i * D:(i + 1) * D], nat[:, i, F3:F3 + W], k.ident[0:D, 0:D])
                    ins.then_inc(s_fold, 1)
                pe.wait_ge(s_c, 2 if one else 4)

                def turn_x(b, h, r):
                    pe.wait_ge(s_in[h], r * 16 + 16)
                    if begun(b):
                        pe.wait_ge(s_Us, b * heads)
                    pe.sem_inc(k.s_pe, 1)
                    for u in range(U):
                        ins = pe.transpose(pX[0:D, u * S:(u + 1) * S], xin[:, h, u, :], k.ident[0:S, 0:S])
                    ins.then_inc(s_xT, 1)

                def folds(b, h, i):
                    pe.wait_ge(s_xTs, b + 1)
                    if i >= 2:
                        pe.wait_ge(s_Us, b * heads + i - 1)
                    pe.sem_inc(k.s_pe, 1)
                    pe.matmul((pU, pX)[i % 2][0:F, 0:SU], fold[:, i * F:(i + 1) * F], xT[:, h, :], start=True, stop=True).then_inc(s_U, 1)

                def turn_rows(b, h, r):
                    g.landed(pe, h, r)
                    if not one:
                        pe.wait_ge(s_attr, b + 1)
                    if begun(b):
                        pe.wait_ge(s_Rs, b)
                    pe.sem_inc(k.s_pe, 1)
                    for u in range(U):
                        ins = pe.transpose(pR[:, u // B0, (u % B0) * K:(u % B0 + 1) * K], g.rows[:, h, u, :], k.ident128[:, :])
                    ins.then_inc(s_R, 1)
                    pe.sem_inc(k.s_pe, 1)

                def scores(b, h, u):
                    n, q = b * U + u, (h + u) % 2
                    if not (isinstance(b, int) and b * U + u < 2):
                        pe.wait_ge(s_E, n - 1)
                    if u == 0:
                        pe.wait_ge(s_Us, b * heads + heads)
                        pe.wait_ge(s_Rs, b + 1)
                        pe.wait_ge(s_pen, b + 1)
                    pe.sem_inc(k.s_pe, 1)
                    for i in range(heads):
                        pe.matmul(pS[q][:, i * K:(i + 1) * K], uT[:, h, i, u * S:(u + 1) * S], rowsT[:, h, u, :], start=True, stop=False, skip_group_check=True)
                        ins = pe.matmul(pS[q][:, i * K:(i + 1) * K], k.ident_b[:, :], pen[:, h, u, :], start=False, stop=True, skip_group_check=True)
                    ins.then_inc(s_S, 1)
                    if not (isinstance(b, int) and b * U + u < 2):
                        pe.wait_ge(s_Ps, n - 1)
                    elif u == 1:
                        pe.wait_ge(s_Vs, n)
                    pe.sem_inc(k.s_pe, 1)
                    pe.matmul(pA[:, 0:HD], rowsT[:, h, u, :], wv[:, :], start=True, stop=True).then_inc(s_V, 1)

                def turn_ex(b, h, u):
                    n, q = b * U + u, (h + u) % 2
                    pe.wait_ge(s_E, n + 1)
                    if not (isinstance(b, int) and b * U + u == TILES - 1):
                        pe.wait_ge(s_Vs, n + 2)
                    pe.sem_inc(k.s_pe, 1)
                    for i in range(heads):
                        ins = pe.transpose(pA[:, HD + i * S:HD + (i + 1) * S], ex[:, q, i, :], k.ident[0:S, 0:S])
                    ins.then_inc(s_P, 1)

                def sums(b, h, u):
                    n, q = b * U + u, (h + u) % 2
                    pe.wait_ge(s_Ps, n + 1)
                    pe.wait_ge(s_Vs, n + 1)
                    if not (isinstance(b, int) and b == 0 and u == 0):
                        pe.wait_ge(s_Oused, n)
                    pe.sem_inc(k.s_pe, 1)
                    for i in range(heads):
                        ins = pe.matmul(pO[0:S, i * D:(i + 1) * D], exT[:, q, i * S:(i + 1) * S], value[:, u, i * D:(i + 1) * D], start=True, stop=True)
                    if not one:
                        ins = pe.matmul(pO[0:S, HD:2 * HD], xT[:, h, u * S:(u + 1) * S], ws[:, :], start=True, stop=True)
                    ins.then_inc(s_O, 1)

                stages = []
                for u in range(U):
                    stages += [tile(0, u, scores), tile(0, u - 2, sums), tile(0, u - 1, turn_ex)]
                    if u == 1:
                        stages.append((1, turn_x))
                    elif u == 2:
                        stages += [(1, lambda b, h, r, i=i: folds(b, h, i)) for i in range(min(heads, 2))]
                    elif u == 3:
                        stages += [(1, lambda b, h, r, i=i: folds(b, h, i)) for i in range(2, heads)] + [(1, turn_rows)]
                stagger(pe, WB, *stages)

            @block.scalar
            def _(act):
                if not one:
                    act.wait_ge(s_fold, 1)
                    act.activation(fold[:, :], pU[0:D + 1, 0:W3], ACT.Copy)
                    act.activation(wv[:, :], pA[0:F3, 0:HD], ACT.Copy).then_inc(s_c, 1)

                def copy_x(b, h, r):
                    act.wait_ge(s_xT, b + 1)
                    if started(r):
                        act.wait_ge(s_O, (b - 1) * U)
                    act.activation(xT[0:D, h, :], pX[0:D, 0:SU], ACT.Copy).then_inc(s_xTs, 1)

                def copy_fold(b, h, i):
                    act.wait_ge(s_U, b * heads + i + 1)
                    act.activation(uT[:, h, i, :], (pU, pX)[i % 2][0:F, 0:SU], ACT.Copy).then_inc(s_Us, 1)

                def copy_rows(b, h, r):
                    act.wait_ge(s_R, b + 1)
                    act.activation(rowsT[:, h, 0:B0, :], pR[:, 0, 0:B0 * K].rearrange("f (u e) -> f u e", e=K), ACT.Copy)
                    act.activation(rowsT[:, h, B0:U, :], pR[:, 1, 0:(U - B0) * K].rearrange("f (u e) -> f u e", e=K), ACT.Copy).then_inc(s_Rs, 1)
                    act.sem_inc(g.s_used, 1)

                def values(b, h, u):
                    n, q = b * U + u, (h + u) % 2
                    act.wait_ge(s_V, n + 1)
                    if begun(b):
                        act.wait_ge(s_O, n - U + 1)
                    act.activation(value[:, u, :], pA[:, 0:HD], ACT.Copy).then_inc(s_Vs, 1)

                def exps(b, h, u):
                    n, q = b * U + u, (h + u) % 2
                    act.wait_ge(s_m, n + 1)
                    for i in range(heads):
                        src = ex[:, q, i, :] if one else pS[q][:, i * K:(i + 1) * K]
                        ins = act.activation(ex[:, q, i, :], src, ACT.Exp, bias=top[:, q, i:i + 1], scale=scale, accum_out=den[:, h, u, i:i + 1])
                    ins.then_inc(s_E, 1)

                def copy_ex(b, h, u):
                    n, q = b * U + u, (h + u) % 2
                    act.wait_ge(s_P, n + 1)
                    if not (isinstance(b, int) and b * U + u < 2):
                        act.wait_ge(s_O, n - 1)
                    act.activation(exT[:, q, :], pA[:, HD:HD + heads * S], ACT.Copy).then_inc(s_Ps, 1)

                stages = []
                for u in range(U):
                    stages.append(tile(0, u, values))
                    stages += [tile(0, u, exps), tile(0, u - 1, copy_ex)]
                    if u == 1:
                        stages.append((1, copy_x))
                    elif u == 2:
                        stages += [(1, lambda b, h, r, i=i: copy_fold(b, h, i)) for i in range(min(heads, 2))]
                    elif u == 3:
                        stages += [(1, lambda b, h, r, i=i: copy_fold(b, h, i)) for i in range(2, heads)] + [(1, copy_rows)]
                stagger(act, WB, *stages)

            @block.vector
            def _(dve):
                if one:
                    dve.memset(fold[:, :], 0.0)
                    dve.memset(wv[:, :], 0.0).then_inc(s_clear, 1)
                    dve.memset(g.rows[:, :, :, D:D + 1], 1.0).then_inc(s_c, 1)
                    dve.memset(xT[D:D + 1, :, :], 1.0).then_inc(s_c, 1)
                else:
                    dve.memset(g.rows[:, :, :, D + 2:F3], 1.0).then_inc(s_c, 1)
                    dve.memset(xT[D:D + 1, :, :], 1.0).then_inc(s_c, 1)
                    dve.wait_ge(s_fold, 1)
                    dve.wait_ge(s_w, 16 * len(loads))
                    dve.tensor_copy(ws[:, :], pO[0:W, 0:HD]).then_inc(s_part, 1)
                    dve.wait_ge(s_part, 1)
                    dve.tensor_tensor(ws[D:W, D:HD], ws[D:W, D:HD], late[D:W, :, :].rearrange("o i d -> o (i d)"), ALU.add).then_inc(s_c, 1)
                MAXIMA, OUTPUTS = (4, 3) if one else (2, 4)
                cm = Chain(dve, s_v, MAXIMA * U)
                co = Chain(dve, s_co, OUTPUTS * U)
                links = [1 + norm.FIRST] + [] if one else [1 + norm.FIRST] + [norm.SECOND + 2 + norm.FIRST] * (H - 1) + [norm.SECOND + 3 + norm.FIRST]
                links.append(norm.SECOND)
                cc = Chain(dve, s_chain, sum(links))

                def penalties(b, h, r):
                    dve.wait_ge(s_rel[h], r * 16 + 16)
                    if started(r):
                        dve.wait_ge(s_V, (b - 1) * U)
                    dve.tensor_scalar(pen[:, h, :, :].rearrange("i u e -> i (u e)"), rel[:, h, :], k.part[0:S, 0:1], -BIG, ALU.not_equal, ALU.mult).then_inc(s_pen, 1)

                def attributes(b, h, r):
                    if started(r):
                        dve.wait_ge(g.s_used, b - 1)
                    dve.tensor_scalar(g.rows[:, h, :, D:D + 2], k.w_attr[:, bass.ds(b * U, U), :], 1.0, None, ALU.mult).then_inc(s_attr, 1)

                def maxima(b, h, u):
                    n, q = b * U + u, (h + u) % 2
                    cm.at(b)
                    cm.n = u * MAXIMA
                    dve.wait_ge(s_S, n + 1)
                    if not (isinstance(b, int) and b * U + u < 2):
                        dve.wait_ge(s_P, n - 1)
                    if one:
                        cm.link(dve.tensor_scalar(low[:, q, :], pS[q][:, 0:K], 0.01, None, ALU.mult))
                        cm.link(dve.tensor_tensor(ex[:, q, 0, :], low[:, q, :], pS[q][:, 0:K], ALU.max))
                        cm.link(dve.tensor_reduce(top[:, q, :], ex[:, q, :, :], AX.X, ALU.max))
                    else:
                        cm.link(dve.tensor_reduce(top[:, q, :], pS[q][:, 0:heads * K].rearrange("i (m e) -> i m e", e=K), AX.X, ALU.max))
                    cm.link(dve.tensor_scalar(top[:, q, :], top[:, q, :], -BIG * 1e-5, -scale, ALU.max, ALU.mult))
                    dve.sem_inc(s_m, 1)

                def outputs(b, h, u):
                    n = b * U + u
                    co.at(b)
                    co.n = u * OUTPUTS
                    dve.wait_ge(s_O, n + 1)
                    d = den[:, h, u, :]
                    co.link(dve.tensor_scalar(d, d, 1e-30, None, ALU.max))
                    co.link(dve.reciprocal(d, d))
                    ov = o[:, h, u, :].rearrange("i (m d) -> i m d", d=D)
                    co.link(dve.tensor_tensor(ov, pO[0:S, 0:HD].rearrange("i (m d) -> i m d", d=D), wide(d.unsqueeze(2), [S, heads, D]), ALU.mult))
                    if not one:
                        co.link(dve.tensor_tensor(o[:, h, u, :], o[:, h, u, :], pO[0:S, HD:2 * HD], ALU.add))
                    dve.sem_inc(s_Oused, 1)

                def chain(b, h, r, j):
                    s = s_[:, :, :]
                    cc.at(b)
                    cc.n = sum(links[:j])
                    if j == 0:
                        if one:
                            dve.wait_ge(s_left[h], r * 16 + 16)
                            cc.link(dve.tensor_tensor(s, o[:, h, :, :], left[:, h, :, :], ALU.add))
                            dve.sem_inc(s_leftused, 1)
                            norm.first(dve, cc.link, s, 0)
                        else:
                            cc.link(dve.tensor_scalar(s, o[:, h, :, 0:D], 1.0, None, ALU.mult))
                            norm.first(dve, cc.link, s, 0)
                    if one and j == 1 or not one and j == H + 1:
                        if started(r):
                            dve.wait_ge(s_out[h], r * 16)
                        norm.second(dve, cc.link, s, 0, y[:, h, :, :], b * NORMS + NORMS)
                        dve.sem_inc(s_y, 1)
                        cc.end()
                    elif not one and j:
                        norm.second(dve, cc.link, s, 0, s, b * NORMS + j)
                        cc.link(dve.tensor_tensor(s, s, wide(gamma[:, j - 1, :].unsqueeze(1), [S, U, D]), ALU.mult))
                        if j < H:
                            cc.link(dve.tensor_tensor(s, s, o[:, h, :, j * D:(j + 1) * D], ALU.add))
                        else:
                            cc.link(dve.tensor_tensor(s, s, wide(beta[:, :].unsqueeze(1), [S, U, D]), ALU.add))
                            dve.wait_ge(s_left[h], r * 16 + 16)
                            cc.link(dve.scalar_tensor_tensor(s, s, 0.0, left[:, h, :, :], ALU.max, ALU.add))
                            dve.sem_inc(s_leftused, 1)
                        norm.first(dve, cc.link, s, 0)

                stages = [] if one else [(2, attributes)]
                for u in range(U):
                    stages.append(tile(0, u, maxima))
                    if u == 3:
                        stages.append((1, penalties))
                    for j in range(NORMS + 1):
                        if (FIRST_SLOT + j) % U == u:
                            stages.append((-1 - (FIRST_SLOT + j) // U, lambda b, h, r, j=j: chain(b, h, r, j)))
                    stages.append(tile(0, u - 2, outputs))
                stagger(dve, WB, *stages)


def norm_steps(k, dve, link, r, tmp, stat, s_var, s_std, nth, out, eps=EPS):
    mean, var = stat[:, 0, :], stat[:, 1, :]
    link(dve.tensor_reduce(mean, r, AX.X, ALU.add))
    link(dve.tensor_scalar(mean, mean, 1.0 / D, None, ALU.mult))
    link(dve.tensor_tensor(r, r, wide(mean.unsqueeze(2), [P, G, D]), ALU.subtract))
    link(dve.tensor_tensor(tmp, r, r, ALU.mult))
    link(dve.tensor_reduce(var, tmp, AX.X, ALU.add))
    link(dve.tensor_scalar(var, var, 1.0 / D, eps, ALU.mult, ALU.add))
    dve.sem_inc(s_var, 1)
    dve.wait_ge(s_std, nth)
    link(dve.reciprocal(var, var))
    link(dve.tensor_tensor(out, r, wide(var.unsqueeze(2), [P, G, D]), ALU.mult))


def node_pass(k, kind, xs, agg_used, weights, bias, outs, skip=None):
    nc, a, sb, sem, ps = k.nc, k.a, k.sb, k.sem, k.ps
    HC = HALF * P
    product = kind != "filter"
    KD = D if kind == "attend" else 2 * D
    with k.stage() as ctx:
        agg = sb(ctx, "agg", [P, 2, G, W])
        left = sb(ctx, "left", [P, 2, G, D])
        stack = sb(ctx, "stack", [P, 2, G, KD])
        stackT = sb(ctx, "stackT", [KD, 2, HC])
        w = sb(ctx, "w", [KD, D])
        brow = sb(ctx, "brow", [1, D])
        arow = sb(ctx, "arow", [P, D])
        r_ = sb(ctx, "r", [P, G, D])
        tmp = sb(ctx, "tmp", [P, G, D])
        stat = sb(ctx, "stat", [P, 3, G])
        y = [sb(ctx, "y", [P, 2, G, o[1]]) for o in outs]
        pT = ps(ctx, "pT", [KD, 2, 512])
        pO = ps(ctx, "pO", [P, G * D])
        s_w, s_v, s_f, s_T, s_Ts, s_O, s_var, s_std, s_y, s_stack, s_a = (
            sem(ctx, n) for n in ("s_w", "s_v", "s_f", "s_T", "s_Ts", "s_O", "s_var", "s_std", "s_y", "s_stack", "s_a"))
        s_in = [sem(ctx, "s_in") for _ in range(2)]
        s_out = [sem(ctx, "s_out") for _ in range(2)]
        n_in = 1 + (xs is not None) + (skip is not None)
        n_w = len(weights) + (bias is not None) + (kind == "filter")
        with nc.Block() as block:

            @block.sync
            def _(sp):
                for i, x in enumerate(weights):
                    sp.dma_start(w[i * D:(i + 1) * D, :], x).then_inc(s_w, 16)
                if bias is not None:
                    sp.dma_start(brow[:, :], bias.unsqueeze(0)).then_inc(s_w, 16)
                if kind == "filter":
                    sp.dma_start(arow[:, :], a["L2_gnn_ar"].rearrange("d o -> (d o)").partition_broadcast(P)).then_inc(s_w, 16)

                def load(b, h, r):
                    sp.dma_start(agg[:, h, :, :], rows(k.agg, b, W)).then_inc(s_in[h], 16)
                    if xs is not None:
                        sp.dma_start(stack[:, h, :, 0:D], rows(xs, b, D)).then_inc(s_in[h], 16)
                    if skip is not None:
                        sp.dma_start(left[:, h, :, :], rows(skip, b, D)).then_inc(s_in[h], 16)

                def store(b, h, r):
                    sp.wait_ge(s_y, b + 1)
                    for t, o in zip(y, outs):
                        sp.dma_start(rows(o[0], b, o[1]), t[:, h, :, :]).then_inc(s_out[h], 16)
                ahead(sp, load, store)
                for h in range(2):
                    sp.wait_ge(s_out[h], 16 * len(outs) * NB // 2)

            if product:
                @block.tensor
                def _(pe):
                    pe.wait_ge(s_w, 16 * n_w)

                    def transposes(b, h, r):
                        pe.wait_ge(s_stack, b + 1)
                        if not (isinstance(b, int) and b == 0):
                            pe.wait_ge(s_Ts, b)
                        pe.sem_inc(k.s_pe, 1)
                        for u in range(G):
                            ins = pe.transpose(pT[:, u // HALF, (u % HALF) * P:(u % HALF + 1) * P], stack[:, h, u, :], k.ident[:, :])
                        ins.then_inc(s_T, 1)

                    def products(b, h, r):
                        pe.wait_ge(s_Ts, b + 1)
                        if not (isinstance(b, int) and b == 0):
                            pe.wait_ge(s_a, b)
                        pe.sem_inc(k.s_pe, 1)
                        for u in range(G):
                            last = bias is None
                            ins = pe.matmul(pO[:, u * D:(u + 1) * D], stackT[:, u // HALF, (u % HALF) * P:(u % HALF + 1) * P], w[:, :], start=True, stop=last)
                            if not last:
                                ins = pe.matmul(pO[:, u * D:(u + 1) * D], k.ones[0:1, :], brow[:, :], start=False, stop=True)
                        ins.then_inc(s_O, 1)

                    def both(b, h, r):
                        transposes(b, h, r)
                        products(b, h, r)
                    plain(pe, both)

            @block.scalar
            def _(act):
                def body(b, h, r):
                    if product:
                        act.wait_ge(s_T, b + 1)
                        if not (isinstance(b, int) and b == 0):
                            act.wait_ge(s_O, b)
                        act.activation(stackT[:, :, :], pT[:, :, 0:HC], ACT.Copy).then_inc(s_Ts, 1)
                    if kind != "cheb1":
                        act.wait_ge(s_var, b + 1)
                        act.activation(stat[:, 1, :], stat[:, 1, :], ACT.Sqrt).then_inc(s_std, 1)
                plain(act, body)

            @block.vector
            def _(dve):
                first = Chain(dve, s_f, {"attend": 3, "filter": 1}.get(kind, 1))
                c = Chain(dve, s_v, {"cheb1": 2, "cheb2": 9, "filter": 11, "attend": 9}[kind])
                dve.wait_ge(s_w, 16 * n_w)

                def stacking(b, h, r):
                    first.at(b)
                    dve.wait_ge(s_in[h], r * (16 * n_in) + 16 * n_in)
                    if kind == "filter":
                        first.link(dve.tensor_tensor(left[:, h, :, :], left[:, h, :, :], agg[:, h, :, 0:D], ALU.add))
                    elif kind == "attend":
                        den = stat[:, 2, :]
                        first.link(dve.tensor_scalar(den, agg[:, h, :, D], 1e-30, None, ALU.max))
                        first.link(dve.reciprocal(den, den))
                        first.link(dve.tensor_tensor(stack[:, h, :, :], agg[:, h, :, 0:D], wide(den.unsqueeze(2), [P, G, D]), ALU.mult))
                    else:
                        first.link(dve.scalar_tensor_tensor(stack[:, h, :, D:2 * D], agg[:, h, :, 0:D], -1.0, wide(cols(k.dinv, b).unsqueeze(2), [P, G, D]), ALU.mult, ALU.mult))
                    first.end()
                    dve.sem_inc(s_stack, 1)

                def rest(b, h, r):
                    c.at(b)
                    po = pO[:, :].rearrange("p (u d) -> p u d", d=D)
                    if product:
                        dve.wait_ge(s_O, b + 1)
                    if started(r):
                        dve.wait_ge(s_out[h], r * (16 * len(outs)))
                    if kind == "cheb1":
                        c.link(dve.tensor_scalar(y[0][:, h, :, :], po, 0.0, None, ALU.max))
                        dve.sem_inc(s_a, 1)
                        c.link(dve.tensor_tensor(y[1][:, h, :, :], y[0][:, h, :, :], wide(cols(k.dinv, b).unsqueeze(2), [P, G, D]), ALU.mult))
                    elif kind == "filter":
                        norm_steps(k, dve, c.link, left[:, h, :, :], tmp[:, :, :], stat, s_var, s_std, b + 1, y[0][:, h, :, :])
                        c.link(dve.tensor_tensor(tmp[:, :, :], y[0][:, h, :, :], wide(arow[:, :].unsqueeze(1), [P, G, D]), ALU.mult))
                        c.link(dve.tensor_reduce(y[1][:, h, :, :], tmp[:, :, :], AX.X, ALU.add))
                        c.link(dve.tensor_scalar(stat[:, 2, :], stat[:, 0, :], 1.0, None, ALU.mult))
                    else:
                        c.link(dve.tensor_tensor(r_[:, :, :], po, left[:, h, :, :], ALU.add))
                        dve.sem_inc(s_a, 1)
                        norm_steps(k, dve, c.link, r_[:, :, :], tmp[:, :, :], stat, s_var, s_std, b + 1, y[0][:, h, :, :])
                    dve.sem_inc(s_y, 1)
                    c.end()

                ahead(dve, stacking, rest)


def transformer_nodes(k, x, agg3, out):
    nc, a, sb, sem, ps = k.nc, k.a, k.sb, k.sem, k.ps
    HC = HALF * P
    with k.stage() as ctx:
        agg = sb(ctx, "agg", [P, 2, G, H, F3])
        xin = sb(ctx, "xin", [P, 2, G, W])
        aggT = sb(ctx, "aggT", [F3, H, P])
        aggT2 = sb(ctx, "aggT2", [F3, H, P])
        xT = sb(ctx, "xT", [W, P])
        xT2 = sb(ctx, "xT2", [W, P])
        nat = sb(ctx, "nat", [D, H, F3 + W])
        wv = sb(ctx, "wv", [F3, H, D])
        ws = sb(ctx, "ws", [W, H * D])
        gamma = sb(ctx, "gamma", [P, H, D])
        beta = sb(ctx, "beta", [P, H, D])
        o3 = sb(ctx, "o3", [P, G, H * D])
        s_ = sb(ctx, "s", [P, G, D])
        tmp = sb(ctx, "tmp", [P, G, D])
        stat = sb(ctx, "stat", [P, 3, G])
        den = sb(ctx, "den", [P, G, H])
        y = sb(ctx, "y", [P, 2, G, D])
        pT = [ps(ctx, "pT", [F3, 512]) for _ in range(2)]
        pO = [ps(ctx, "pO", [P, 512]) for _ in range(2)]
        names = ("s_w", "s_wT", "s_wc", "s_v", "s_f", "s_T", "s_Ts", "s_O", "s_Oc", "s_var", "s_std", "s_y", "s_stack", "s_one", "s_part", "s_o3")
        s_w, s_wT, s_wc, s_v, s_f, s_T, s_Ts, s_O, s_Oc, s_var, s_std, s_y, s_stack, s_one, s_part, s_o3 = (sem(ctx, n) for n in names)
        s_in = [sem(ctx, "s_in") for _ in range(2)]
        s_out = [sem(ctx, "s_out") for _ in range(2)]
        aT, xTs = [aggT, aggT2], [xT, xT2]
        with nc.Block() as block:

            @block.sync
            def _(sp):
                for i in range(H):
                    for t, src in ((nat[:, i, 0:D], a["L3_gnn_Wv"][i, :, :]), (nat[:, i, D:D + 2], a["L3_gnn_We"][i, :, :]),
                                   (nat[:, i, D + 2:F3], a["L3_gnn_bv"][i, :].unsqueeze(1)),
                                   (nat[:, i, F3:F3 + D], a["L3_gnn_Wskip"][i, :, :]), (nat[:, i, F3 + D:F3 + W], a["L3_gnn_bskip"][i, :].unsqueeze(1)),
                                   (gamma[:, i, :], a["L3_gnn_gamma"][i, :].partition_broadcast(P)), (beta[:, i, :], a["L3_gnn_beta"][i, :].partition_broadcast(P))):
                        sp.dma_start(t, src).then_inc(s_w, 16)
                sp.wait_ge(s_one, 1)

                def load(b, h, r):
                    sp.dma_start(agg[:, h, :, :, :].rearrange("p u i f -> p u (i f)"), rows(agg3, b, W3)).then_inc(s_in[h], 16)
                    sp.dma_start(xin[:, h, :, 0:D], rows(x, b, D)).then_inc(s_in[h], 16)

                def store(b, h, r):
                    sp.wait_ge(s_y, b + 1)
                    sp.dma_start(rows(out, b, D), y[:, h, :, :]).then_inc(s_out[h], 16)
                ahead(sp, load, store)
                for h in range(2):
                    sp.wait_ge(s_out[h], 16 * NB // 2)

            @block.tensor
            def _(pe):
                pe.wait_ge(s_w, 16 * 7 * H)
                for i in range(H):
                    if i:
                        pe.wait_ge(s_wc, 2 * i)
                    pe.transpose(pT[0][0:F3, 0:D], nat[:, i, 0:F3], k.ident[0:D, 0:D])
                    pe.transpose(pT[1][0:W, 0:D], nat[:, i, F3:F3 + W], k.ident[0:D, 0:D]).then_inc(s_wT, 1)
                pe.wait_ge(s_wc, 2 * H)

                def body(b, h, r):
                    pe.wait_ge(s_stack, b + 1)

                    def turn(u):
                        i = u % 2
                        if not (isinstance(b, int) and b == 0 and u < 2):
                            pe.wait_ge(s_Ts, b * G + u - 1)
                        pe.sem_inc(k.s_pe, 1)
                        for j in range(H):
                            pe.transpose(pT[i][:, j * P:(j + 1) * P], agg[:, h, u, j, :], k.ident[:, :])
                        pe.transpose(pT[i][0:W, H * P:H * P + P], xin[:, h, u, :], k.ident[:, :]).then_inc(s_T, 1)

                    def product(u):
                        i = u % 2
                        pe.wait_ge(s_Ts, b * G + u + 1)
                        if not (isinstance(b, int) and b == 0 and u < 2):
                            pe.wait_ge(s_Oc, b * G + u - 1)
                        pe.sem_inc(k.s_pe, 1)
                        pe.matmul(pO[i][:, 0:H * D], xTs[i][:, :], ws[:, :], start=True, stop=False, skip_group_check=True)
                        for j in range(H):
                            ins = pe.matmul(pO[i][:, j * D:(j + 1) * D], aT[i][:, j, :], wv[:, j, :], start=False, stop=True, skip_group_check=True)
                        ins.then_inc(s_O, 1)
                    turn(0)
                    for u in range(G):
                        if u + 1 < G:
                            turn(u + 1)
                        product(u)
                plain(pe, body)

            @block.scalar
            def _(act):
                for i in range(H):
                    act.wait_ge(s_wT, i + 1)
                    act.activation(wv[:, i, :], pT[0][0:F3, 0:D], ACT.Copy).then_inc(s_wc, 1)
                    act.activation(ws[:, i * D:(i + 1) * D], pT[1][0:W, 0:D], ACT.Copy).then_inc(s_wc, 1)

                def body(b, h, r):
                    for u in range(G + 1):
                        if u < G:
                            i = u % 2
                            act.wait_ge(s_T, b * G + u + 1)
                            if not (isinstance(b, int) and b == 0 and u < 2):
                                act.wait_ge(s_O, b * G + u - 1)
                            act.activation(aT[i][:, :, :], pT[i][:, 0:H * P].rearrange("f (i p) -> f i p", i=H), ACT.Copy).then_inc(s_part, 1)
                            act.activation(xTs[i][:, :], pT[i][0:W, H * P:H * P + P], ACT.Copy).then_inc(s_part, 1)
                            act.wait_ge(s_part, b * (2 * G) + 2 * u + 2)
                            act.sem_inc(s_Ts, 1)
                        if u:
                            i = (u - 1) % 2
                            if u == 1 and not (isinstance(b, int) and b == 0):
                                act.wait_ge(s_o3, b)
                            act.wait_ge(s_O, b * G + u)
                            act.activation(o3[:, u - 1, :], pO[i][:, 0:H * D], ACT.Copy).then_inc(s_Oc, 1)
                    for j in range(H + 1):
                        act.wait_ge(s_var, b * (H + 1) + j + 1)
                        act.activation(stat[:, 1, :], stat[:, 1, :], ACT.Sqrt).then_inc(s_std, 1)
                plain(act, body)

            @block.vector
            def _(dve):
                first = Chain(dve, s_f, 3)
                c = Chain(dve, s_v, H + H * (8 + 2) + 1 + 8)
                dve.memset(xin[:, :, :, D:W], 1.0).then_inc(s_one, 1)
                dve.wait_ge(s_w, 16 * 7 * H)

                def stacking(b, h, r):
                    first.at(b)
                    dve.wait_ge(s_in[h], r * 32 + 32)
                    first.link(dve.tensor_scalar(den[:, :, :], agg[:, h, :, :, F3 - 1], 1e-30, None, ALU.max))
                    first.link(dve.reciprocal(den[:, :, :], den[:, :, :]))
                    first.link(dve.tensor_tensor(agg[:, h, :, :, :], agg[:, h, :, :, :], wide(den[:, :, :].unsqueeze(3), [P, G, H, F3]), ALU.mult))
                    first.end()
                    dve.sem_inc(s_stack, 1)

                def rest(b, h, r):
                    c.at(b)
                    dve.wait_ge(s_Oc, b * G + G)
                    s = s_[:, :, :]
                    c.link(dve.tensor_scalar(s, o3[:, :, 0:D], 1.0, None, ALU.mult))
                    for j in range(H):
                        if j:
                            c.link(dve.tensor_tensor(s, s, o3[:, :, j * D:(j + 1) * D], ALU.add))
                        if j == H - 1:
                            dve.sem_inc(s_o3, 1)
                        norm_steps(k, dve, c.link, s, tmp[:, :, :], stat, s_var, s_std, b * (H + 1) + j + 1, s)
                        c.link(dve.tensor_tensor(s, s, wide(gamma[:, j, :].unsqueeze(1), [P, G, D]), ALU.mult))
                        c.link(dve.tensor_tensor(s, s, wide(beta[:, j, :].unsqueeze(1), [P, G, D]), ALU.add))
                    c.link(dve.scalar_tensor_tensor(s, s, 0.0, xin[:, h, :, 0:D], ALU.max, ALU.add))
                    if started(r):
                        dve.wait_ge(s_out[h], r * 16)
                    norm_steps(k, dve, c.link, s, tmp[:, :, :], stat, s_var, s_std, b * (H + 1) + H + 1, y[:, h, :, :])
                    dve.sem_inc(s_y, 1)
                    c.end()

                ahead(dve, stacking, rest)


def build(nc, a, out):
    with ExitStack() as keep:
        k = Program(nc, a, out, keep)
        k.s_act, k.s_pe, k.s_pool = k.sem(keep, "s_act"), k.sem(keep, "s_pe"), k.sem(keep, "s_pool")

        def table(name, width):
            return nc.dram_tensor(name, (N, width), F32).ap()
        k.scaled = table("scaled", D)
        k.agg, k.agg3 = table("agg", W), table("agg3", W3)
        hidden, scaled2, x1, x2, x3, er = table("hidden", D), table("scaled2", D), table("x1", D), table("x2", D), table("x3", D), table("er", 1)
        k.rel_rows = nc.dram_tensor("rel_rows", (TILES, K), F32).ap()
        setup(k, keep)
        windows(k, keep)
        fits = nc.values_load(k.fits[0:1, 0:1], min_val=0, max_val=1)
        with nc.If(fits > 0):
            window_cheb(k, a["x"], k.scaled, a["L0_gnn_W0_1"], a["L0_gnn_W1_1"], a["L0_gnn_b1"], [hidden, scaled2])
            window_cheb(k, hidden, scaled2, a["L0_gnn_W0_2"], a["L0_gnn_W1_2"], a["L0_gnn_b2"], [x1], skip=a["x"])
            window_filter(k, x1, x2)
            window_attend(k, 1, x2, x3)
            window_attend(k, H, x3, out)
        with nc.Else():
            cheb_edges(k, k.scaled)
            node_pass(k, "cheb1", a["x"], True, [a["L0_gnn_W0_1"], a["L0_gnn_W1_1"]], a["L0_gnn_b1"], [(hidden, D), (scaled2, D)])
            cheb_edges(k, scaled2)
            node_pass(k, "cheb2", hidden, True, [a["L0_gnn_W0_2"], a["L0_gnn_W1_2"]], a["L0_gnn_b2"], [(x1, D)], skip=a["x"])
            filter_edges(k, x1)
            node_pass(k, "filter", None, True, [], None, [(x2, D), (er, 1)], skip=x1)
            with ExitStack() as ctx:
                kept, logits = k.sb(ctx, "kept", [P, T, W]), k.sb(ctx, "logits", [P, T, 1])
                attend_logits(k, kept, logits, x2, er)
                segment_softmax(k, logits, 1)
                attend_sums(k, kept, logits, k.agg, 1, W)
            node_pass(k, "attend", None, True, [a["L2_gnn_W"]], None, [(x3, D)], skip=x2)
            with ExitStack() as ctx:
                kept, logits = k.sb(ctx, "kept", [P, T, F3]), k.sb(ctx, "logits", [P, T, H])
                transformer_logits(k, kept, logits, x3)
                segment_softmax(k, logits, H)
                attend_sums(k, kept, logits, k.agg3, H, F3)
            transformer_nodes(k, x3, k.agg3, out)


_INS = ['x', 'src', 'dst', 'edge_attr_2', 'edge_attr_48', 'edge_attr_64', 'edge_weight',
        'L0_gnn_W0_1', 'L0_gnn_W1_1', 'L0_gnn_b1', 'L0_gnn_W0_2', 'L0_gnn_W1_2', 'L0_gnn_b2',
        'L1_gnn_W1', 'L1_gnn_b1', 'L1_gnn_W2', 'L1_gnn_b2', 'L1_gnn_W3', 'L1_gnn_b3', 'L1_gnn_W4', 'L1_gnn_b4',
        'L2_gnn_W', 'L2_gnn_al', 'L2_gnn_ar',
        'L3_gnn_Wq', 'L3_gnn_bq', 'L3_gnn_Wk', 'L3_gnn_bk', 'L3_gnn_Wv', 'L3_gnn_bv', 'L3_gnn_We',
        'L3_gnn_Wskip', 'L3_gnn_bskip', 'L3_gnn_gamma', 'L3_gnn_beta']


def kernel(**inputs):
    import numpy as _np
    import concourse.bacc as _bacc
    from concourse import mybir as _mybir
    from concourse.bass_utils import run_bass_kernel_spmd as _run

    nc = _bacc.Bacc("TRN2", target_bir_lowering=False, num_devices=1)
    arrays, args = {}, {}
    for name in _INS:
        a = _np.ascontiguousarray(inputs[name])
        arrays[f"in_{name}_dram"] = a
        args[name] = nc.dram_tensor(f"in_{name}_dram", a.shape, _mybir.dt.from_np(a.dtype), kind="ExternalInput").ap()
    out = nc.dram_tensor("out_0_dram", (N, D), _mybir.dt.float32, kind="ExternalOutput").ap()
    build(nc, args, out)
    r = _run(nc, [arrays], core_ids=[0])
    return r.results[0]["out_0_dram"]
```
